# Optimizing a Trainium2 kernel written in Bass

```python
import numpy as np
import jax
import jax.numpy as jnp

def _softmax(x, axis=-1):
    return jax.nn.softmax(x, axis=axis)

def _gelu(x):
    return jax.nn.gelu(x, approximate=True)

def _silu(x):
    return jax.nn.silu(x)

def _sigmoid(x):
    return jax.nn.sigmoid(x)

def _layernorm(x, axis=-1, eps=1e-05):
    m = jnp.mean(x, axis=axis, keepdims=True)
    v = jnp.var(x, axis=axis, keepdims=True)
    return (x - m) / jnp.sqrt(v + eps)

def _scatter_add(tgt, idx, src, axis=0):
    return tgt.at[idx].add(src)

def _segment_sum(src, seg, n):
    return jax.ops.segment_sum(src, seg, n)
kernel_name = 'mk_gnn_preln_d2_gnn_r32_ecd8b2'

def setup_inputs(seed: int=0):
    np.random.seed(seed)
    _w = jnp.asarray

    def _rec_inputs():
        import jax
        import jax.numpy as jnp
        _gk = jax.random.key(seed)
        x = -0.000202 + 1 * jax.random.normal(jax.random.fold_in(_gk, 1), (3125, 128), jnp.float32)
        _s = jax.random.randint(jax.random.fold_in(_gk, 2), (25000,), 0, 3125, jnp.int32)
        _d = jax.random.randint(jax.random.fold_in(_gk, 3), (25000,), 0, 3125, jnp.int32)
        _loop = jnp.arange(3125, dtype=jnp.int32)
        src = jnp.concatenate([_s, _d, _loop])
        dst = jnp.concatenate([_d, _s, _loop])
        _o = jnp.argsort(dst, stable=True)
        src = src[_o]
        dst = dst[_o]
        edge_attr_128 = 5.93493e-05 + 1.00006 * jax.random.normal(jax.random.fold_in(_gk, 11), (53125, 128), jnp.float32)
        return (x, src, dst, edge_attr_128)
    x, src, dst, edge_attr_128 = _rec_inputs()

    def _L0_gnn_setup():
        import jax, jax.numpy as jnp
        import numpy as np
        N_NODES = 50000
        N_EDGES = 25000
        C_IN = 128
        HID = 128
        C_OUT = 128

        def _glorot(key, shape):
            fan_in, fan_out = shape
            lim = (6.0 / (fan_in + fan_out)) ** 0.5
            return jax.random.uniform(key, shape, jnp.float32, -lim, lim)

        def _edge_conv(x, src, dst, W1, b1, W2, b2, n_nodes):
            xi = x[dst]
            xj = x[src]
            m = jnp.concatenate([xi, xj - xi], axis=-1)
            h = jax.nn.relu(m @ W1 + b1) @ W2 + b2
            agg = jax.ops.segment_max(h, dst, num_segments=n_nodes)
            return jnp.where(jnp.isfinite(agg), agg, 0.0)
        key = jax.random.key(seed)
        ks = jax.random.split(key, 8)
        x = jax.random.normal(ks[0], (N_NODES, C_IN), jnp.float32)
        edge_index = jax.random.randint(ks[1], (2, N_EDGES), 0, N_NODES, jnp.int32)
        return {'x': x, 'edge_index': edge_index, 'W1_in': _glorot(ks[2], (2 * C_IN, HID)), 'b1_in': jnp.zeros((HID,), jnp.float32), 'W2_in': _glorot(ks[3], (HID, HID)), 'b2_in': jnp.zeros((HID,), jnp.float32), 'W1_hid': _glorot(ks[4], (2 * HID, HID)), 'b1_hid': jnp.zeros((HID,), jnp.float32), 'W2_hid': _glorot(ks[5], (HID, HID)), 'b2_hid': jnp.zeros((HID,), jnp.float32), 'W1_out': _glorot(ks[6], (2 * HID, HID)), 'b1_out': jnp.zeros((HID,), jnp.float32), 'W2_out': _glorot(ks[7], (HID, C_OUT)), 'b2_out': jnp.zeros((C_OUT,), jnp.float32)}
    _L0_gnn_all = _L0_gnn_setup()
    _L0_gnn_in = {k: v for k, v in _L0_gnn_all.items() if k in ('W1_in', 'b1_in', 'W2_in', 'b2_in', 'W1_hid', 'b1_hid', 'W2_hid', 'b2_hid', 'W1_out', 'b1_out', 'W2_out', 'b2_out')}
    del _L0_gnn_all

    def _L1_gnn_setup():
        import jax, jax.numpy as jnp
        import numpy as np
        N_NODES = 3125
        N_EDGES = 18750
        D = 128
        H = 256
        LN_EPS = 1e-05
        key = jax.random.key(seed)
        ks = jax.random.split(key, 8)
        x = jax.random.normal(ks[0], (N_NODES, D), dtype=jnp.float32)
        edge_index = jax.random.randint(ks[1], (2, N_EDGES), 0, N_NODES, dtype=jnp.int64)
        edge_attr = jax.random.normal(ks[2], (N_EDGES, D), dtype=jnp.float32)
        s1 = 1.0 / np.sqrt(H)
        s2 = 1.0 / np.sqrt(H)
        W1 = jax.random.uniform(ks[3], (H, H), jnp.float32, -s1, s1)
        b1 = jax.random.uniform(ks[4], (H,), jnp.float32, -s1, s1)
        W2 = jax.random.uniform(ks[5], (H, D), jnp.float32, -s2, s2)
        b2 = jax.random.uniform(ks[6], (D,), jnp.float32, -s2, s2)
        ln_gamma = jnp.ones((D,), jnp.float32)
        ln_beta = jnp.zeros((D,), jnp.float32)
        return {'x': x, 'edge_index': edge_index, 'edge_attr': edge_attr, 'W1': W1, 'b1': b1, 'W2': W2, 'b2': b2, 'ln_gamma': ln_gamma, 'ln_beta': ln_beta}
    _L1_gnn_all = _L1_gnn_setup()
    _L1_gnn_in = {k: v for k, v in _L1_gnn_all.items() if k in ('W1', 'b1', 'W2', 'b2', 'ln_gamma', 'ln_beta')}
    del _L1_gnn_all
    return {'x': x, 'src': src, 'dst': dst, 'edge_attr_128': edge_attr_128, 'L0_gnn_W1_in': _L0_gnn_in['W1_in'], 'L0_gnn_b1_in': _L0_gnn_in['b1_in'], 'L0_gnn_W2_in': _L0_gnn_in['W2_in'], 'L0_gnn_b2_in': _L0_gnn_in['b2_in'], 'L0_gnn_W1_hid': _L0_gnn_in['W1_hid'], 'L0_gnn_b1_hid': _L0_gnn_in['b1_hid'], 'L0_gnn_W2_hid': _L0_gnn_in['W2_hid'], 'L0_gnn_b2_hid': _L0_gnn_in['b2_hid'], 'L0_gnn_W1_out': _L0_gnn_in['W1_out'], 'L0_gnn_b1_out': _L0_gnn_in['b1_out'], 'L0_gnn_W2_out': _L0_gnn_in['W2_out'], 'L0_gnn_b2_out': _L0_gnn_in['b2_out'], 'L1_gnn_W1': _L1_gnn_in['W1'], 'L1_gnn_b1': _L1_gnn_in['b1'], 'L1_gnn_W2': _L1_gnn_in['W2'], 'L1_gnn_b2': _L1_gnn_in['b2'], 'L1_gnn_ln_gamma': _L1_gnn_in['ln_gamma'], 'L1_gnn_ln_beta': _L1_gnn_in['ln_beta']}

def reference(x, src, dst, edge_attr_128, L0_gnn_W1_in, L0_gnn_b1_in, L0_gnn_W2_in, L0_gnn_b2_in, L0_gnn_W1_hid, L0_gnn_b1_hid, L0_gnn_W2_hid, L0_gnn_b2_hid, L0_gnn_W1_out, L0_gnn_b1_out, L0_gnn_W2_out, L0_gnn_b2_out, L1_gnn_W1, L1_gnn_b1, L1_gnn_W2, L1_gnn_b2, L1_gnn_ln_gamma, L1_gnn_ln_beta):
    import jax
    import jax.numpy as jnp

    def _L0_gnn_ref(x, edge_index, W1_in, b1_in, W2_in, b2_in, W1_hid, b1_hid, W2_hid, b2_hid, W1_out, b1_out, W2_out, b2_out):
        import jax, jax.numpy as jnp
        import numpy as np
        N_NODES = 50000
        N_EDGES = 25000
        C_IN = 128
        HID = 128
        C_OUT = 128

        def _glorot(key, shape):
            fan_in, fan_out = shape
            lim = (6.0 / (fan_in + fan_out)) ** 0.5
            return jax.random.uniform(key, shape, jnp.float32, -lim, lim)

        def _edge_conv(x, src, dst, W1, b1, W2, b2, n_nodes):
            xi = x[dst]
            xj = x[src]
            m = jnp.concatenate([xi, xj - xi], axis=-1)
            h = jax.nn.relu(m @ W1 + b1) @ W2 + b2
            agg = jax.ops.segment_max(h, dst, num_segments=n_nodes)
            return jnp.where(jnp.isfinite(agg), agg, 0.0)
        src, dst = (edge_index[0], edge_index[1])
        n = x.shape[0]
        x = _edge_conv(x, src, dst, W1_in, b1_in, W2_in, b2_in, n)
        x = jax.nn.relu(x)
        x = _edge_conv(x, src, dst, W1_hid, b1_hid, W2_hid, b2_hid, n)
        x = jax.nn.relu(x)
        x = _edge_conv(x, src, dst, W1_out, b1_out, W2_out, b2_out, n)
        return x

    def _L1_gnn_ref(x, edge_index, edge_attr, W1, b1, W2, b2, ln_gamma, ln_beta):
        import jax, jax.numpy as jnp
        import numpy as np
        N_NODES = 3125
        N_EDGES = 18750
        D = 128
        H = 256
        LN_EPS = 1e-05
        i = edge_index[0]
        agg = jax.ops.segment_sum(edge_attr, i, num_segments=x.shape[0])
        h = jnp.concatenate([x, agg], axis=-1)
        h = jax.nn.silu(h @ W1 + b1)
        h = h @ W2 + b2
        mu = jnp.mean(h, axis=-1, keepdims=True)
        var = jnp.mean(jnp.square(h - mu), axis=-1, keepdims=True)
        h = (h - mu) * jax.lax.rsqrt(var + LN_EPS) * ln_gamma + ln_beta
        return h + x
    edge_index = jnp.stack([src, dst])
    h = jnp.maximum(_layernorm(x, axis=-1), 0.0)
    x = x + _L0_gnn_ref(h, edge_index, L0_gnn_W1_in, L0_gnn_b1_in, L0_gnn_W2_in, L0_gnn_b2_in, L0_gnn_W1_hid, L0_gnn_b1_hid, L0_gnn_W2_hid, L0_gnn_b2_hid, L0_gnn_W1_out, L0_gnn_b1_out, L0_gnn_W2_out, L0_gnn_b2_out)
    h = jnp.maximum(_layernorm(x, axis=-1), 0.0)
    x = x + _L1_gnn_ref(h, edge_index, edge_attr_128, L1_gnn_W1, L1_gnn_b1, L1_gnn_W2, L1_gnn_b2, L1_gnn_ln_gamma, L1_gnn_ln_beta)
    return x

_drawn_inputs = setup_inputs


def setup_inputs(seed=0):
    import zlib

    import numpy as np

    out = dict(_drawn_inputs(seed))
    spreads = {'L0_gnn_b1_in': (0.0, 0.283),
     'L0_gnn_b2_in': (0.0, 0.268),
     'L0_gnn_b1_hid': (0.0, 0.1),
     'L0_gnn_b2_hid': (0.0, 0.1),
     'L0_gnn_b1_out': (0.0, 0.1),
     'L0_gnn_b2_out': (0.0, 0.1),
     'L1_gnn_ln_gamma': (1.0, 0.2),
     'L1_gnn_ln_beta': (0.0, 0.1)}
    factors = {'L1_gnn_b1': 4.495}
    for name, (base, spread) in spreads.items():
        noise = np.random.default_rng([zlib.crc32(name.encode()), seed]).standard_normal(out[name].shape)
        drawn = base * np.exp(spread * noise) if base else spread * noise
        out[name] = jnp.asarray(drawn.astype(out[name].dtype))
    for name, factor in factors.items():
        out[name] = (out[name] * factor).astype(out[name].dtype)
    return out
```

```python
from contextlib import ExitStack

import numpy as np
import concourse.bass as bass
from concourse import mybir

F32 = mybir.dt.float32
BF16 = mybir.dt.bfloat16
FP16 = mybir.dt.float16
I32 = mybir.dt.int32
ALU = mybir.AluOpType
ACT = mybir.ActivationFunctionType
AX_X = mybir.AxisListType.X

P = 128
N, D, E = 3125, 128, 53125
LAYERS = 3
EPS = 1e-5
CH = -(-N // P)
NP = CH * P
NLAST = N - (CH - 1) * P
TILES = -(-E // P)
EP = TILES * P
GROUP = 4
GE = GROUP * P
GROUPS = TILES // GROUP
ITER = GROUPS // 2
IT = 2 * GROUP
FULLROWS = E // GE
TAIL = E - FULLROWS * GE
LO = 64
HI = NP // LO
HUGE = 3.0e38
SKIP = 1 << 17
assert TILES % IT == 0 and FULLROWS == GROUPS - 1 and TAIL < GE


def build(nc, x, src, dst, attr, w1, b1, w2, b2, v1, c1, v2, c2, gamma, beta, out):
    with ExitStack() as ctx:
        def sb(name, shape, dt=F32):
            return ctx.enter_context(nc.sbuf_tensor(name, shape, dt))

        def sem(name):
            return ctx.enter_context(nc.semaphore(name))

        def dram(name, shape, dt=F32):
            return nc.dram_tensor(name, shape, dt).ap()

        def view(region, at, shape, dt=F32):
            n = int(np.prod(shape)) * (2 if dt in (BF16, FP16) else 4) // 4
            ap = region[:, at:at + n]
            if dt != F32:
                ap = ap.bitcast(dt)
            if len(shape) == 2:
                ap = ap.rearrange("p (a b) -> p a b", a=shape[0])
            if len(shape) == 3:
                ap = ap.rearrange("p (a b c) -> p a b c", a=shape[0], b=shape[1])
            return ap

        b_rows = dram("b_rows", (NP, D))
        a_rows = dram("a_rows", (NP, D))
        run_rows = dram("run_rows", (EP, D))
        code_row = dram("code_row", (EP,), BF16)
        base_row = dram("base_row", (TILES,), I32)
        count_row = dram("count_row", (GROUPS,), I32)
        srcf_row = dram("srcf_row", (EP,))
        seg_node = dram("seg_node", (NP, 1), I32)
        node_cols = dram("node_cols", (4, NP))
        keep_row = dram("keep_row", (EP,), BF16)

        xres = sb("xres", [P, CH, D])
        nodes = sb("nodes", [P, CH, D])
        rows_a = sb("rows_a", [P, CH, D])
        big = sb("big", [P, EP // 2])
        work = sb("work", [P, 2 * CH * D])
        a_parts = sb("a_parts", [P, CH + 1, 3, D], BF16)
        ring = sb("ring", [P, 2, GROUP, D])
        src_cols = sb("src_cols", [P, TILES], I32)
        perm_cols = sb("perm_cols", [P, TILES], I32)
        base_sb = sb("base_sb", [1, TILES], I32)
        idx = sb("idx", [P, 2, GROUP], I32)
        w_ab = sb("w_ab", [P, LAYERS, 2 * D])
        w2_sb = sb("w2_sb", [P, LAYERS, D])
        b1_sb = sb("b1_sb", [P, LAYERS, D])
        b2_sb = sb("b2_sb", [P, LAYERS, D])
        ident = sb("ident", [P, P])
        before = sb("before", [P, P])
        place = sb("place", [P, 2])
        first_state = sb("first_state", [P, 1])
        present = sb("present", [P, CH])
        end_dst = sb("end_dst", [P, CH], I32)
        end_src = sb("end_src", [P, CH], I32)
        first_src = sb("first_src", [P, CH])
        stat = sb("stat", [P, 4, CH])
        counter = sb("counter", [1, 4], I32)

        base_keep = sb("base_keep", [P, LO])
        list_idx = sb("list_idx", [P, CH], I32)
        list_at = sb("list_at", [P, 1], I32)
        list_val = sb("list_val", [P, 1], I32)

        rows_b = view(work, 0, (CH, D))
        xt = view(work, CH * D, (CH * D,))
        hin = view(work, 0, (2, GE))
        run = view(work, 2 * GE, (2, GE))
        outb = view(work, 4 * GE, (2, GROUP, D))
        onehot = [view(work, 6 * GE + a * GE, (2, GE), BF16) for a in range(2)]
        mask = view(work, 8 * GE, (2, GE), BF16)
        spots = view(work, 9 * GE, (2, GE), BF16)
        codes = big[:, :].bitcast(BF16)

        banks = [ctx.enter_context(nc.psum_tensor(f"bank{i}", [P, 512], F32)) for i in range(8)]
        mixed, hidden, back = banks[0:2], banks[2:4], banks[4:6]

        x_cleared = sem("x_cleared")
        x_loaded = sem("x_loaded")
        consts = sem("consts")
        ids_cleared = sem("ids_cleared")
        ids_loaded = sem("ids_loaded")
        weights_loaded = sem("weights_loaded")
        w_ready = sem("w_ready")
        seg_totals = sem("seg_totals")
        seg_before = sem("seg_before")
        codes_ready = sem("codes_ready")
        codes_saved = sem("codes_saved")
        codes_loaded = sem("codes_loaded")
        srcf_ready = sem("srcf_ready")
        src_turned = sem("src_turned")
        hist_zero = sem("hist_zero")
        hist_src = sem("hist_src")
        hist_dst = sem("hist_dst")
        hist_src_used = sem("hist_src_used")
        hist_dst_used = sem("hist_dst_used")
        hist_done = sem("hist_done")
        hist_rows = sem("hist_rows")
        hist_base = sem("hist_base")
        cols_ready = sem("cols_ready")
        cols_saved = sem("cols_saved")
        cols_loaded = sem("cols_loaded")
        tables_ready = sem("tables_ready")
        heads_ready = sem("heads_ready")
        node_list_ready = sem("node_list_ready")
        ln_var = sem("ln_var")
        pool_steps = sem("pool_steps")
        dve_steps = sem("dve_steps")
        node_list = sem("node_list")
        rk_zeroed = sem("rk_zeroed")
        ln_std = sem("ln_std")
        ln_done = sem("ln_done")
        rows_turned_up = sem("rows_turned_up")
        xt_ready = sem("xt_ready")
        ab_ready = sem("ab_ready")
        a_ready = sem("a_ready")
        b_ready = sem("b_ready")
        a_saved = sem("a_saved")
        b_saved = sem("b_saved")
        compact = sem("compact")
        split_done = sem("split_done")
        mixed_done = sem("mixed_done")
        spots_ready = sem("spots_ready")
        relu_done = sem("relu_done")
        hidden_done = sem("hidden_done")
        hot_done = sem("hot_done")
        scanned = sem("scanned")
        backed = sem("backed")
        out_copied = sem("out_copied")
        idx_ready = sem("idx_ready")
        nodes_cleared = sem("nodes_cleared")
        ends_gathered = sem("ends_gathered")
        rows_ready = sem("rows_ready")
        rk_rows = sem("rk_rows")
        rk_hot = sem("rk_hot")
        rk_prefix = sem("rk_prefix")
        rk_turned = sem("rk_turned")
        rk_turned_sb = sem("rk_turned_sb")
        rk_base = sem("rk_base")
        rk_sel = sem("rk_sel")
        rk_place = sem("rk_place")
        rk_placed = sem("rk_placed")
        perm_ready = sem("perm_ready")
        keep_hot = sem("keep_hot")
        keep_used = sem("keep_used")
        keep_sb = sem("keep_sb")
        keep_saved = sem("keep_saved")
        keep_loaded = sem("keep_loaded")
        fin_turned = sem("fin_turned")
        fin_t = sem("fin_t")
        fin_h1 = sem("fin_h1")
        fin_act = sem("fin_act")
        fin_h2 = sem("fin_h2")
        fin_rows = sem("fin_rows")
        fin_saved = sem("fin_saved")
        fin_copied = sem("fin_copied")
        fin_w = sem("fin_w")
        list_copied = sem("list_copied")
        a_gather = sem("a_gather")
        rk_used = sem("rk_used")
        rk_step = sem("rk_step")
        may_gather = sem("may_gather")
        gathered = [sem(f"gathered{i}") for i in range(IT)]
        stored = [sem(f"stored{i}") for i in range(2)]

        def some(n):
            return not (isinstance(n, int) and n <= 0)

        def chunks(ap):
            return ap.rearrange("(c p) f -> p c f", p=P)

        def row(ap):
            return ap.rearrange("(a n) -> a n", a=1)

        dst_i, prev_i, src_i = (view(big, i * GE, (GE,), I32)[0:GROUPS] for i in range(3))
        dst_f, src_f, head, cum, ones_e, seg = (view(big, (3 + i) * GE, (GE,))[0:GROUPS] for i in range(6))
        sign = view(big, 9 * GE, (GE,))[0:GROUPS]
        code_b = view(big, 10 * GE, (GE,), BF16)[0:GROUPS]
        rel = view(big, 11 * GE, (GE,))[0:GROUPS]
        sm = 12 * GE
        base_i = view(big, sm, (GROUP,), I32)[0:GROUPS]
        base_f = view(big, sm + 8, (GROUP,))[0:GROUPS]
        seg_i = view(big, sm + 16, (GE,), I32)[0:GROUPS]
        head_seg = view(big, sm + 16 + GE, (GE,))[0:GROUPS]
        seg_last = view(big, sm + 16 + 2 * GE, (1,), I32)[0:GROUPS]
        hp = 16 * GE
        src_hi, src_lo, dst_hi, dst_lo = (view(big, hp + i * TILES, (TILES,)) for i in range(4))
        src_ci, dst_ci, head_ci, tmp_ci = (view(big, hp + (4 + i) * TILES, (TILES,), I32) for i in range(4))
        hq = hp + 8 * TILES
        iota_hi = view(big, hq, (HI,))
        iota_lo = view(big, hq + 64, (LO,))
        c_sb = view(big, hq + 128, (2 * LO,))[0:HI]
        c_cum = view(big, hq + 256, (2 * LO,))[0:HI]
        c_base = view(big, hq + 384, (2,))[0:HI]
        c_end = view(big, hq + 392, (2 * LO,))[0:HI]
        c_has = view(big, hq + 520, (2 * LO,))[0:HI]
        c_none = view(big, hq + 648, (2 * LO,))[0:HI]
        ones_h = view(big, hq + 776, (2 * LO,))[0:HI]
        c_out = view(big, hq + 904, (4, LO))[0:HI]
        cols_f = view(big, hq + 1160, (4, CH))
        zeros_b = view(big, hq + 1260, (2 * LO,), BF16)
        ring_region = ring[:, :, :, :].rearrange("p a j d -> p (a j d)")
        hot_src_hi = view(ring_region, 0, (IT, HI), BF16)
        hot_src_lo = view(ring_region, IT * HI // 2, (IT, LO), BF16)
        hot_dst_hi = view(ring_region, IT * (HI + LO) // 2, (IT, HI), BF16)
        hot_dst_lo = view(ring_region, IT * (2 * HI + LO) // 2, (IT, LO), BF16)

        def edges_2d(ap, lo, hi):
            return ap[lo * GE:hi * GE].rearrange("(q r) -> q r", r=GE)

        rk_row = view(work, 0, (IT * P,))
        rk_hot_hi = view(work, 1024, (IT, HI), BF16)
        rk_hot_lo = view(work, 1280, (IT, LO), BF16)
        rk_hi_t = view(work, 1600, (IT, P))[0:HI]
        rk_bases = view(work, 2624, (IT + 1, LO))[0:HI]
        rk_prod = view(work, 3264, (IT, LO))
        rk_junk = view(work, 3776, (P,))
        rk_prior = view(work, 3904, (IT,))
        rk_within = view(work, 3912, (IT,))
        rk_rank = view(work, 3920, (IT,), I32)
        rk_p_i = view(work, 3928, (IT,), I32)
        rk_t_i = view(work, 3936, (IT,), I32)
        rk_p = view(work, 3944, (IT,))
        rk_t = view(work, 3952, (IT,))
        rk_l1 = view(work, 3968, (IT, P), FP16)
        rk_l2 = view(work, 4480, (IT, P), FP16)
        rk_r = view(work, 4992, (2, TILES), FP16)
        rb = 0
        rk_src = view(big, rb, (TILES,))
        rk_hi = view(big, rb + 416, (TILES,))
        rk_lo = view(big, rb + 832, (TILES,))
        rk_tmp = view(big, rb + 1248, (TILES,), I32)
        rk_iota_hi = view(big, rb + 1664, (HI,))
        rk_iota_lo = view(big, rb + 1728, (LO,))
        rk_iota_p = view(big, rb + 1792, (P,), FP16)
        rk_iota_t = view(big, rb + 1856, (GE,), FP16)
        rk_tile = view(big, rb + 2112, (TILES,))
        rk_pcol = view(big, rb + 2528, (1,))
        rk_zero = view(big, rb + 2536, (GE,), FP16)
        after = view(big, rb + 2800, (P,))
        keep_i = view(big, rb + 2928, (CH,), I32)
        keep_t_i = view(big, rb + 2960, (CH,), I32)
        keep_hi = view(big, rb + 2992, (CH,))
        keep_lo = view(big, rb + 3024, (CH,))
        keep_l = view(big, rb + 3072, (2, P), FP16)
        keep_r = view(big, rb + 3200, (2, GE), FP16)
        keep_q = view(big, rb + 3712, (GE,), BF16)[0:GROUPS]
        rk_perm = view(big, rb + 3968, (TILES,))
        rk_ident = view(big, rb + 4400, (P,), BF16)

        fv1 = view(big, 0, (2, 2 * D))
        fv2 = view(big, 512, (2, D))
        fc1 = view(big, 768, (2,))
        fc2, fgamma, fbeta = (view(big, 776 + i * D, (D,)) for i in range(3))
        fin_xt = view(big, 1280, (2, NP))
        fin_g = view(big, 1280 + 2 * NP, (2, NP))
        fin_y = view(big, 1280 + 4 * NP, (CH, D))
        fin_tmp = view(big, 1280 + 5 * NP, (CH, D))

        block = ctx.enter_context(nc.Block())

        @block.sync
        def _(sp):
            sp.wait_ge(x_cleared, 1)
            sp.dma_start(xres[:, 0:CH - 1, :], chunks(x[0:(CH - 1) * P, :])).then_inc(x_loaded, 16)
            sp.dma_start(xres[0:NLAST, CH - 1, :], x[(CH - 1) * P:N, :]).then_inc(x_loaded, 16)
            sp.wait_ge(ids_cleared, 1)
            for buf, ids in ((dst_i, dst), (src_i, src)):
                sp.dma_start(buf[0:FULLROWS, :], edges_2d(ids, 0, FULLROWS)).then_inc(ids_loaded, 16)
                sp.dma_start(buf[FULLROWS:GROUPS, 0:TAIL], row(ids[FULLROWS * GE:E])).then_inc(ids_loaded, 16)
            sp.dma_start(prev_i[0:1, 1:GE], row(dst[0:GE - 1])).then_inc(ids_loaded, 16)
            sp.dma_start(prev_i[1:FULLROWS, :],
                         dst[GE - 1:FULLROWS * GE - 1].rearrange("(q r) -> q r", r=GE)).then_inc(ids_loaded, 16)
            sp.dma_start(prev_i[FULLROWS:GROUPS, 0:TAIL + 1],
                         row(dst[FULLROWS * GE - 1:E])).then_inc(ids_loaded, 16)
            for l in range(LAYERS):
                for ap, w in ((w_ab[:, l, 0:D], w1[l][0:D, :]), (w_ab[:, l, D:2 * D], w1[l][D:2 * D, :]),
                              (w2_sb[:, l, :], w2[l][:, :]), (b1_sb[:, l, :], b1[l].partition_broadcast(P)),
                              (b2_sb[:, l, :], b2[l].partition_broadcast(P))):
                    sp.dma_start(ap, w).then_inc(weights_loaded, 16)
            sp.wait_ge(codes_ready, 1)
            sp.dma_start(code_row.rearrange("(q r) -> q r", r=GE), code_b[:, :]).then_inc(codes_saved, 16)
            sp.dma_start(base_row.rearrange("(q r) -> q r", r=GROUP), base_i[:, :]).then_inc(codes_saved, 16)
            sp.dma_start(srcf_row.rearrange("(q r) -> q r", r=GE), src_f[:, :]).then_inc(codes_saved, 16)
            sp.dma_start(count_row.rearrange("(q r) -> q r", r=1), seg_last[:, :]).then_inc(codes_saved, 16)
            sp.wait_ge(codes_saved, 64)
            sp.dma_start(base_sb[:, :], row(base_row)).then_inc(codes_loaded, 16)
            sp.dma_start(counter[0:1, 0:1], row(count_row[GROUPS - 1:GROUPS])).then_inc(codes_loaded, 16)
            sp.wait_ge(cols_ready, 1)
            sp.dma_start(node_cols.rearrange("k (h l) -> h k l", l=LO), c_out[:, :, :]).then_inc(cols_saved, 16)
            sp.wait_ge(cols_saved, 16)
            with nc.allow_non_contiguous_dma(reason="3200 node words, once"):
                for k in range(4):
                    sp.dma_start(cols_f[:, k, :], node_cols[k].rearrange("(c p) -> p c", p=P)).then_inc(cols_loaded, 16)
            sp.wait_ge(tables_ready, 1)
            sp.wait_ge(node_list_ready, 1)
            piece = EP // 8
            for i in range(8):
                sp.dma_start(codes[:, i * piece:(i + 1) * piece],
                             code_row[i * piece:(i + 1) * piece].partition_broadcast(P)).then_inc(codes_loaded, 16)

            def store(g, a, base, first):
                sp.wait_ge(out_copied, base + g + 1)
                sp.dma_start(run_rows[bass.ds(g * GE, GE), :].rearrange("(j p) f -> p j f", p=P),
                             outb[:, a, :, :]).then_inc(stored[a], 16)

            for l in range(LAYERS + 1):
                base = l * GROUPS
                if l < LAYERS:
                    sp.wait_ge(a_ready, 13 * (l + 1))
                    sp.dma_start(chunks(a_rows), rows_a[:, :, :]).then_inc(a_saved, 16)
                    sp.wait_ge(b_ready, 13 * (l + 1))
                    sp.dma_start(chunks(b_rows), rows_b[:, :, :]).then_inc(b_saved, 16)
                else:
                    sp.wait_ge(ln_done, 1)
                    def load_sources(it):
                        if some(it):
                            sp.wait_ge(rk_used, it)
                        sp.dma_start(rk_row[:, :],
                                     srcf_row[bass.ds(it * IT * P, IT * P)].partition_broadcast(P)).then_inc(rk_rows, 16)

                    load_sources(0)
                    with sp.Fori(1, ITER) as it:
                        load_sources(it)
                    sp.wait_ge(keep_sb, 1)
                    sp.dma_start(keep_row.rearrange("(q r) -> q r", r=GE), keep_q[:, :]).then_inc(keep_saved, 16)
                    sp.wait_ge(keep_saved, 16)
                    sp.wait_ge(perm_ready, 1)
                    for i in range(8):
                        sp.dma_start(codes[:, i * piece:(i + 1) * piece],
                                     keep_row[i * piece:(i + 1) * piece].partition_broadcast(P)).then_inc(keep_loaded, 16)
                with sp.Fori(0, ITER) as it:
                    for a in range(2):
                        store(it * 2 + a, a, base, False)
                if l == LAYERS:
                    sp.wait_ge(scanned, (LAYERS + 1) * GROUPS)
                    sp.dma_start(fv1[:, :, :], v1.rearrange("(s p) n -> p s n", p=P)).then_inc(fin_w, 16)
                    sp.dma_start(fv2[:, :, :], v2.rearrange("(s p) n -> p s n", p=P)).then_inc(fin_w, 16)
                    with nc.allow_non_contiguous_dma(reason="256 words, once"):
                        sp.dma_start(fc1[:, :], c1.rearrange("(m p) -> p m", p=P)).then_inc(fin_w, 16)
                    for ap, v in ((fc2, c2), (fgamma, gamma), (fbeta, beta)):
                        sp.dma_start(ap, v.partition_broadcast(P)).then_inc(fin_w, 16)
                    sp.wait_ge(fin_rows, 1)
                    sp.dma_start(chunks(out[0:(CH - 1) * P, :]), rows_a[:, 0:CH - 1, :]).then_inc(fin_saved, 16)
                    sp.dma_start(out[(CH - 1) * P:N, :], rows_a[0:NLAST, CH - 1, :]).then_inc(fin_saved, 16)
            sp.wait_ge(fin_saved, 32)

        @block.gpsimd
        def _(pool):
            taken = [0]

            def step(ins):
                taken[0] += 1
                ins.then_inc(pool_steps, 1)
                pool.wait_ge(pool_steps, taken[0])

            step(nc.gpsimd.memset(ident[:, :], 0.0))
            step(nc.gpsimd.affine_select(out=ident[:, :], in_=ident[:, :], compare_op=ALU.not_equal, fill=1.0,
                                         base=0, pattern=[[-1, P]], channel_multiplier=1))
            step(nc.gpsimd.memset(before[:, :], 0.0))
            step(nc.gpsimd.affine_select(out=before[:, :], in_=before[:, :], compare_op=ALU.is_ge, fill=1.0,
                                         base=0, pattern=[[-1, P]], channel_multiplier=1))
            step(nc.gpsimd.iota(place[:, :], pattern=[[P, 2]], base=1, channel_multiplier=1,
                                allow_small_or_imprecise_dtypes=True))
            step(nc.gpsimd.iota(iota_hi[:, :], pattern=[[1, HI]], base=0, channel_multiplier=0,
                                allow_small_or_imprecise_dtypes=True))
            nc.gpsimd.iota(iota_lo[:, :], pattern=[[1, LO]], base=0, channel_multiplier=0,
                                allow_small_or_imprecise_dtypes=True).then_inc(consts, 1)

            pool.wait_ge(codes_loaded, 32)
            pool.wait_ge(heads_ready, 1)
            occurring = pool.value_load(counter[0:1, 0:1], min_val=0, max_val=NP)
            with pool.If(occurring != N):
                with nc.allow_non_contiguous_dma(reason="3200 words, only where nodes lack edges"):
                    pool.dma_start(chunks(seg_node), list_idx[:, :].unsqueeze(2)).then_inc(node_list, 16)
                pool.wait_ge(node_list, 16)
                with pool.Fori(0, TILES) as t:
                    nc.gpsimd.tensor_copy(list_at[:, 0:1], head_ci[:, bass.ds(t, 1)]).then_inc(list_copied, 1)
                    nc.gpsimd.tensor_copy(list_val[:, 0:1], dst_ci[:, bass.ds(t, 1)]).then_inc(list_copied, 1)
                    pool.wait_ge(list_copied, 2 * t + 2)
                    nc.gpsimd.sem_inc(may_gather, 1)
                    nc.gpsimd.indirect_dma_start(seg_node, bass.IndirectOffsetOnAxis(ap=list_at[:, 0:1], axis=0),
                                                 list_val[:, 0:1], None, bounds_check=NP - 1,
                                                 oob_is_err=False).then_inc(node_list, 16)
                    pool.wait_ge(node_list, 16 * t + 32)
                with nc.allow_non_contiguous_dma(reason="3200 words, only where nodes lack edges"):
                    pool.dma_start(list_idx[:, :].unsqueeze(2), chunks(seg_node)).then_inc(node_list, 16)
                pool.wait_ge(node_list, 16 * TILES + 32)
                nc.gpsimd.sem_inc(node_list_ready, 1)
            with pool.Else():
                nc.gpsimd.sem_inc(node_list_ready, 1)

            def gather_group(g, it, a, base, table, cols):
                for j in range(GROUP):
                    if some(base // 2 + it):
                        pool.wait_ge(gathered[a * GROUP + j], 16 * (base // 2 + it))
                nc.gpsimd.tensor_copy(idx[:, a, :], cols[:, bass.ds(g * GROUP, GROUP)]).then_inc(idx_ready, 1)
                pool.wait_ge(idx_ready, base + g + 1)
                if some(base + g - 1):
                    pool.wait_ge(mixed_done, base + g - 1)
                nc.gpsimd.sem_inc(may_gather, 1)
                for j in range(GROUP):
                    nc.gpsimd.indirect_dma_start(
                        ring[:, a, j, :], None, table,
                        bass.IndirectOffsetOnAxis(ap=idx[:, a, j:j + 1], axis=0)).then_inc(gathered[a * GROUP + j], 16)

            for l in range(LAYERS + 1):
                base = l * GROUPS
                if l < LAYERS:
                    pool.wait_ge(a_saved, 16 * (l + 1))
                    with pool.If(occurring != N):
                        for c in range(CH):
                            nc.gpsimd.indirect_dma_start(rows_a[:, c, :], None, a_rows,
                                                         bass.IndirectOffsetOnAxis(ap=list_idx[:, c:c + 1], axis=0),
                                                         bounds_check=NP - 1, oob_is_err=False).then_inc(a_gather, 16)
                        pool.wait_ge(a_gather, 16 * CH * (l + 1))
                        nc.gpsimd.sem_inc(compact, 1)
                    with pool.Else():
                        nc.gpsimd.sem_inc(compact, 1)
                    pool.wait_ge(b_saved, 16 * (l + 1))
                    table, cols = b_rows, src_cols
                else:
                    pool.wait_ge(backed, base)
                    step(nc.gpsimd.iota(rk_iota_hi[:, :], pattern=[[1, HI]], base=0, channel_multiplier=0,
                                        allow_small_or_imprecise_dtypes=True))
                    step(nc.gpsimd.iota(rk_iota_lo[:, :], pattern=[[1, LO]], base=0, channel_multiplier=0,
                                        allow_small_or_imprecise_dtypes=True))
                    step(nc.gpsimd.iota(rk_iota_p[:, :], pattern=[[1, P]], base=0, channel_multiplier=0,
                                        allow_small_or_imprecise_dtypes=True))
                    step(nc.gpsimd.iota(rk_iota_t[:, :], pattern=[[1, GE]], base=0, channel_multiplier=0,
                                        allow_small_or_imprecise_dtypes=True))
                    step(nc.gpsimd.iota(rk_tile[:, :], pattern=[[1, TILES]], base=0, channel_multiplier=0,
                                        allow_small_or_imprecise_dtypes=True))
                    step(nc.gpsimd.iota(rk_pcol[:, :], pattern=[[0, 1]], base=0, channel_multiplier=1,
                                        allow_small_or_imprecise_dtypes=True))
                    step(nc.gpsimd.memset(after[:, :], 0.0))
                    nc.gpsimd.affine_select(out=after[:, :], in_=after[:, :], compare_op=ALU.is_ge, fill=1.0,
                                                 base=0, pattern=[[1, P]], channel_multiplier=-1).then_inc(consts, 1)
                    pool.wait_ge(perm_ready, 1)
                    table, cols = attr, perm_cols
                for it in (0, 1):
                    for a in range(2):
                        gather_group(2 * it + a, it, a, base, table, cols)
                with pool.Fori(2, ITER) as it:
                    for a in range(2):
                        gather_group(it * 2 + a, it, a, base, table, cols)
                pool.wait_ge(nodes_cleared, l + 1)
                for a in range(2):
                    pool.wait_ge(stored[a], 16 * ITER * (l + 1))
                ends = end_dst if l < LAYERS else end_src
                for c in range(CH):
                    nc.gpsimd.indirect_dma_start(nodes[:, c, :], None, run_rows,
                                                 bass.IndirectOffsetOnAxis(ap=ends[:, c:c + 1], axis=0),
                                                 bounds_check=EP - 1, oob_is_err=False).then_inc(ends_gathered, 16)

        @block.tensor
        def _(pe):
            pe.wait_ge(seg_totals, 1)
            pe.wait_ge(consts, 1)
            nc.tensor.matmul(banks[7][0:GROUPS, 0:1], before[0:GROUPS, 0:GROUPS], cum[:, GE - 1:GE],
                                  start=True, stop=True).then_inc(seg_before, 1)
            pe.wait_ge(srcf_ready, 1)
            for k, rows in enumerate((src_f, dst_f, head_seg)):
                if k == 2:
                    pe.wait_ge(codes_ready, 1)
                for j in range(GROUP):
                    last = nc.tensor.transpose(banks[k][:, j * P:j * P + GROUPS], rows[:, j * P:(j + 1) * P],
                                               ident[0:GROUPS, 0:GROUPS])
                last.then_inc(src_turned, 1)
            pe.wait_ge(hist_zero, 1)
            nc.tensor.matmul(banks[6][0:HI, 0:2 * LO], zeros_b[:, 0:HI], zeros_b[:, :], start=True, stop=False)
            def count_edges(it):
                pe.wait_ge(hist_src, it + 1)
                for j in range(IT):
                    last = nc.tensor.matmul(banks[6][0:HI, 0:LO], hot_src_hi[:, j, :], hot_src_lo[:, j, :],
                                            start=False, stop=False, skip_group_check=True)
                last.then_inc(hist_src_used, 1)
                pe.wait_ge(hist_dst, it + 1)
                for j in range(IT):
                    last = nc.tensor.matmul(banks[6][0:HI, LO:2 * LO], hot_dst_hi[:, j, :], hot_dst_lo[:, j, :],
                                            start=False, stop=False, skip_group_check=True)
                last.then_inc(hist_dst_used, 1)

            count_edges(0)
            with pe.Fori(1, ITER) as it:
                count_edges(it)
            nc.tensor.matmul(banks[6][0:HI, 0:2 * LO], zeros_b[:, 0:HI], zeros_b[:, :], start=False, stop=True).then_inc(hist_done, 1)
            pe.wait_ge(hist_rows, 1)
            for k in range(2):
                last = nc.tensor.matmul(banks[7][0:HI, 8 * k:8 * k + 1], before[0:HI, 0:HI],
                                        c_cum[:, (k + 1) * LO - 1:(k + 1) * LO], start=True, stop=True)
            last.then_inc(hist_base, 1)

            def mix(g, a, base, bases, conv):
                if some(base + g - 1):
                    pe.wait_ge(relu_done if conv else scanned, base + g - 1)
                if conv:
                    pe.wait_ge(hot_done, base + g + 1)
                for j in range(GROUP):
                    pe.wait_ge(gathered[a * GROUP + j], bases[1])
                    to = mixed[a][:, j * P:(j + 1) * P]
                    if not conv:
                        last = nc.tensor.transpose(to, ring[:, a, j, :], ident[:, :])
                        continue
                    nc.tensor.matmul(to, ring[:, a, j, :], ident[:, :], is_transpose=True, start=True, stop=False)
                    for k in range(2):
                        for part in range(3):
                            at = (bases[0][a * GROUP + j] + k) * (3 * D) + part * D
                            last = nc.tensor.matmul(to, flat_parts[:, bass.ds(at, D)], onehot[a][:, k, j * P:(j + 1) * P],
                                                    start=False, stop=(k == 1 and part == 2))
                last.then_inc(mixed_done, 1)

            def second(g, a, base, l):
                pe.wait_ge(relu_done, base + g + 1)
                if some(base + g - 1):
                    pe.wait_ge(scanned, base + g - 1)
                nc.tensor.matmul(hidden[a][:, :], w2_sb[:, l, :], hin[:, a, :], start=True, stop=True).then_inc(hidden_done, 1)

            def turn_back(g, a, base):
                pe.wait_ge(scanned, base + g + 1)
                if some(base + g - 1):
                    pe.wait_ge(out_copied, base + g - 1)
                for j in range(GROUP):
                    last = nc.tensor.transpose(back[a][:, j * P:(j + 1) * P], run[:, a, j * P:(j + 1) * P], ident[:, :])
                last.then_inc(backed, 1)

            flat_parts = a_parts[:, :, :, :].rearrange("p c k d -> p (c k d)")

            def edge_pass(l):
                base, conv = l * GROUPS, l < LAYERS

                def iteration(it):
                    landed = 16 * (base // 2) + it * 16 + 16
                    bases = None
                    if conv:
                        _, bases = nc.values_load_multi_w_load_instructions(
                            base_sb[0:1, bass.ds(it * IT, IT)], engines=[mybir.EngineType.PE], min_val=0, max_val=CH - 1)
                    for a in range(2):
                        g = it * 2 + a
                        mix(g, a, base, (bases, landed), conv)
                        if conv and not (isinstance(g, int) and g < 1):
                            second(g - 1, 1 - a, base, l)
                        if not (isinstance(g, int) and g < 2):
                            turn_back(g - 2, a, base)

                iteration(0)
                iteration(1)
                with pe.Fori(2, ITER) as it:
                    iteration(it)
                if conv:
                    second(GROUPS - 1, 1, base, l)
                turn_back(GROUPS - 2, 0, base)
                turn_back(GROUPS - 1, 1, base)

            for l in range(LAYERS):
                pe.wait_ge(rows_ready, l + 1)
                for k in range(7):
                    if some(7 * l + k - 1):
                        pe.wait_ge(xt_ready, 7 * l + k - 1)
                    for c in range(4 * k, min(4 * k + 4, CH)):
                        last = nc.tensor.transpose(mixed[k % 2][:, (c % 4) * P:(c % 4 + 1) * P], nodes[:, c, :], ident[:, :])
                    last.then_inc(rows_turned_up, 1)
                if l == 0:
                    pe.wait_ge(w_ready, 1)
                for k in range(13):
                    pe.wait_ge(xt_ready, 7 * l + min(7, (2 * k + 1) // 4 + 1))
                    if k >= 2 or l >= 1:
                        if some(13 * l + k - 1):
                            pe.wait_ge(a_ready, 13 * l + k - 1)
                        if some(13 * l + k - 1):
                            pe.wait_ge(b_ready, 13 * l + k - 1)
                    if l >= 1 and k < 2:
                        pe.wait_ge(scanned, l * GROUPS)
                    for c in range(2 * k, min(2 * k + 2, CH)):
                        last = nc.tensor.matmul(hidden[k % 2][:, (c % 2) * 2 * D:(c % 2 + 1) * 2 * D],
                                                xt[:, c * P:(c + 1) * P], w_ab[:, l, :], start=True, stop=True)
                    last.then_inc(ab_ready, 1)
                pe.wait_ge(split_done, l + 1)
                pe.wait_ge(codes_loaded, 32 + 8 * 16)
                edge_pass(l)

            pe.wait_ge(rk_zeroed, 1)
            for k in range(2):
                nc.tensor.matmul(banks[6 + k][:, :], rk_zero[:, 0:P], rk_zero[:, :], start=True, stop=False)
            def place_edges(it):
                pe.wait_ge(rk_hot, it + 1)
                for t in range(IT):
                    last = nc.tensor.matmul(banks[0][0:HI, t * LO:IT * LO].rearrange("h (t l) -> h t l", l=LO),
                                            rk_hot_hi[:, t, :],
                                            rk_hot_lo[:, t:t + 1, :].to_broadcast((P, IT - t, LO)),
                                            start=(t == 0), stop=(t == IT - 1))
                last.then_inc(rk_prefix, 1)
                for t in range(IT):
                    last = nc.tensor.transpose(banks[1][:, :].bitcast(BF16)[0:HI, t * P:(t + 1) * P],
                                               rk_hot_hi[:, t, :], rk_ident[:, :])
                last.then_inc(rk_turned, 1)
                pe.wait_ge(rk_turned_sb, it + 1)
                pe.wait_ge(rk_base, it + 1)
                for t in range(IT):
                    last = nc.tensor.matmul(banks[2][:, t * LO:(t + 1) * LO], rk_hi_t[:, t, :], rk_bases[:, t, :],
                                            start=True, stop=True)
                last.then_inc(rk_sel, 1)
                for t in range(IT):
                    pe.wait_ge(rk_place, it * IT + (t + 1))
                    nc.tensor.matmul(banks[6][:, 0:TILES], rk_l1[:, t, :], rk_r[:, t % 2, :], start=False, stop=False,
                                     skip_group_check=True)
                    nc.tensor.matmul(banks[7][:, 0:TILES], rk_l2[:, t, :], rk_r[:, t % 2, :], start=False, stop=False,
                                          skip_group_check=True).then_inc(rk_placed, 1)

            place_edges(0)
            with pe.Fori(1, ITER) as it:
                place_edges(it)
            for k in range(2):
                last = nc.tensor.matmul(banks[6 + k][:, :], rk_zero[:, 0:P], rk_zero[:, :], start=False, stop=True)
            last.then_inc(rk_placed, 1)
            for c in range(CH):
                pe.wait_ge(keep_hot, c + 1)
                nc.tensor.matmul(banks[3][0:GROUPS, :], keep_l[:, c % 2, 0:GROUPS], keep_r[:, c % 2, :],
                                      start=(c == 0), stop=(c == CH - 1)).then_inc(keep_used, 1)
            edge_pass(LAYERS)

            def tail_second(pe, k):
                pe.wait_ge(fin_act, 2 * k + 2)
                if some(k - 1):
                    pe.wait_ge(fin_copied, k - 1)
                for c in range(4 * k, min(4 * k + 4, CH)):
                    for m in range(2):
                        last = nc.tensor.matmul(back[k % 2][:, (c % 4) * D:(c % 4 + 1) * D],
                                                fin_g[:, m, c * P:(c + 1) * P], fv2[:, m, :], start=(m == 0), stop=(m == 1))
                last.then_inc(fin_h2, 1)

            pe.wait_ge(ends_gathered, 16 * CH * (LAYERS + 1))
            pe.wait_ge(ln_done, 1)
            for s, rows in enumerate((nodes, rows_a)):
                for k in range(7):
                    n = 7 * s + k
                    if some(n - 1):
                        pe.wait_ge(fin_t, n - 1)
                    for c in range(4 * k, min(4 * k + 4, CH)):
                        last = nc.tensor.transpose(mixed[n % 2][:, (c % 4) * P:(c % 4 + 1) * P], rows[:, c, :], ident[:, :])
                    last.then_inc(fin_turned, 1)
            pe.wait_ge(fin_t, 14)
            pe.wait_ge(fin_w, 96)
            for k in range(7):
                w = min(512, NP - 512 * k)
                for m in range(2):
                    n = 2 * k + m
                    if some(n - 1):
                        pe.wait_ge(fin_act, n - 1)
                    for s in range(2):
                        last = nc.tensor.matmul(hidden[m][:, 0:w], fv1[:, s, m * P:(m + 1) * P],
                                                fin_xt[:, 1 - s, k * 512:k * 512 + w], start=(s == 0), stop=(s == 1))
                    last.then_inc(fin_h1, 1)
                if k >= 1:
                    tail_second(pe, k - 1)
            tail_second(pe, 6)


        @block.scalar
        def _(act):
            def root(n):
                act.wait_ge(ln_var, n)
                nc.scalar.sqrt(stat[:, 1, :], stat[:, 0, :]).then_inc(ln_std, 1)

            def spot(g, a, base):
                if some(base + g - 1):
                    act.wait_ge(hot_done, base + g - 1)
                nc.scalar.activation(spots[:, a, :], codes[:, bass.ds(g * GE, GE)], ACT.Abs).then_inc(spots_ready, 1)

            def relu(g, a, base):
                act.wait_ge(mixed_done, base + g + 1)
                if some(base + g - 1):
                    act.wait_ge(hidden_done, base + g - 1)
                nc.scalar.activation(hin[:, a, :], mixed[a][:, :], ACT.Relu).then_inc(relu_done, 1)

            def copy_out(g, a, it, base):
                act.wait_ge(backed, base + g + 1)
                if some(base // 2 + it):
                    act.wait_ge(stored[a], 16 * (base // 2 + it))
                nc.scalar.copy(outb[:, a, :, :].rearrange("p j d -> p (j d)"), back[a][:, :]).then_inc(out_copied, 1)

            root(1)
            for l in range(LAYERS + 1):
                base, conv = l * GROUPS, l < LAYERS
                if conv:
                    for a in range(2):
                        if l >= 1:
                            act.wait_ge(stored[a], 16 * ITER * l)
                    for k in range(7):
                        w = min(512, NP - 512 * k)
                        act.wait_ge(rows_turned_up, 7 * l + k + 1)
                        nc.scalar.copy(xt[:, k * 512:k * 512 + w], mixed[k % 2][:, 0:w]).then_inc(xt_ready, 1)
                    for k in range(13):
                        w = min(2, CH - 2 * k)
                        act.wait_ge(a_ready, 13 * l + k + 1)
                        nc.scalar.copy(rows_b[:, 2 * k:2 * k + w, :],
                                            hidden[k % 2][:, :].rearrange("p (c n) -> p c n", c=2)[:, 0:w, D:2 * D]).then_inc(b_ready, 1)
                    act.wait_ge(codes_loaded, 32 + 8 * 16)
                    act.wait_ge(b_saved, 16 * (l + 1))
                    act.wait_ge(split_done, l + 1)
                else:
                    root(2)
                    def copy_turned(it):
                        act.wait_ge(rk_turned, it + 1)
                        if some(it):
                            act.wait_ge(rk_sel, it)
                        nc.scalar.copy(rk_hi_t[:, :, :].rearrange("h t e -> h (t e)"),
                                            banks[1][:, :].bitcast(BF16)[0:HI, :]).then_inc(rk_turned_sb, 1)

                    copy_turned(0)
                    with act.Fori(1, ITER) as it:
                        copy_turned(it)

                def iteration(it):
                    for a in range(2):
                        g = it * 2 + a
                        if conv:
                            spot(g, a, base)
                            relu(g, a, base)
                        if not (isinstance(g, int) and g < 2):
                            copy_out(g - 2, a, it - 1, base)

                iteration(0)
                iteration(1)
                with act.Fori(2, ITER) as it:
                    iteration(it)
                copy_out(GROUPS - 2, 0, ITER - 1, base)
                copy_out(GROUPS - 1, 1, ITER - 1, base)
            for s in range(2):
                for k in range(7):
                    w = min(512, NP - 512 * k)
                    n = 7 * s + k
                    act.wait_ge(fin_turned, n + 1)
                    nc.scalar.copy(fin_xt[:, s, k * 512:k * 512 + w], mixed[n % 2][:, 0:w]).then_inc(fin_t, 1)
            act.wait_ge(fin_w, 96)
            for k in range(7):
                w = min(512, NP - 512 * k)
                for m in range(2):
                    act.wait_ge(fin_h1, 2 * k + m + 1)
                    nc.scalar.activation(fin_g[:, m, k * 512:k * 512 + w], hidden[m][:, 0:w], ACT.Silu,
                                              bias=fc1[:, m:m + 1]).then_inc(fin_act, 1)
            root(3)

        @block.vector
        def _(dve):
            taken = [0]

            def step(ins):
                taken[0] += 1
                ins.then_inc(dve_steps, 1)
                dve.wait_ge(dve_steps, taken[0])

            v = nc.vector

            def spread(col):
                return col.unsqueeze(2).to_broadcast((P, CH, D))

            def normalise(n, rows, centred, squares):
                step(v.tensor_reduce(stat[:, 2, :], rows, AX_X, ALU.add))
                step(v.tensor_scalar(stat[:, 3, :], stat[:, 2, :], -1.0 / D, None, ALU.mult))
                step(v.tensor_tensor(centred, rows, spread(stat[:, 3, :]), ALU.add))
                step(v.tensor_tensor(squares, centred, centred, ALU.mult))
                step(v.tensor_reduce(stat[:, 2, :], squares, AX_X, ALU.add))
                v.tensor_scalar(stat[:, 0, :], stat[:, 2, :], 1.0 / D, EPS, ALU.mult, ALU.add).then_inc(ln_var, 1)
                dve.wait_ge(ln_std, n)
                step(v.reciprocal(stat[:, 2, :], stat[:, 1, :]))

            v.memset(xres[:, CH - 1, :], 0.0).then_inc(x_cleared, 1)
            step(v.memset(prev_i[:, :], N))
            step(v.memset(prev_i[0:1, 0:1], -1))
            v.memset(dst_i[:, :], N)
            v.memset(src_i[:, :], N).then_inc(ids_cleared, 1)
            v.memset(list_idx[:, :], SKIP)
            v.memset(a_parts[:, CH, :, :], 0.0)
            v.memset(first_state[:, :], 0.0)
            v.memset(ones_e[:, :], 1.0)
            v.memset(ones_h[:, :], 1.0)
            step(v.memset(zeros_b[:, :], 0.0))

            dve.wait_ge(ids_loaded, 16 * 7)
            v.tensor_copy(src_f[:, :], src_i[:, :])
            v.tensor_copy(dst_f[:, :], dst_i[:, :])
            step(v.tensor_tensor(head[:, :], dst_i[:, :], prev_i[:, :], ALU.not_equal))
            v.tensor_tensor_scan(cum[:, :], ones_e[:, :], head[:, :], 0.0, ALU.mult, ALU.add).then_inc(seg_totals, 1)
            v.tensor_scalar(sign[:, :], head[:, :], -2.0, 1.0, ALU.mult, ALU.add)
            dve.wait_ge(seg_totals, 1)
            v.tensor_scalar(rel[:, :], head[:, :], -float(SKIP), float(SKIP - 1), ALU.mult, ALU.add).then_inc(srcf_ready, 1)
            dve.wait_ge(seg_before, 1)
            step(v.tensor_scalar(seg[:, :], cum[:, :], banks[7][0:GROUPS, 0:1], None, ALU.add))
            step(v.tensor_tensor(head_seg[:, :], seg[:, :], rel[:, :], ALU.add))
            step(v.tensor_scalar(seg[:, :], seg[:, :], -1.0, None, ALU.add))
            step(v.tensor_copy(seg_i[:, :], seg[:, :]))
            v.tensor_copy(seg_last[:, :], seg_i[:, GE - 1:GE])
            step(v.tensor_scalar(base_i[:, :], seg_i[:, 0:GE:P], 7, None, ALU.logical_shift_right))
            step(v.tensor_copy(base_f[:, :], base_i[:, :]))
            step(v.tensor_scalar(base_f[:, :], base_f[:, :], float(P), -1.0, ALU.mult, ALU.add))
            tiles = lambda ap: ap.rearrange("q (j r) -> q j r", r=P)
            step(v.tensor_tensor(tiles(rel[:, :]), tiles(seg[:, :]), base_f[:, :].unsqueeze(2).to_broadcast((GROUPS, GROUP, P)),
                                 ALU.subtract))
            v.tensor_tensor(code_b[:, :], rel[:, :], sign[:, :], ALU.mult).then_inc(codes_ready, 1)

            dve.wait_ge(src_turned, 3)
            for bank, cols in ((banks[0], src_cols), (banks[1], dst_ci), (banks[2], head_ci)):
                last = v.tensor_copy(cols[:, :].rearrange("p (q j) -> p j q", j=GROUP),
                                     bank[:, :].rearrange("p (j q) -> p j q", j=GROUP)[:, :, 0:GROUPS])
            last.then_inc(heads_ready, 1)
            dve.wait_ge(heads_ready, 1)
            for cols, hi, lo in ((src_cols, src_hi, src_lo), (dst_ci, dst_hi, dst_lo)):
                step(v.tensor_scalar(tmp_ci[:, :], cols[:, :], 6, None, ALU.logical_shift_right))
                step(v.tensor_copy(hi[:, :], tmp_ci[:, :]))
                step(v.tensor_scalar(tmp_ci[:, :], cols[:, :], LO - 1, None, ALU.bitwise_and))
                step(v.tensor_copy(lo[:, :], tmp_ci[:, :]))
            v.tensor_copy(src_ci[:, 0:1], tmp_ci[:, 0:1]).then_inc(hist_zero, 1)

            def one_hot(to, cols, it, table, width):
                return v.tensor_tensor(to, cols[:, bass.ds(it * IT, IT)].unsqueeze(2).to_broadcast((P, IT, width)),
                                       table.unsqueeze(1).to_broadcast((P, IT, width)), ALU.is_equal)

            dve.wait_ge(consts, 1)
            def one_hots_to_count(it):
                if some(it):
                    dve.wait_ge(hist_src_used, it)
                one_hot(hot_src_hi[:, :, :], src_hi, it, iota_hi[:, :], HI)
                one_hot(hot_src_lo[:, :, :], src_lo, it, iota_lo[:, :], LO).then_inc(hist_src, 1)
                if some(it):
                    dve.wait_ge(hist_dst_used, it)
                one_hot(hot_dst_hi[:, :, :], dst_hi, it, iota_hi[:, :], HI)
                one_hot(hot_dst_lo[:, :, :], dst_lo, it, iota_lo[:, :], LO).then_inc(hist_dst, 1)

            one_hots_to_count(0)
            with dve.Fori(1, ITER) as it:
                one_hots_to_count(it)
            dve.wait_ge(hist_done, 1)
            step(v.tensor_copy(c_sb[:, :], banks[6][0:HI, 0:2 * LO]))
            v.tensor_tensor_scan(c_cum[:, 0:LO], ones_h[:, 0:LO], c_sb[:, 0:LO], 0.0, ALU.mult, ALU.add)
            v.tensor_tensor_scan(c_cum[:, LO:2 * LO], ones_h[:, LO:2 * LO], c_sb[:, LO:2 * LO], 0.0,
                                      ALU.mult, ALU.add).then_inc(hist_rows, 1)
            v.tensor_scalar(c_has[:, :], c_sb[:, :], 0.0, None, ALU.is_gt)
            step(v.tensor_scalar(c_none[:, :], c_sb[:, :], 0.0, float(SKIP), ALU.is_equal, ALU.mult))
            dve.wait_ge(hist_base, 1)
            v.tensor_scalar(c_end[:, 0:LO], c_cum[:, 0:LO], banks[7][0:HI, 0:1], None, ALU.add)
            step(v.tensor_scalar(c_end[:, LO:2 * LO], c_cum[:, LO:2 * LO], banks[7][0:HI, 8:9], None, ALU.add))
            step(v.tensor_tensor(base_keep[0:HI, :], c_end[:, 0:LO], c_sb[:, 0:LO], ALU.subtract))
            v.scalar_tensor_tensor(c_out[:, 0, :], c_end[:, LO:2 * LO], -1.0, c_none[:, LO:2 * LO], ALU.add, ALU.add)
            v.scalar_tensor_tensor(c_out[:, 1, :], c_end[:, 0:LO], -1.0, c_none[:, 0:LO], ALU.add, ALU.add)
            v.tensor_tensor(c_out[:, 2, :], base_keep[0:HI, :], c_none[:, 0:LO], ALU.add)
            v.tensor_copy(c_out[:, 3, :], c_has[:, LO:2 * LO]).then_inc(cols_ready, 1)
            dve.wait_ge(cols_loaded, 64)
            v.tensor_copy(end_dst[:, :], cols_f[:, 0, :])
            v.tensor_copy(end_src[:, :], cols_f[:, 1, :])
            v.tensor_copy(first_src[:, :], cols_f[:, 2, :])
            v.tensor_copy(present[:, :], cols_f[:, 3, :]).then_inc(tables_ready, 1)

            dve.wait_ge(x_loaded, 32)
            normalise(1, xres[:, :, :], nodes[:, :, :], rows_a[:, :, :])
            v.scalar_tensor_tensor(nodes[:, :, :], nodes[:, :, :], 0.0, spread(stat[:, 2, :]), ALU.max, ALU.mult).then_inc(rows_ready, 1)
            dve.wait_ge(rows_ready, 1)
            dve.wait_ge(weights_loaded, 16 * 5 * LAYERS)
            v.tensor_tensor(w_ab[:, :, 0:D], w_ab[:, :, 0:D], w_ab[:, :, D:2 * D], ALU.subtract).then_inc(w_ready, 1)

            def hot(g, a, base):
                if some(base + g - 1):
                    dve.wait_ge(mixed_done, base + g - 1)
                if some(base + g - 1):
                    dve.wait_ge(scanned, base + g - 1)
                dve.wait_ge(spots_ready, base + g + 1)
                code = codes[:, bass.ds(g * GE, GE)]
                for k in range(2):
                    v.tensor_scalar(onehot[a][:, k, :], spots[:, a, :], place[:, k:k + 1], None, ALU.is_equal)
                v.tensor_scalar(mask[:, a, :], code, 0.0, -HUGE, ALU.is_lt, ALU.mult).then_inc(hot_done, 1)

            def scan(g, a, base, conv):
                dve.wait_ge(hidden_done if conv else mixed_done, base + g + 1)
                if some(base + g - 1):
                    dve.wait_ge(backed, base + g - 1)
                if some(base + g):
                    dve.wait_ge(scanned, base + g)
                state = first_state[:, :] if isinstance(g, int) and g == 0 else run[:, 1 - a, GE - 1:GE]
                if conv:
                    dve.wait_ge(hot_done, base + g + 1)
                    ins = v.tensor_tensor_scan(run[:, a, :], mask[:, a, :], hidden[a][:, :], state, ALU.add, ALU.max)
                else:
                    ins = v.tensor_tensor_scan(run[:, a, :], codes[:, bass.ds(g * GE, GE)], mixed[a][:, :], state,
                                               ALU.mult, ALU.add)
                ins.then_inc(scanned, 1)

            def edge_pass(l):
                base, conv = l * GROUPS, l < LAYERS

                def iteration(it):
                    for a in range(2):
                        g = it * 2 + a
                        if conv:
                            hot(g, a, base)
                        if not (isinstance(g, int) and g < 1):
                            scan(g - 1, 1 - a, base, conv)

                iteration(0)
                iteration(1)
                with dve.Fori(2, ITER) as it:
                    iteration(it)
                scan(GROUPS - 1, 1, base, conv)

            for l in range(LAYERS):
                for k in range(13):
                    w = min(2, CH - 2 * k)
                    dve.wait_ge(ab_ready, 13 * l + k + 1)
                    v.tensor_tensor(rows_a[:, 2 * k:2 * k + w, :],
                                         hidden[k % 2][:, :].rearrange("p (c n) -> p c n", c=2)[:, 0:w, 0:D],
                                         b1_sb[:, l:l + 1, :].to_broadcast((P, w, D)), ALU.add).then_inc(a_ready, 1)
                dve.wait_ge(compact, l + 1)
                rest = xt.rearrange("p (c d) -> p c d", c=CH)
                step(v.tensor_copy(a_parts[:, 0:CH, 0, :], rows_a[:, :, :]))
                step(v.tensor_tensor(rest, rows_a[:, :, :], a_parts[:, 0:CH, 0, :], ALU.subtract))
                step(v.tensor_copy(a_parts[:, 0:CH, 1, :], rest))
                step(v.tensor_tensor(rest, rest, a_parts[:, 0:CH, 1, :], ALU.subtract))
                v.tensor_copy(a_parts[:, 0:CH, 2, :], rest).then_inc(split_done, 1)
                dve.wait_ge(rows_turned_up, 7 * (l + 1))
                v.memset(nodes[:, :, :], 0.0).then_inc(nodes_cleared, 1)
                dve.wait_ge(codes_loaded, 32 + 8 * 16)
                dve.wait_ge(b_saved, 16 * (l + 1))
                dve.wait_ge(split_done, l + 1)
                edge_pass(l)
                dve.wait_ge(ends_gathered, 16 * CH * (l + 1))
                step(v.tensor_tensor(nodes[:, :, :], nodes[:, :, :], b2_sb[:, l:l + 1, :].to_broadcast((P, CH, D)), ALU.add))
                if l < LAYERS - 1:
                    v.scalar_tensor_tensor(nodes[:, :, :], nodes[:, :, :], 0.0, spread(present[:, :]),
                                                ALU.max, ALU.mult).then_inc(rows_ready, 1)
                    dve.wait_ge(rows_ready, l + 2)
                else:
                    step(v.tensor_tensor(nodes[:, :, :], nodes[:, :, :], spread(present[:, :]), ALU.mult))
                    step(v.tensor_tensor(xres[:, :, :], xres[:, :, :], nodes[:, :, :], ALU.add))
            normalise(2, xres[:, :, :], rows_a[:, :, :], rows_b)
            v.scalar_tensor_tensor(rows_a[:, :, :], rows_a[:, :, :], 0.0, spread(stat[:, 2, :]), ALU.max, ALU.mult).then_inc(ln_done, 1)
            dve.wait_ge(ln_done, 1)
            v.memset(nodes[:, :, :], 0.0).then_inc(nodes_cleared, 1)

            dve.wait_ge(consts, 2)
            step(v.tensor_copy(rk_ident[:, :], ident[:, :]))
            step(v.tensor_copy(rk_src[:, :], src_cols[:, :]))
            step(v.tensor_scalar(rk_tmp[:, :], src_cols[:, :], 6, None, ALU.logical_shift_right))
            step(v.tensor_copy(rk_hi[:, :], rk_tmp[:, :]))
            step(v.tensor_scalar(rk_tmp[:, :], src_cols[:, :], LO - 1, None, ALU.bitwise_and))
            step(v.tensor_copy(rk_lo[:, :], rk_tmp[:, :]))
            step(v.tensor_copy(rk_bases[:, 0, :], base_keep[0:HI, :]))
            v.memset(rk_zero[:, :], 0.0).then_inc(rk_zeroed, 1)
            def rank_edges(it):
                if some(it):
                    dve.wait_ge(rk_turned, it)
                one_hot(rk_hot_hi[:, :, :], rk_hi, it, rk_iota_hi[:, :], HI)
                one_hot(rk_hot_lo[:, :, :], rk_lo, it, rk_iota_lo[:, :], LO).then_inc(rk_hot, 1)
                dve.wait_ge(rk_rows, 16 * it + 16)
                for t in range(IT):
                    last = v.scalar_tensor_tensor(rk_row[:, t * P:(t + 1) * P], rk_row[:, t * P:(t + 1) * P],
                                                  rk_src[:, bass.ds(it * IT + t, 1)], after[:, :], ALU.is_equal, ALU.mult,
                                                  accum_out=rk_within[:, t:t + 1])
                last.then_inc(rk_used, 1)
                dve.wait_ge(rk_prefix, it + 1)
                v.tensor_tensor(rk_bases[:, 1:IT + 1, :], banks[0][0:HI, :].rearrange("h (t l) -> h t l", l=LO),
                                     rk_bases[:, 0:1, :].to_broadcast((HI, IT, LO)), ALU.add).then_inc(rk_base, 1)
                dve.wait_ge(rk_sel, it + 1)
                dve.wait_ge(rk_hot, it + 1)
                dve.wait_ge(rk_base, it + 1)
                dve.wait_ge(rk_used, it + 1)
                v.tensor_copy(rk_bases[:, 0, :], rk_bases[:, IT, :])
                v.tensor_tensor(rk_prod[:, :, :], banks[2][:, :].rearrange("p (t l) -> p t l", l=LO),
                                rk_hot_lo[:, :, :], ALU.mult).then_inc(rk_step, 1)
                dve.wait_ge(rk_step, 6 * it + 1)
                v.tensor_reduce(rk_prior[:, :], rk_prod[:, :, :], AX_X, ALU.add).then_inc(rk_step, 1)
                dve.wait_ge(rk_step, 6 * it + 2)
                v.tensor_tensor(rk_rank[:, :], rk_prior[:, :], rk_within[:, :], ALU.add).then_inc(rk_step, 1)
                dve.wait_ge(rk_step, 6 * it + 3)
                v.tensor_scalar(rk_p_i[:, :], rk_rank[:, :], P - 1, None, ALU.bitwise_and)
                v.tensor_scalar(rk_t_i[:, :], rk_rank[:, :], 7, None, ALU.logical_shift_right).then_inc(rk_step, 1)
                dve.wait_ge(rk_step, 6 * it + 4)
                v.tensor_copy(rk_p[:, :], rk_p_i[:, :]).then_inc(rk_step, 1)
                v.tensor_copy(rk_t[:, :], rk_t_i[:, :]).then_inc(rk_step, 1)
                dve.wait_ge(rk_step, 6 * it + 6)
                for t in range(IT):
                    if some(it * IT + max(t - 1, 0)):
                        dve.wait_ge(rk_placed, it * IT + max(t - 1, 0))
                    v.tensor_scalar(rk_l1[:, t, :], rk_iota_p[:, :], rk_p[:, t:t + 1], rk_pcol[:, :], ALU.is_equal, ALU.mult)
                    v.tensor_scalar(rk_l2[:, t, :], rk_iota_p[:, :], rk_p[:, t:t + 1], rk_tile[:, bass.ds(it * IT + t, 1)],
                                    ALU.is_equal, ALU.mult)
                    v.tensor_scalar(rk_r[:, t % 2, :], rk_iota_t[:, 0:TILES], rk_t[:, t:t + 1], None, ALU.is_equal).then_inc(rk_place, 1)

            rank_edges(0)
            with dve.Fori(1, ITER) as it:
                rank_edges(it)
            dve.wait_ge(rk_placed, TILES + 1)
            step(v.tensor_copy(rk_perm[:, :], banks[6][:, 0:TILES]))
            step(v.scalar_tensor_tensor(rk_perm[:, :], banks[7][:, 0:TILES], float(P), rk_perm[:, :], ALU.mult, ALU.add))
            v.tensor_scalar(perm_cols[:, :], rk_perm[:, :], float(E - 1), None, ALU.min).then_inc(perm_ready, 1)
            step(v.tensor_copy(keep_i[:, :], first_src[:, :]))
            step(v.tensor_scalar(keep_t_i[:, :], keep_i[:, :], 9, None, ALU.logical_shift_right))
            step(v.tensor_copy(keep_hi[:, :], keep_t_i[:, :]))
            step(v.tensor_scalar(keep_t_i[:, :], keep_i[:, :], GE - 1, None, ALU.bitwise_and))
            step(v.tensor_copy(keep_lo[:, :], keep_t_i[:, :]))
            for c in range(CH):
                if some(c - 1):
                    dve.wait_ge(keep_used, c - 1)
                v.tensor_scalar(keep_l[:, c % 2, :], rk_iota_t[:, 0:P], keep_hi[:, c:c + 1], None, ALU.is_equal)
                v.tensor_scalar(keep_r[:, c % 2, :], rk_iota_t[:, :], keep_lo[:, c:c + 1], None, ALU.is_equal).then_inc(keep_hot, 1)
            dve.wait_ge(keep_used, CH)
            v.tensor_scalar(keep_q[:, :], banks[3][0:GROUPS, :], -1.0, 1.0, ALU.mult, ALU.add).then_inc(keep_sb, 1)
            dve.wait_ge(keep_loaded, 8 * 16)
            edge_pass(LAYERS)

            dve.wait_ge(fin_w, 96)
            for k in range(7):
                w = min(4, CH - 4 * k)
                dve.wait_ge(fin_h2, k + 1)
                v.tensor_tensor(fin_y[:, 4 * k:4 * k + w, :],
                                     back[k % 2][:, :].rearrange("p (c d) -> p c d", d=D)[:, 0:w, :],
                                     fc2.unsqueeze(1).to_broadcast((P, w, D)), ALU.add).then_inc(fin_copied, 1)
            dve.wait_ge(fin_copied, 7)
            y = fin_y[:, :, :]
            normalise(3, y, y, fin_tmp[:, :, :])
            step(v.tensor_tensor(y, y, spread(stat[:, 2, :]), ALU.mult))
            step(v.tensor_tensor(y, y, fgamma.unsqueeze(1).to_broadcast((P, CH, D)), ALU.mult))
            step(v.tensor_tensor(y, y, fbeta.unsqueeze(1).to_broadcast((P, CH, D)), ALU.add))
            step(v.tensor_tensor(y, y, rows_a[:, :, :], ALU.add))
            v.tensor_tensor(rows_a[:, :, :], y, xres[:, :, :], ALU.add).then_inc(fin_rows, 1)


_INS = ["x", "src", "dst", "edge_attr_128"] + [
    f"L0_gnn_{w}_{l}" for l in ("in", "hid", "out") for w in ("W1", "b1", "W2", "b2")] + [
    f"L1_gnn_{w}" for w in ("W1", "b1", "W2", "b2", "ln_gamma", "ln_beta")]


def kernel(**inputs):
    import concourse.bacc as _bacc
    from concourse.bass_utils import run_bass_kernel_spmd as _run

    nc = _bacc.Bacc("TRN2", target_bir_lowering=False, num_devices=1)
    arrays, aps = {}, {}
    for name in _INS:
        a = np.ascontiguousarray(inputs[name])
        arrays[f"in_{name}"] = a
        aps[name] = nc.dram_tensor(f"in_{name}", a.shape, mybir.dt.from_np(a.dtype), kind="ExternalInput").ap()
    out = nc.dram_tensor("out_0", (N, D), F32, kind="ExternalOutput").ap()
    layers = [[aps[f"L0_gnn_{w}_{l}"] for l in ("in", "hid", "out")] for w in ("W1", "b1", "W2", "b2")]
    build(nc, aps["x"], aps["src"], aps["dst"], aps["edge_attr_128"], *layers,
          *(aps[f"L1_gnn_{w}"] for w in ("W1", "b1", "W2", "b2", "ln_gamma", "ln_beta")), out)
    r = _run(nc, [arrays], core_ids=[0])
    return r.results[0]["out_0"]
```

```python
from contextlib import ExitStack

import numpy as np
import concourse.bass as bass
from concourse import mybir

F32 = mybir.dt.float32
BF16 = mybir.dt.bfloat16
FP16 = mybir.dt.float16
I32 = mybir.dt.int32
I16 = mybir.dt.int16
ALU = mybir.AluOpType
ACT = mybir.ActivationFunctionType
AX_X = mybir.AxisListType.X

P = 128
N, D, E = 3125, 128, 53125
LAYERS = 3
EPS = 1e-5
CH = -(-N // P)
NP = CH * P
NLAST = N - (CH - 1) * P
TILES = -(-E // P)
EP = TILES * P
GROUP = 4
GE = GROUP * P
GROUPS = TILES // GROUP
UNROLL = 4
ITER = GROUPS // UNROLL
IT = 8
ROUNDS = TILES // IT
FULLROWS = E // GE
TAIL = E - FULLROWS * GE
BLOCKS = -(-CH // 4)
PAIRS = -(-CH // 2)
LO = 64
HI = NP // LO
HUGE = 3.0e38
SKIP = 1 << 17
assert GROUPS % UNROLL == 0 and ITER % 2 == 0 and FULLROWS == GROUPS - 1 and TAIL < GE
assert ROUNDS * 2 == GROUPS and NP == HI * LO


def some(n):
    return not (isinstance(n, int) and n <= 0)


def block_chunks(k):
    return 4 * k, min(4, CH - 4 * k)


def pairs_of(k):
    return range(2 * k, min(2 * k + 2, PAIRS))


def build(nc, x, src, dst, attr, w1, b1, w2, b2, v1, c1, v2, c2, gamma, beta, out):
    with ExitStack() as ctx:
        def sb(name, shape, dt=F32):
            return ctx.enter_context(nc.sbuf_tensor(name, shape, dt))

        def sem(name):
            return ctx.enter_context(nc.semaphore(name))

        def dram(name, shape, dt=F32):
            return nc.dram_tensor(name, shape, dt).ap()

        def view(region, at, shape, dt=F32):
            n = int(np.prod(shape)) * (2 if dt in (BF16, FP16) else 4) // 4
            ap = region[:, at:at + n]
            if dt != F32:
                ap = ap.bitcast(dt)
            if len(shape) == 2:
                ap = ap.rearrange("p (a b) -> p a b", a=shape[0])
            if len(shape) == 3:
                ap = ap.rearrange("p (a b c) -> p a b c", a=shape[0], b=shape[1])
            return ap

        b_rows = dram("b_rows", (NP, D))
        a_rows = dram("a_rows", (NP, D))
        max_rows = dram("max_rows", (EP, D))
        sum_rows = dram("sum_rows", (EP, D))
        code_row = dram("code_row", (EP,), FP16)
        base_row = dram("base_row", (TILES,), I16)
        count_row = dram("count_row", (GROUPS * 2,), I32)
        srcf_row = dram("srcf_row", (EP,))
        seg_node = dram("seg_node", (NP, 1), I32)
        node_cols = dram("node_cols", (4, NP))
        keep_row = dram("keep_row", (EP,), BF16)

        xres = sb("xres", [P, CH, D])
        nodes = sb("nodes", [P, CH, D])
        rows_a = sb("rows_a", [P, CH, D])
        big = sb("big", [P, EP // 2])
        work = sb("work", [P, 2 * CH * D])
        a_parts = sb("a_parts", [P, CH + 1, 3, D], BF16)
        ring_lo = sb("ring_lo", [P, 2, GROUP, D])
        src_cols = sb("src_cols", [P, TILES], I32)
        perm_cols = sb("perm_cols", [P, TILES], I32)
        base_sb = sb("base_sb", [1, TILES], I16)
        idx = sb("idx", [P, UNROLL, GROUP], I32)
        w_ab = sb("w_ab", [P, LAYERS, 2 * D])
        w2_sb = sb("w2_sb", [P, LAYERS, D])
        b1_sb = sb("b1_sb", [P, LAYERS, D])
        b2_sb = sb("b2_sb", [P, LAYERS, D])
        ident = sb("ident", [P, P])
        before = sb("before", [P, P])
        after = sb("after", [P, P])
        place = sb("place", [P, 2])
        part16 = sb("part16", [P, 2], FP16)
        iota = sb("iota", [P, GE], FP16)
        src_hi = sb("src_hi", [P, TILES], BF16)
        src_lo = sb("src_lo", [P, TILES], BF16)
        first_state = sb("first_state", [P, 1])
        present = sb("present", [P, CH])
        end_dst = sb("end_dst", [P, CH], I32)
        end_src = sb("end_src", [P, CH], I32)
        first_src = sb("first_src", [P, CH])
        stat = sb("stat", [P, 4, CH])
        counter = sb("counter", [1, 4], I32)
        base_keep = sb("base_keep", [P, LO])
        list_idx = sb("list_idx", [P, CH], I32)
        list_at = sb("list_at", [P, 1], I32)
        list_val = sb("list_val", [P, 1], I32)

        rows_b = view(work, 0, (CH, D))
        xt = view(work, CH * D, (CH * D,))
        rest = view(work, CH * D, (CH, D))
        hin = view(work, 0, (2, GE))
        run = view(work, 2 * GE, (2, GE))
        outb = view(work, 4 * GE, (2, GROUP, D))
        onehot = [view(work, 6 * GE + a * GE, (2, GE), BF16) for a in range(2)]
        mask = view(work, 8 * GE, (2, GE), BF16)
        spots = view(work, 9 * GE, (2, GE), FP16)
        ring_hi = view(work, 10 * GE, (2, GROUP, D))
        ring = [ring_lo[:, 0], ring_lo[:, 1], ring_hi[:, 0], ring_hi[:, 1]]
        codes = big[:, :].bitcast(FP16)
        dst_cols = perm_cols
        rank_pt = perm_cols[:, :].bitcast(FP16)

        banks = [ctx.enter_context(nc.psum_tensor(f"bank{i}", [P, 512], F32)) for i in range(8)]
        mixed, hidden, back, sort_a, sort_b = banks[0:2], banks[2:4], banks[4:6], banks[6], banks[7]

        ids_cleared = sem("ids_cleared")
        ids_loaded = sem("ids_loaded")
        src_loaded = sem("src_loaded")
        x_cleared = sem("x_cleared")
        x_loaded = sem("x_loaded")
        weights_loaded = sem("weights_loaded")
        w_ready = sem("w_ready")
        consts = sem("consts")
        clears = sem("clears")
        seg_totals = sem("seg_totals")
        seg_before = sem("seg_before")
        wide_groups = sem("wide_groups")
        wide_sum = sem("wide_sum")
        codes_ready = sem("codes_ready")
        codes_saved = sem("codes_saved")
        codes_loaded = sem("codes_loaded")
        srcf_ready = sem("srcf_ready")
        cols_turned = sem("cols_turned")
        edge_cols_done = sem("edge_cols_done")
        node_list = sem("node_list")
        node_list_ready = sem("node_list_ready")
        list_copied = sem("list_copied")
        may_gather = sem("may_gather")
        a_gather = sem("a_gather")
        a_saved = sem("a_saved")
        compact = sem("compact")
        a_resplit = sem("a_resplit")
        ln_var = sem("ln_var")
        ln_std = sem("ln_std")
        ln_done = sem("ln_done")
        rows_ready = sem("rows_ready")
        rows_turned = sem("rows_turned")
        xt_ready = sem("xt_ready")
        ab_ready = sem("ab_ready")
        a_ready = sem("a_ready")
        b_ready = sem("b_ready")
        b_saved = sem("b_saved")
        a_split = sem("a_split")
        split_done = sem("split_done")
        idx_ready = sem("idx_ready")
        mixed_done = sem("mixed_done")
        spots_ready = sem("spots_ready")
        hot_done = sem("hot_done")
        mask_ready = sem("mask_ready")
        relu_done = sem("relu_done")
        hidden_done = sem("hidden_done")
        scanned = sem("scanned")
        backed = sem("backed")
        out_copied = sem("out_copied")
        hist_zero = sem("hist_zero")
        hist_src = sem("hist_src")
        hist_dst = sem("hist_dst")
        hist_src_used = sem("hist_src_used")
        hist_dst_used = sem("hist_dst_used")
        hist_done = sem("hist_done")
        hist_rows = sem("hist_rows")
        hist_base = sem("hist_base")
        tables_ready = sem("tables_ready")
        tables_saved = sem("tables_saved")
        tables_loaded = sem("tables_loaded")
        cols_ready = sem("cols_ready")
        keep_hot = sem("keep_hot")
        keep_used = sem("keep_used")
        keep_ready = sem("keep_ready")
        keep_saved = sem("keep_saved")
        rk_rows = sem("rk_rows")
        rk_hot = sem("rk_hot")
        rk_prefix = sem("rk_prefix")
        rk_turned = sem("rk_turned")
        rk_turned_sb = sem("rk_turned_sb")
        rk_base = sem("rk_base")
        rk_sel = sem("rk_sel")
        rk_read = sem("rk_read")
        rk_used = sem("rk_used")
        rk_step = sem("rk_step")
        pl_zeroed = sem("pl_zeroed")
        pl_ready = sem("pl_ready")
        pl_used = sem("pl_used")
        perm_ready = sem("perm_ready")
        nodes_cleared = sem("nodes_cleared")
        agg_cleared = sem("agg_cleared")
        fin_w = sem("fin_w")
        fin_turned = sem("fin_turned")
        fin_t = sem("fin_t")
        fin_h1 = sem("fin_h1")
        fin_act = sem("fin_act")
        fin_h2 = sem("fin_h2")
        fin_copied = sem("fin_copied")
        fin_rows = sem("fin_rows")
        fin_saved = sem("fin_saved")
        pool_steps = sem("pool_steps")
        dve_steps = sem("dve_steps")
        keep_loaded = [sem(f"keep_loaded{i}") for i in range(2)]
        gathered = [sem(f"gathered{i}") for i in range(UNROLL * GROUP)]
        stored = [sem(f"stored{i}") for i in range(2)]
        ends = [sem(f"ends{k}") for k in range(BLOCKS)]

        def chunks(ap):
            return ap.rearrange("(c p) f -> p c f", p=P)

        def row(ap):
            return ap.rearrange("(a n) -> a n", a=1)

        def edges_2d(ap, lo, hi):
            return ap[lo * GE:hi * GE].rearrange("(q r) -> q r", r=GE)

        dst_i, prev_i, src_i = (view(big, i * GE, (GE,), I32)[0:GROUPS] for i in range(3))
        dst_f, src_f, head, cum, ones_e, seg = (view(big, (3 + i) * GE, (GE,))[0:GROUPS] for i in range(6))
        sign = view(big, 9 * GE, (GE,))[0:GROUPS]
        code_b = view(big, 10 * GE, (GE,), FP16)[0:GROUPS]
        rel = view(big, 11 * GE, (GE,))[0:GROUPS]
        head_seg = view(big, 12 * GE, (GE,))[0:GROUPS]
        seg_i = view(big, 13 * GE, (GE,), I32)[0:GROUPS]
        sm = 14 * GE
        base_i = view(big, sm, (GROUP,), I32)[0:GROUPS]
        base_h = view(big, sm + 8, (GROUP,), BF16)[0:GROUPS].bitcast(I16)
        base_f = view(big, sm + 16, (GROUP,))[0:GROUPS]
        seg_last = view(big, sm + 24, (2,), I32)[0:GROUPS]
        base_u = view(big, sm + 40, (GROUP,))[0:GROUPS]
        last_i = view(big, sm + 48, (1,), I32)[0:GROUPS]
        last_f, wide_q, wide_f = (view(big, sm + 56 + 8 * i, (1,))[0:GROUPS] for i in range(3))
        head_cols = view(big, sm + 80, (TILES,), I32)
        part_i = view(big, sm + 80 + TILES, (TILES,), I32)

        sort = rows_a[:, :, :].rearrange("p c d -> p (c d)")
        hot_hi = [view(sort, i * 512, (IT, HI), BF16) for i in range(2)]
        hot_lo = [view(sort, i * 512 + 256, (IT, LO), BF16) for i in range(2)]
        dst_hi = view(sort, 1024, (TILES,), BF16)
        dst_lo = view(sort, 1024 + TILES // 2, (TILES,), BF16)
        c_sb, c_cum, c_end, c_none, ones_h = (view(sort, 1440 + i * 2 * LO, (2 * LO,))[0:HI] for i in range(5))
        c_out = view(sort, 2080, (4, LO))[0:HI]
        cols_f = view(sort, 2336, (4, CH))
        zeros_b = view(sort, 2440, (2 * LO,), BF16)
        keep_q = view(sort, 1440, (GE,), BF16)[0:GROUPS]
        keep_l = view(sort, 1700, (2, P), FP16)
        keep_r = view(sort, 2600, (2, GE), FP16)
        keep_i, keep_t = (view(sort, 2504 + i * 32, (CH,), I32) for i in range(2))
        keep_hi, keep_lo = (view(sort, 1840 + i * 32, (CH,)) for i in range(2))
        dst_part = view(sort, 2600, (TILES,), I32)
        rk_row = view(sort, 0, (IT * P,))
        rk_prod = view(sort, 0, (IT, LO))
        rk_hot_hi = view(sort, 1024, (IT, HI), BF16)
        rk_hot_lo = view(sort, 1224, (IT, LO), BF16)
        rk_hi_t = view(sort, 1480, (IT, P))[0:HI]
        rk_bases = view(sort, 2504, (IT + 1, LO))[0:HI]
        rk_prior, rk_within = (view(sort, 3080 + 8 * i, (IT,)) for i in range(2))
        rk_rank, rk_p_i, rk_t_i = (view(sort, 3096 + 8 * i, (IT,), I32) for i in range(3))
        rk_ident = view(sort, 3120, (P,), BF16)
        pl_tile = view(sort, 0, (2, GROUP, TILES), FP16)
        pl_p = view(sort, 1664, (2, GROUP, P), FP16)
        pl_t = view(sort, 2176, (2, GROUP, P), FP16)
        pl_zero = view(sort, 2688, (TILES,), FP16)
        pl_perm = view(sort, 0, (TILES,))

        fv1 = view(big, 0, (2, 2 * D))
        fv2 = view(big, 512, (2, D))
        fc1 = view(big, 768, (2,))
        fc2, fgamma, fbeta = (view(big, 776 + i * D, (D,)) for i in range(3))
        fin_xt = view(big, 1280, (2, NP))
        fin_g = view(big, 1280 + 2 * NP, (2, NP))
        fin_y = view(big, 1280 + 4 * NP, (CH, D))
        fin_tmp = view(big, 1280 + 5 * NP, (CH, D))

        block = ctx.enter_context(nc.Block())

        @block.sync
        def _(sp):
            sp.wait_ge(ids_cleared, 1)
            sp.dma_start(dst_i[0:FULLROWS, :], edges_2d(dst, 0, FULLROWS)).then_inc(ids_loaded, 16)
            sp.dma_start(dst_i[FULLROWS:GROUPS, 0:TAIL], row(dst[FULLROWS * GE:E])).then_inc(ids_loaded, 16)
            sp.dma_start(prev_i[0:1, 1:GE], row(dst[0:GE - 1])).then_inc(ids_loaded, 16)
            sp.dma_start(prev_i[1:FULLROWS, :],
                         dst[GE - 1:FULLROWS * GE - 1].rearrange("(q r) -> q r", r=GE)).then_inc(ids_loaded, 16)
            sp.dma_start(prev_i[FULLROWS:GROUPS, 0:TAIL + 1],
                         row(dst[FULLROWS * GE - 1:E])).then_inc(ids_loaded, 16)
            sp.dma_start(src_i[0:FULLROWS, :], edges_2d(src, 0, FULLROWS)).then_inc(src_loaded, 16)
            sp.dma_start(src_i[FULLROWS:GROUPS, 0:TAIL], row(src[FULLROWS * GE:E])).then_inc(src_loaded, 16)
            sp.wait_ge(x_cleared, 1)
            sp.dma_start(xres[:, 0:CH - 1, :], chunks(x[0:(CH - 1) * P, :])).then_inc(x_loaded, 16)
            sp.dma_start(xres[0:NLAST, CH - 1, :], x[(CH - 1) * P:N, :]).then_inc(x_loaded, 16)
            for l in range(LAYERS):
                for ap, w in ((w_ab[:, l, 0:D], w1[l][0:D, :]), (w_ab[:, l, D:2 * D], w1[l][D:2 * D, :]),
                              (w2_sb[:, l, :], w2[l][:, :]), (b1_sb[:, l, :], b1[l].partition_broadcast(P)),
                              (b2_sb[:, l, :], b2[l].partition_broadcast(P))):
                    sp.dma_start(ap, w).then_inc(weights_loaded, 16)
            sp.wait_ge(codes_ready, 1)
            sp.dma_start(code_row.rearrange("(q r) -> q r", r=GE), code_b[:, :]).then_inc(codes_saved, 16)
            sp.dma_start(base_row.rearrange("(q r) -> q r", r=GROUP), base_h[:, :]).then_inc(codes_saved, 16)
            sp.dma_start(count_row.rearrange("(q r) -> q r", r=2), seg_last[:, :]).then_inc(codes_saved, 16)
            sp.wait_ge(srcf_ready, 1)
            sp.dma_start(srcf_row.rearrange("(q r) -> q r", r=GE), src_f[:, :]).then_inc(codes_saved, 16)
            sp.wait_ge(codes_saved, 64)
            sp.dma_start(base_sb[:, :], row(base_row)).then_inc(codes_loaded, 16)
            sp.dma_start(counter[0:1, 0:2], row(count_row[2 * GROUPS - 2:2 * GROUPS])).then_inc(codes_loaded, 16)
            sp.wait_ge(edge_cols_done, 1)
            sp.wait_ge(node_list_ready, 1)
            piece = EP // 8
            for i in range(8):
                sp.dma_start(codes[:, i * piece:(i + 1) * piece],
                             code_row[i * piece:(i + 1) * piece].partition_broadcast(P)).then_inc(codes_loaded, 16)

            def save_b(l):
                for k in range(BLOCKS):
                    c, n = block_chunks(k)
                    sp.wait_ge(b_ready, PAIRS * l + pairs_of(k)[-1] + 1)
                    sp.dma_start(chunks(b_rows)[:, c:c + n, :], rows_b[:, c:c + n, :]).then_inc(b_saved, 16)

            def store(g, a, base, rows):
                sp.wait_ge(out_copied, base + g + 1)
                sp.dma_start(rows[bass.ds(g * GE, GE), :].rearrange("(j p) f -> p j f", p=P),
                             outb[:, a, :, :]).then_inc(stored[a], 16)

            def load_sources(r):
                if some(r):
                    sp.wait_ge(rk_used, r)
                sp.dma_start(rk_row[:, :], srcf_row[bass.ds(r * IT * P, IT * P)].partition_broadcast(P)).then_inc(rk_rows, 16)

            def load_keep(g, a, base):
                sp.wait_ge(scanned, base + g - 1)
                sp.dma_start(mask[:, a, :], keep_row[bass.ds(g * GE, GE)].partition_broadcast(P)).then_inc(keep_loaded[a], 16)

            def save_pass(l):
                base = l * GROUPS

                def iteration(it):
                    for u in range(UNROLL):
                        g = it * UNROLL + u
                        if l == 1 and u % 2 == 0:
                            load_sources(it * 2 + u // 2)
                        if l == LAYERS:
                            load_keep(g, u % 2, base)
                        if not (isinstance(g, int) and g < 2):
                            store(g - 2, u % 2, base, max_rows if l < LAYERS else sum_rows)

                def node_tables_out():
                    sp.wait_ge(tables_ready, 1)
                    sp.dma_start(node_cols.rearrange("k (h l) -> h k l", l=LO), c_out[:, :, :]).then_inc(tables_saved, 16)
                    sp.wait_ge(tables_saved, 16)
                    with nc.allow_non_contiguous_dma(reason="3200 node words, once"):
                        for k in range(4):
                            sp.dma_start(cols_f[:, k, :], node_cols[k].rearrange("(c p) -> p c", p=P)).then_inc(tables_loaded, 16)

                iteration(0)
                if l == 0:
                    with sp.Fori(1, ITER // 2) as it:
                        iteration(it)
                    node_tables_out()
                    with sp.Fori(ITER // 2, ITER - 1) as it:
                        iteration(it)
                    sp.wait_ge(keep_ready, 1)
                    sp.dma_start(keep_row.rearrange("(q r) -> q r", r=GE), keep_q[:, :]).then_inc(keep_saved, 16)
                else:
                    with sp.Fori(1, ITER - 1) as it:
                        iteration(it)
                iteration(ITER - 1)
                store(GROUPS - 2, 0, base, max_rows if l < LAYERS else sum_rows)
                store(GROUPS - 1, 1, base, max_rows if l < LAYERS else sum_rows)

            for l in range(LAYERS):
                save_b(l)
                if l == 1:
                    sp.wait_ge(split_done, l + 1)
                save_pass(l)
            sp.wait_ge(keep_saved, 16)
            sp.wait_ge(scanned, LAYERS * GROUPS)
            sp.dma_start(fv1[:, :, :], v1.rearrange("(s p) n -> p s n", p=P)).then_inc(fin_w, 16)
            sp.dma_start(fv2[:, :, :], v2.rearrange("(s p) n -> p s n", p=P)).then_inc(fin_w, 16)
            with nc.allow_non_contiguous_dma(reason="256 words, once"):
                sp.dma_start(fc1[:, :], c1.rearrange("(m p) -> p m", p=P)).then_inc(fin_w, 16)
            for ap, v in ((fc2, c2), (fgamma, gamma), (fbeta, beta)):
                sp.dma_start(ap, v.partition_broadcast(P)).then_inc(fin_w, 16)
            save_pass(LAYERS)
            for k in range(BLOCKS):
                c, n = block_chunks(k)
                sp.wait_ge(fin_rows, k + 1)
                if k < BLOCKS - 1:
                    sp.dma_start(chunks(out[c * P:(c + n) * P, :]), fin_y[:, c:c + n, :]).then_inc(fin_saved, 16)
                else:
                    sp.dma_start(out[c * P:N, :], fin_y[0:NLAST, c, :]).then_inc(fin_saved, 16)
            sp.wait_ge(fin_saved, 16 * BLOCKS)

        @block.gpsimd
        def _(pool):
            taken = [0]

            def step(ins):
                taken[0] += 1
                ins.then_inc(pool_steps, 1)
                pool.wait_ge(pool_steps, taken[0])

            step(nc.gpsimd.memset(ident[:, :], 0.0))
            step(nc.gpsimd.affine_select(out=ident[:, :], in_=ident[:, :], compare_op=ALU.not_equal, fill=1.0,
                                         base=0, pattern=[[-1, P]], channel_multiplier=1))
            step(nc.gpsimd.memset(before[:, :], 0.0))
            nc.gpsimd.affine_select(out=before[:, :], in_=before[:, :], compare_op=ALU.is_ge, fill=1.0,
                                    base=0, pattern=[[-1, P]], channel_multiplier=1).then_inc(consts, 1)
            step(nc.gpsimd.memset(after[:, :], 0.0))
            nc.gpsimd.affine_select(out=after[:, :], in_=after[:, :], compare_op=ALU.is_ge, fill=1.0,
                                    base=0, pattern=[[1, P]], channel_multiplier=-1)
            nc.gpsimd.iota(place[:, :], pattern=[[P, 2]], base=1, channel_multiplier=1,
                           allow_small_or_imprecise_dtypes=True)
            nc.gpsimd.iota(part16[:, :], pattern=[[0, 2]], base=0, channel_multiplier=1,
                           allow_small_or_imprecise_dtypes=True)
            nc.gpsimd.iota(iota[:, :], pattern=[[1, GE]], base=0, channel_multiplier=0,
                           allow_small_or_imprecise_dtypes=True).then_inc(consts, 1)

            pool.wait_ge(codes_loaded, 32)
            pool.wait_ge(edge_cols_done, 1)
            occurring = pool.value_load(counter[0:1, 0:1], min_val=0, max_val=NP)
            with pool.If(occurring != N):
                with nc.allow_non_contiguous_dma(reason="3200 words, only where nodes lack edges"):
                    pool.dma_start(chunks(seg_node), list_idx[:, :].unsqueeze(2)).then_inc(node_list, 16)
                pool.wait_ge(node_list, 16)
                with pool.Fori(0, TILES) as t:
                    nc.gpsimd.tensor_copy(list_at[:, 0:1], head_cols[:, bass.ds(t, 1)]).then_inc(list_copied, 1)
                    nc.gpsimd.tensor_copy(list_val[:, 0:1], dst_cols[:, bass.ds(t, 1)]).then_inc(list_copied, 1)
                    pool.wait_ge(list_copied, 2 * t + 2)
                    nc.gpsimd.sem_inc(may_gather, 1)
                    nc.gpsimd.indirect_dma_start(seg_node, bass.IndirectOffsetOnAxis(ap=list_at[:, 0:1], axis=0),
                                                 list_val[:, 0:1], None, bounds_check=NP - 1,
                                                 oob_is_err=False).then_inc(node_list, 16)
                    pool.wait_ge(node_list, 16 * t + 32)
                with nc.allow_non_contiguous_dma(reason="3200 words, only where nodes lack edges"):
                    pool.dma_start(list_idx[:, :].unsqueeze(2), chunks(seg_node)).then_inc(node_list, 16)
                pool.wait_ge(node_list, 16 * TILES + 32)
                nc.gpsimd.sem_inc(node_list_ready, 1)
            with pool.Else():
                nc.gpsimd.sem_inc(node_list_ready, 1)

            def compact_a(l):
                with pool.If(occurring != N):
                    pool.wait_ge(a_split, BLOCKS * (l + 1))
                    pool.dma_start(chunks(a_rows), rows_a[:, :, :]).then_inc(a_saved, 16)
                    pool.wait_ge(a_saved, 16 * (l + 1))
                    for c in range(CH):
                        nc.gpsimd.indirect_dma_start(rows_a[:, c, :], None, a_rows,
                                                     bass.IndirectOffsetOnAxis(ap=list_idx[:, c:c + 1], axis=0),
                                                     bounds_check=NP - 1, oob_is_err=False).then_inc(a_gather, 16)
                    pool.wait_ge(a_gather, 16 * CH * (l + 1))
                    nc.gpsimd.sem_inc(compact, 1)
                with pool.Else():
                    nc.gpsimd.sem_inc(may_gather, 1)

            def gather_group(g, u, base, table):
                pool.wait_ge(idx_ready, base + g + 1)
                if some(base + g - UNROLL + 1):
                    pool.wait_ge(mixed_done, base + g - UNROLL + 1)
                nc.gpsimd.sem_inc(may_gather, 1)
                for j in range(GROUP):
                    nc.gpsimd.indirect_dma_start(
                        ring[u][:, j, :], None, table,
                        bass.IndirectOffsetOnAxis(ap=idx[:, u, j:j + 1], axis=0)).then_inc(gathered[u * GROUP + j], 16)

            for l in range(LAYERS + 1):
                base = l * GROUPS
                if l < LAYERS:
                    compact_a(l)
                    pool.wait_ge(b_saved, 16 * BLOCKS * (l + 1))
                table = b_rows if l < LAYERS else attr
                for u in range(UNROLL):
                    if u == 2 and l < LAYERS:
                        pool.wait_ge(split_done, l + 1)
                    gather_group(u, u, base, table)
                with pool.Fori(1, ITER) as it:
                    for u in range(UNROLL):
                        gather_group(it * UNROLL + u, u, base, table)
                if l == LAYERS:
                    pool.wait_ge(agg_cleared, 1)
                elif l == 0:
                    pool.wait_ge(nodes_cleared, 1)
                    pool.wait_ge(cols_ready, 1)
                for a in range(2):
                    pool.wait_ge(stored[a], 16 * (GROUPS // 2) * (l + 1))
                for k in range(BLOCKS):
                    c0, n = block_chunks(k)
                    for c in range(c0, c0 + n):
                        nc.gpsimd.indirect_dma_start(
                            (nodes if l < LAYERS else rows_a)[:, c, :], None, max_rows if l < LAYERS else sum_rows,
                            bass.IndirectOffsetOnAxis(ap=(end_dst if l < LAYERS else end_src)[:, c:c + 1], axis=0),
                            bounds_check=EP - 1, oob_is_err=False).then_inc(ends[k], 16)

        @block.tensor
        def _(pe):
            pe.wait_ge(seg_totals, 1)
            pe.wait_ge(consts, 1)
            nc.tensor.matmul(banks[7][0:GROUPS, 0:1], before[0:GROUPS, 0:GROUPS], cum[:, GE - 1:GE],
                             start=True, stop=True).then_inc(seg_before, 1)
            pe.wait_ge(wide_groups, 1)
            nc.tensor.matmul(banks[7][0:GROUPS, 8:9], ones_e[:, 0:GROUPS], wide_q[:, :],
                             start=True, stop=True).then_inc(wide_sum, 1)
            for k, (rows, ready, count) in enumerate(((dst_f, seg_totals, 1), (head_seg, codes_ready, 1), (src_f, srcf_ready, 1))):
                pe.wait_ge(ready, count)
                for j in range(GROUP):
                    last = nc.tensor.transpose(banks[4 + k][:, j * P:j * P + GROUPS], rows[:, j * P:(j + 1) * P],
                                               ident[0:GROUPS, 0:GROUPS])
                last.then_inc(cols_turned, 1)

            flat_parts = a_parts[:, :, :, :].rearrange("p c k d -> p (c k d)")

            def node_tables(l):
                for k in range(BLOCKS + 1):
                    if k < BLOCKS:
                        pe.wait_ge(rows_ready, BLOCKS * l + k + 1)
                        if some(BLOCKS * l + k - 1):
                            pe.wait_ge(xt_ready, BLOCKS * l + k - 1)
                        c0, n = block_chunks(k)
                        for c in range(n):
                            last = nc.tensor.transpose(mixed[k % 2][:, c * P:(c + 1) * P], nodes[:, c0 + c, :], ident[:, :])
                        last.then_inc(rows_turned, 1)
                    if k == 0:
                        if l == 0:
                            pe.wait_ge(w_ready, 1)
                        continue
                    pe.wait_ge(xt_ready, BLOCKS * l + k)
                    for q in pairs_of(k - 1):
                        if some(PAIRS * l + q - 1):
                            pe.wait_ge(b_ready, PAIRS * l + q - 1)
                        for c in range(2 * q, min(2 * q + 2, CH)):
                            last = nc.tensor.matmul(hidden[q % 2][:, (c % 2) * 2 * D:(c % 2 + 1) * 2 * D],
                                                    xt[:, c * P:(c + 1) * P], w_ab[:, l, :], start=True, stop=True)
                        last.then_inc(ab_ready, 1)

            def mix(g, u, base, landed, bases):
                if some(base + g - 1):
                    pe.wait_ge(relu_done if bases else scanned, base + g - 1)
                if bases:
                    pe.wait_ge(hot_done, base + g + 1)
                for j in range(GROUP):
                    pe.wait_ge(gathered[u * GROUP + j], landed)
                    to = mixed[u % 2][:, j * P:(j + 1) * P]
                    if not bases:
                        last = nc.tensor.transpose(to, ring[u][:, j, :], ident[:, :])
                        continue
                    nc.tensor.matmul(to, ring[u][:, j, :], ident[:, :], is_transpose=True,
                                     start=(len(bases) > 1 or j == 0), stop=False)
                    if j >= GROUP - len(bases):
                        edges = slice(j * P, (j + 1) * P) if len(bases) > 1 else slice(0, GE)
                        first = bases[j if len(bases) > 1 else 0]
                        for k in range(2):
                            for part in range(3):
                                at = (first + k) * (3 * D) + part * D
                                last = nc.tensor.matmul(mixed[u % 2][:, edges], flat_parts[:, bass.ds(at, D)],
                                                        onehot[u % 2][:, k, edges], start=False,
                                                        stop=(k == 1 and part == 2))
                last.then_inc(mixed_done, 1)

            def second(g, a, base, l):
                pe.wait_ge(relu_done, base + g + 1)
                if some(base + g - 1):
                    pe.wait_ge(scanned, base + g - 1)
                nc.tensor.matmul(hidden[a][:, :], w2_sb[:, l, :], hin[:, a, :], start=True, stop=True).then_inc(hidden_done, 1)

            def turn_back(g, a, base):
                pe.wait_ge(scanned, base + g + 1)
                if some(base + g - 1):
                    pe.wait_ge(out_copied, base + g - 1)
                for j in range(GROUP):
                    last = nc.tensor.transpose(back[a][:, j * P:(j + 1) * P], run[:, a, j * P:(j + 1) * P], ident[:, :])
                last.then_inc(backed, 1)

            def count_edges(r):
                pe.wait_ge(hist_src, r + 1)
                for j in range(IT):
                    last = nc.tensor.matmul(sort_a[0:HI, 0:LO], hot_hi[0][:, j, :], hot_lo[0][:, j, :],
                                            start=False, stop=False, skip_group_check=True)
                last.then_inc(hist_src_used, 1)
                pe.wait_ge(hist_dst, r + 1)
                for j in range(IT):
                    last = nc.tensor.matmul(sort_a[0:HI, LO:2 * LO], hot_hi[1][:, j, :], hot_lo[1][:, j, :],
                                            start=False, stop=False, skip_group_check=True)
                last.then_inc(hist_dst_used, 1)

            def tables():
                nc.tensor.matmul(sort_a[0:HI, 0:2 * LO], zeros_b[:, 0:HI], zeros_b[:, :], start=False,
                                 stop=True).then_inc(hist_done, 1)
                pe.wait_ge(hist_rows, 1)
                for k in range(2):
                    last = nc.tensor.matmul(sort_b[0:HI, 8 * k:8 * k + 1], before[0:HI, 0:HI],
                                            c_cum[:, (k + 1) * LO - 1:(k + 1) * LO], start=True, stop=True)
                last.then_inc(hist_base, 1)

            def keep_flags():
                for c in range(CH):
                    pe.wait_ge(keep_hot, c + 1)
                    nc.tensor.matmul(sort_b[0:GROUPS, :], keep_l[:, c % 2, 0:GROUPS], keep_r[:, c % 2, :],
                                     start=(c == 0), stop=(c == CH - 1)).then_inc(keep_used, 1)

            def rank_counts(r):
                pe.wait_ge(rk_hot, r + 1)
                if some(r):
                    pe.wait_ge(rk_base, r)
                    pe.wait_ge(rk_read, r)
                for t in range(IT):
                    last = nc.tensor.matmul(sort_a[0:HI, t * LO:IT * LO].rearrange("h (t l) -> h t l", l=LO),
                                            rk_hot_hi[:, t, :],
                                            rk_hot_lo[:, t:t + 1, :].to_broadcast((P, IT - t, LO)),
                                            start=(t == 0), stop=(t == IT - 1))
                last.then_inc(rk_prefix, 1)
                for t in range(IT):
                    last = nc.tensor.transpose(sort_b[:, :].bitcast(BF16)[0:HI, t * P:(t + 1) * P],
                                               rk_hot_hi[:, t, :], rk_ident[:, :])
                last.then_inc(rk_turned, 1)

            def rank_select(r):
                pe.wait_ge(rk_turned_sb, r + 1)
                pe.wait_ge(rk_base, r + 1)
                for t in range(IT):
                    last = nc.tensor.matmul(sort_b[:, t * LO:(t + 1) * LO], rk_hi_t[:, t, :], rk_bases[:, t, :],
                                            start=True, stop=True)
                last.then_inc(rk_sel, 1)

            def put(g, a):
                pe.wait_ge(pl_ready, g + 1)
                for j in range(GROUP):
                    nc.tensor.matmul(sort_a[:, 0:TILES], pl_p[:, a, j, :], pl_tile[:, a, j, :], start=False, stop=False,
                                     skip_group_check=True)
                    last = nc.tensor.matmul(sort_b[:, 0:TILES], pl_t[:, a, j, :], pl_tile[:, a, j, :], start=False, stop=False,
                                            skip_group_check=True)
                last.then_inc(pl_used, 1)

            def edge_pass(l, wide=False):
                base, conv = l * GROUPS, l < LAYERS

                def iteration(it, counting=False):
                    firsts = None
                    for u in range(UNROLL):
                        g = it * UNROLL + u
                        if conv and u % 2 == 0 and wide:
                            _, firsts = nc.values_load_multi_w_load_instructions(
                                base_sb[0:1, bass.ds(g * GROUP, 2 * GROUP)], engines=[mybir.EngineType.PE],
                                min_val=0, max_val=CH - 1)
                        if conv and u == 0 and not wide:
                            _, firsts = nc.values_load_multi_w_load_instructions(
                                base_sb[0:1, bass.ds(g * GROUP, UNROLL, GROUP)], engines=[mybir.EngineType.PE],
                                min_val=0, max_val=CH - 1)
                        bases = None
                        if conv:
                            bases = firsts[u % 2 * GROUP:(u % 2 + 1) * GROUP] if wide else firsts[u:u + 1]
                        mix(g, u, base, 16 * ITER * l + it * 16 + 16, bases)
                        if counting:
                            count_edges(g)
                        if l == 1 and u % 2 == 0:
                            rank_counts(it * 2 + u // 2)
                        if l == 1 and u % 2 == 1:
                            rank_select(it * 2 + u // 2)
                        if conv and not (isinstance(g, int) and g < 1):
                            second(g - 1, 1 - u % 2, base, l)
                        if l == 2 and not (isinstance(g, int) and g < 1):
                            put(g - 1, 1 - u % 2)
                        if not (isinstance(g, int) and g < 2):
                            turn_back(g - 2, u % 2, base)

                if l == 0:
                    pe.wait_ge(hist_zero, 1)
                    nc.tensor.matmul(sort_a[0:HI, 0:2 * LO], zeros_b[:, 0:HI], zeros_b[:, :], start=True, stop=False)
                    iteration(0, True)
                    with pe.Fori(1, ITER // 2) as it:
                        iteration(it, True)
                    tables()
                    keep_flags()
                    with pe.Fori(ITER // 2, ITER - 1) as it:
                        iteration(it)
                else:
                    if l == 2:
                        pe.wait_ge(pl_zeroed, 1)
                        for bank in (sort_a, sort_b):
                            nc.tensor.matmul(bank[:, 0:TILES], pl_zero[:, 0:P], pl_zero[:, :], start=True, stop=False)
                    iteration(0)
                    with pe.Fori(1, ITER - 1) as it:
                        iteration(it)
                iteration(ITER - 1)
                if conv:
                    second(GROUPS - 1, 1, base, l)
                turn_back(GROUPS - 2, 0, base)
                if l == 2:
                    put(GROUPS - 1, 1)
                    for bank in (sort_a, sort_b):
                        last = nc.tensor.matmul(bank[:, 0:TILES], pl_zero[:, 0:P], pl_zero[:, :], start=False, stop=True)
                    last.then_inc(pl_used, 1)
                turn_back(GROUPS - 1, 1, base)

            for l in range(LAYERS):
                node_tables(l)
                pe.wait_ge(split_done, l + 1)
                pe.wait_ge(codes_loaded, 32 + 8 * 16)
                if l == 0:
                    wide = pe.value_load(counter[0:1, 1:2], min_val=0, max_val=1)
                with pe.If(wide != 0):
                    edge_pass(l, True)
                with pe.Else():
                    edge_pass(l)
            edge_pass(LAYERS)

            pe.wait_ge(fin_w, 96)

            def tail_first(k):
                c0, n = block_chunks(k)
                for s, rows in enumerate((nodes, rows_a)):
                    if s == 0:
                        pe.wait_ge(ln_done, k + 1)
                    else:
                        pe.wait_ge(ends[k], 16 * n * (LAYERS + 1))
                    if some(2 * k + s - 1):
                        pe.wait_ge(fin_t, 2 * k + s - 1)
                    for c in range(n):
                        last = nc.tensor.transpose(mixed[s][:, c * P:(c + 1) * P], rows[:, c0 + c, :], ident[:, :])
                    last.then_inc(fin_turned, 1)
                for m in range(2):
                    if some(2 * k + m - 1):
                        pe.wait_ge(fin_act, 2 * k + m - 1)
                    for s in range(2):
                        pe.wait_ge(fin_t, 2 * k + s + 1)
                        last = nc.tensor.matmul(hidden[m][:, 0:n * P], fv1[:, s, m * P:(m + 1) * P],
                                                fin_xt[:, s, c0 * P:(c0 + n) * P], start=(s == 0), stop=(s == 1))
                    last.then_inc(fin_h1, 1)

            def tail_second(k):
                pe.wait_ge(fin_act, 2 * k + 2)
                if some(k - 1):
                    pe.wait_ge(fin_copied, k - 1)
                c0, n = block_chunks(k)
                for c in range(n):
                    for m in range(2):
                        last = nc.tensor.matmul(back[k % 2][:, c * D:(c + 1) * D],
                                                fin_g[:, m, (c0 + c) * P:(c0 + c + 1) * P], fv2[:, m, :],
                                                start=(m == 0), stop=(m == 1))
                last.then_inc(fin_h2, 1)

            for k in range(BLOCKS):
                tail_first(k)
                if k >= 1:
                    tail_second(k - 1)
            tail_second(BLOCKS - 1)

        @block.scalar
        def _(act):
            def root(n):
                act.wait_ge(ln_var, n)
                nc.scalar.sqrt(stat[:, 1, :], stat[:, 0, :]).then_inc(ln_std, 1)

            def spot(g, a, base):
                if some(base + g - 1):
                    act.wait_ge(hot_done, base + g - 1)
                nc.scalar.activation(spots[:, a, :], codes[:, bass.ds(g * GE, GE)], ACT.Abs).then_inc(spots_ready, 1)

            def relu(g, a, base):
                act.wait_ge(mixed_done, base + g + 1)
                if some(base + g - 1):
                    act.wait_ge(hidden_done, base + g - 1)
                nc.scalar.activation(hin[:, a, :], mixed[a][:, :], ACT.Relu).then_inc(relu_done, 1)

            def indices(g, u, cols):
                nc.scalar.copy(idx[:, u, :], cols[:, bass.ds(g * GROUP, GROUP)]).then_inc(idx_ready, 1)

            def copy_out(g, a, base):
                act.wait_ge(backed, base + g + 1)
                nc.scalar.copy(outb[:, a, :, :].rearrange("p j d -> p (j d)"), back[a][:, :]).then_inc(out_copied, 1)

            def edge_pass(l):
                base, conv = l * GROUPS, l < LAYERS
                cols = src_cols if conv else perm_cols

                def iteration(it, last=False):
                    for u in range(UNROLL):
                        g = it * UNROLL + u
                        if conv:
                            if not (last and u == UNROLL - 1):
                                spot(g + 1, 1 - u % 2, base)
                            relu(g, u % 2, base)
                        else:
                            act.wait_ge(mixed_done, base + g + 1)
                        if not last:
                            indices(g + UNROLL, u, cols)
                        if l == 1 and u % 2 == 0:
                            r = it * 2 + u // 2
                            act.wait_ge(rk_turned, r + 1)
                            if some(r):
                                act.wait_ge(rk_sel, r)
                            nc.scalar.copy(rk_hi_t[:, :, :].rearrange("h t e -> h (t e)"),
                                           sort_b[:, :].bitcast(BF16)[0:HI, :]).then_inc(rk_turned_sb, 1)
                        if not (isinstance(g, int) and g < 2):
                            before_g = GROUPS // 2 * l + it * 2 + u // 2 - 1
                            if some(before_g):
                                act.wait_ge(stored[u % 2], 16 * before_g)
                            copy_out(g - 2, u % 2, base)

                if conv:
                    spot(0, 0, base)
                iteration(0)
                with act.Fori(1, ITER - 1) as it:
                    iteration(it)
                iteration(ITER - 1, True)
                for a in range(2):
                    act.wait_ge(stored[a], 16 * (GROUPS // 2 * (l + 1) - 1))
                    copy_out(GROUPS - 2 + a, a, base)

            root(1)
            act.wait_ge(edge_cols_done, 1)
            for u in range(UNROLL):
                indices(u, u, src_cols)
            for l in range(LAYERS):
                for k in range(BLOCKS + 1):
                    if k < BLOCKS:
                        c0, n = block_chunks(k)
                        act.wait_ge(rows_turned, BLOCKS * l + k + 1)
                        nc.scalar.copy(xt[:, c0 * P:(c0 + n) * P], mixed[k % 2][:, 0:n * P]).then_inc(xt_ready, 1)
                    if k == 0:
                        continue
                    for q in pairs_of(k - 1):
                        n = min(2, CH - 2 * q)
                        act.wait_ge(a_ready, PAIRS * l + q + 1)
                        nc.scalar.copy(rows_b[:, 2 * q:2 * q + n, :],
                                       hidden[q % 2][:, :].rearrange("p (c n) -> p c n", c=2)[:, 0:n, D:2 * D]).then_inc(b_ready, 1)
                act.wait_ge(codes_loaded, 32 + 8 * 16)
                act.wait_ge(split_done, l + 1)
                act.wait_ge(b_saved, 16 * BLOCKS * (l + 1))
                edge_pass(l)
                if l < LAYERS - 1:
                    for u in range(UNROLL):
                        indices(u, u, src_cols)
            act.wait_ge(perm_ready, 1)
            for u in range(UNROLL):
                indices(u, u, perm_cols)
            edge_pass(LAYERS)
            root(2)
            for k in range(BLOCKS):
                c0, n = block_chunks(k)
                for s in range(2):
                    act.wait_ge(fin_turned, 2 * k + s + 1)
                    nc.scalar.copy(fin_xt[:, s, c0 * P:(c0 + n) * P], mixed[s][:, 0:n * P]).then_inc(fin_t, 1)
                for m in range(2):
                    act.wait_ge(fin_h1, 2 * k + m + 1)
                    nc.scalar.activation(fin_g[:, m, c0 * P:(c0 + n) * P], hidden[m][:, 0:n * P], ACT.Silu,
                                         bias=fc1[:, m:m + 1]).then_inc(fin_act, 1)
            root(3)

        @block.vector
        def _(dve):
            taken = [0]
            v = nc.vector

            def step(ins):
                taken[0] += 1
                ins.then_inc(dve_steps, 1)
                dve.wait_ge(dve_steps, taken[0])

            def spread(col, n=CH):
                return col.unsqueeze(2).to_broadcast((P, n, D))

            def along(vec, n=CH):
                return vec.unsqueeze(1).to_broadcast((P, n, D))

            def normalise(n, rows, centred, squares):
                step(v.tensor_reduce(stat[:, 2, :], rows, AX_X, ALU.add))
                step(v.tensor_scalar(stat[:, 3, :], stat[:, 2, :], -1.0 / D, None, ALU.mult))
                step(v.tensor_tensor(centred, rows, spread(stat[:, 3, :]), ALU.add))
                step(v.tensor_tensor(squares, centred, centred, ALU.mult))
                step(v.tensor_reduce(stat[:, 2, :], squares, AX_X, ALU.add))
                v.tensor_scalar(stat[:, 0, :], stat[:, 2, :], 1.0 / D, EPS, ALU.mult, ALU.add).then_inc(ln_var, 1)
                dve.wait_ge(ln_std, n)
                step(v.reciprocal(stat[:, 2, :], stat[:, 1, :]))

            v.memset(prev_i[:, :], N).then_inc(clears, 1)
            v.memset(dst_i[:, :], N)
            v.memset(src_i[:, :], N)
            dve.wait_ge(clears, 1)
            v.memset(prev_i[0:1, 0:1], -1).then_inc(ids_cleared, 1)
            v.memset(xres[:, CH - 1, :], 0.0).then_inc(x_cleared, 1)
            v.memset(list_idx[:, :], SKIP)
            v.memset(a_parts[:, CH, :, :], 0.0)
            v.memset(first_state[:, :], 0.0)
            step(v.memset(ones_e[:, :], 1.0))

            dve.wait_ge(ids_loaded, 16 * 5)
            step(v.tensor_tensor(head[:, :], dst_i[:, :], prev_i[:, :], ALU.not_equal))
            v.tensor_copy(dst_f[:, :], dst_i[:, :])
            v.tensor_tensor_scan(cum[:, :], ones_e[:, :], head[:, :], 0.0, ALU.mult, ALU.add).then_inc(seg_totals, 1)
            v.tensor_scalar(sign[:, :], head[:, :], -2.0, 1.0, ALU.mult, ALU.add)
            dve.wait_ge(seg_totals, 1)
            step(v.tensor_scalar(rel[:, :], head[:, :], -float(SKIP), float(SKIP - 1), ALU.mult, ALU.add))
            dve.wait_ge(seg_before, 1)
            step(v.tensor_scalar(seg[:, :], cum[:, :], banks[7][0:GROUPS, 0:1], None, ALU.add))
            step(v.tensor_tensor(head_seg[:, :], seg[:, :], rel[:, :], ALU.add))
            step(v.tensor_scalar(seg[:, :], seg[:, :], -1.0, None, ALU.add))
            step(v.tensor_copy(seg_i[:, :], seg[:, :]))
            v.tensor_copy(seg_last[:, 0:1], seg_i[:, GE - 1:GE])
            v.tensor_scalar(last_i[:, :], seg_i[:, GE - 1:GE], 7, None, ALU.logical_shift_right)
            step(v.tensor_scalar(base_i[:, :], seg_i[:, 0:GE:P], 7, None, ALU.logical_shift_right))
            v.tensor_copy(last_f[:, :], last_i[:, :])
            step(v.tensor_copy(base_f[:, :], base_i[:, :]))
            v.tensor_scalar(wide_q[:, :], last_f[:, :], base_f[:, 0:1], 1.5, ALU.subtract, ALU.is_gt).then_inc(wide_groups, 1)
            dve.wait_ge(wide_sum, 1)
            step(v.tensor_scalar(wide_f[:, :], banks[7][0:GROUPS, 8:9], 0.5, None, ALU.is_gt))
            v.tensor_copy(seg_last[:, 1:2], wide_f[:, :])
            step(v.tensor_scalar(base_u[:, :], base_f[:, :], base_f[:, 0:1], wide_f[:, 0:1], ALU.subtract, ALU.mult))
            step(v.tensor_scalar(base_u[:, :], base_u[:, :], base_f[:, 0:1], None, ALU.add))
            v.tensor_copy(base_h[:, :], base_u[:, :])
            step(v.tensor_scalar(base_f[:, :], base_u[:, :], float(P), -1.0, ALU.mult, ALU.add))
            tiles = lambda ap: ap.rearrange("q (j r) -> q j r", r=P)
            step(v.tensor_tensor(tiles(rel[:, :]), tiles(seg[:, :]), base_f[:, :].unsqueeze(2).to_broadcast((GROUPS, GROUP, P)),
                                 ALU.subtract))
            v.tensor_tensor(code_b[:, :], rel[:, :], sign[:, :], ALU.mult).then_inc(codes_ready, 1)
            dve.wait_ge(src_loaded, 32)
            v.tensor_copy(src_f[:, :], src_i[:, :]).then_inc(srcf_ready, 1)

            dve.wait_ge(cols_turned, 3)
            for bank, cols in ((banks[4], dst_cols), (banks[5], head_cols), (banks[6], src_cols)):
                last = v.tensor_copy(cols[:, :].rearrange("p (q j) -> p j q", j=GROUP),
                                     bank[:, :].rearrange("p (j q) -> p j q", j=GROUP)[:, :, 0:GROUPS])
            step(last)
            step(v.tensor_scalar(part_i[:, :], src_cols[:, :], 6, None, ALU.logical_shift_right))
            step(v.tensor_copy(src_hi[:, :], part_i[:, :]))
            step(v.tensor_scalar(part_i[:, :], src_cols[:, :], LO - 1, None, ALU.bitwise_and))
            v.tensor_copy(src_lo[:, :], part_i[:, :]).then_inc(edge_cols_done, 1)

            dve.wait_ge(x_loaded, 32)
            normalise(1, xres[:, :, :], nodes[:, :, :], rows_a[:, :, :])
            for k in range(BLOCKS):
                c, n = block_chunks(k)
                v.scalar_tensor_tensor(nodes[:, c:c + n, :], nodes[:, c:c + n, :], 0.0, spread(stat[:, 2, c:c + n], n),
                                       ALU.max, ALU.mult).then_inc(rows_ready, 1)
            dve.wait_ge(weights_loaded, 16 * 5 * LAYERS)
            v.tensor_tensor(w_ab[:, :, 0:D], w_ab[:, :, 0:D], w_ab[:, :, D:2 * D], ALU.subtract).then_inc(w_ready, 1)

            dve.wait_ge(codes_loaded, 32)
            occurring = dve.value_load(counter[0:1, 0:1], min_val=0, max_val=NP)

            def split(k):
                c, n = block_chunks(k)
                a, left, parts = rows_a[:, c:c + n, :], rest[:, c:c + n, :], a_parts[:, c:c + n]
                step(v.tensor_copy(parts[:, :, 0, :], a))
                step(v.tensor_tensor(left, a, parts[:, :, 0, :], ALU.subtract))
                step(v.tensor_copy(parts[:, :, 1, :], left))
                step(v.tensor_tensor(left, left, parts[:, :, 1, :], ALU.subtract))
                return v.tensor_copy(parts[:, :, 2, :], left)


            def node_rows(l, k):
                c, n = block_chunks(k)
                rows = nodes[:, c:c + n, :]
                dve.wait_ge(ends[k], 16 * n * l)
                step(v.tensor_tensor(rows, rows, along(b2_sb[:, l - 1, :], n), ALU.add))
                v.scalar_tensor_tensor(rows, rows, 0.0, spread(present[:, c:c + n], n),
                                       ALU.max, ALU.mult).then_inc(rows_ready, 1)

            def hot(g, a, base):
                if some(base + g - 1):
                    dve.wait_ge(mixed_done, base + g - 1)
                dve.wait_ge(spots_ready, base + g + 1)
                for k in range(2):
                    last = v.tensor_scalar(onehot[a][:, k, :], spots[:, a, :], place[:, k:k + 1], None, ALU.is_equal)
                last.then_inc(hot_done, 1)

            def mark(g, a, base):
                if some(base + g - 1):
                    dve.wait_ge(scanned, base + g - 1)
                v.tensor_scalar(mask[:, a, :], codes[:, bass.ds(g * GE, GE)], 0.0, -HUGE, ALU.is_lt,
                                ALU.mult).then_inc(mask_ready, 1)

            def scan(g, a, base, conv, keeps=0):
                dve.wait_ge(hidden_done if conv else mixed_done, base + g + 1)
                if some(base + g - 1):
                    dve.wait_ge(backed, base + g - 1)
                if some(base + g):
                    dve.wait_ge(scanned, base + g)
                state = first_state[:, :] if isinstance(g, int) and g == 0 else run[:, 1 - a, GE - 1:GE]
                if not conv:
                    dve.wait_ge(keep_loaded[a], keeps)
                    v.tensor_tensor_scan(run[:, a, :], mask[:, a, :], mixed[a][:, :], state,
                                         ALU.mult, ALU.add).then_inc(scanned, 1)
                else:
                    dve.wait_ge(mask_ready, base + g + 1)
                    v.tensor_tensor_scan(run[:, a, :], mask[:, a, :], hidden[a][:, :], state,
                                         ALU.add, ALU.max).then_inc(scanned, 1)

            def one_hot(to, cols, r, width):
                return v.tensor_tensor(to, cols[:, bass.ds(r * IT, IT)].unsqueeze(2).to_broadcast((P, IT, width)),
                                       iota[:, 0:width].unsqueeze(1).to_broadcast((P, IT, width)), ALU.is_equal)

            def count_edges(r):
                if some(r):
                    dve.wait_ge(hist_src_used, r)
                one_hot(hot_hi[0][:, :, :], src_hi, r, HI)
                one_hot(hot_lo[0][:, :, :], src_lo, r, LO).then_inc(hist_src, 1)
                if some(r):
                    dve.wait_ge(hist_dst_used, r)
                one_hot(hot_hi[1][:, :, :], dst_hi, r, HI)
                one_hot(hot_lo[1][:, :, :], dst_lo, r, LO).then_inc(hist_dst, 1)

            def tables():
                dve.wait_ge(hist_done, 1)
                step(v.tensor_copy(c_sb[:, :], sort_a[0:HI, 0:2 * LO]))
                v.tensor_tensor_scan(c_cum[:, 0:LO], ones_h[:, 0:LO], c_sb[:, 0:LO], 0.0, ALU.mult, ALU.add)
                v.tensor_tensor_scan(c_cum[:, LO:2 * LO], ones_h[:, LO:2 * LO], c_sb[:, LO:2 * LO], 0.0,
                                     ALU.mult, ALU.add).then_inc(hist_rows, 1)
                v.tensor_scalar(c_out[:, 3, :], c_sb[:, LO:2 * LO], 0.0, None, ALU.is_gt)
                step(v.tensor_scalar(c_none[:, :], c_sb[:, :], 0.0, float(SKIP), ALU.is_equal, ALU.mult))
                dve.wait_ge(hist_base, 1)
                v.tensor_scalar(c_end[:, 0:LO], c_cum[:, 0:LO], sort_b[0:HI, 0:1], None, ALU.add)
                step(v.tensor_scalar(c_end[:, LO:2 * LO], c_cum[:, LO:2 * LO], sort_b[0:HI, 8:9], None, ALU.add))
                step(v.tensor_tensor(base_keep[0:HI, :], c_end[:, 0:LO], c_sb[:, 0:LO], ALU.subtract))
                v.scalar_tensor_tensor(c_out[:, 0, :], c_end[:, LO:2 * LO], -1.0, c_none[:, LO:2 * LO], ALU.add, ALU.add)
                v.scalar_tensor_tensor(c_out[:, 1, :], c_end[:, 0:LO], -1.0, c_none[:, 0:LO], ALU.add, ALU.add)
                v.tensor_tensor(c_out[:, 2, :], base_keep[0:HI, :], c_none[:, 0:LO], ALU.add).then_inc(tables_ready, 1)

            def keep_flags():
                dve.wait_ge(tables_loaded, 64)
                v.tensor_copy(end_dst[:, :], cols_f[:, 0, :])
                v.tensor_copy(end_src[:, :], cols_f[:, 1, :])
                v.tensor_copy(present[:, :], cols_f[:, 3, :]).then_inc(cols_ready, 1)
                step(v.tensor_copy(keep_i[:, :], cols_f[:, 2, :]))
                step(v.tensor_scalar(keep_t[:, :], keep_i[:, :], 9, None, ALU.logical_shift_right))
                step(v.tensor_copy(keep_hi[:, :], keep_t[:, :]))
                step(v.tensor_scalar(keep_t[:, :], keep_i[:, :], GE - 1, None, ALU.bitwise_and))
                step(v.tensor_copy(keep_lo[:, :], keep_t[:, :]))
                for c in range(CH):
                    if some(c - 1):
                        dve.wait_ge(keep_used, c - 1)
                    v.tensor_scalar(keep_l[:, c % 2, :], iota[:, 0:P], keep_hi[:, c:c + 1], None, ALU.is_equal)
                    v.tensor_scalar(keep_r[:, c % 2, :], iota[:, :], keep_lo[:, c:c + 1], None, ALU.is_equal).then_inc(keep_hot, 1)
                dve.wait_ge(keep_used, CH)
                v.tensor_scalar(keep_q[:, :], sort_b[0:GROUPS, :], -1.0, 1.0, ALU.mult, ALU.add).then_inc(keep_ready, 1)

            def rank_begin(r):
                if some(r):
                    dve.wait_ge(rk_turned, r)
                one_hot(rk_hot_hi[:, :, :], src_hi, r, HI)
                one_hot(rk_hot_lo[:, :, :], src_lo, r, LO).then_inc(rk_hot, 1)
                dve.wait_ge(rk_rows, 16 * r + 16)
                for t in range(IT):
                    last = v.scalar_tensor_tensor(rk_row[:, t * P:(t + 1) * P], rk_row[:, t * P:(t + 1) * P],
                                                  src_cols[:, bass.ds(r * IT + t, 1)], after[:, :], ALU.is_equal, ALU.mult,
                                                  accum_out=rk_within[:, t:t + 1])
                last.then_inc(rk_step, 1)

            def rank_bases(r):
                dve.wait_ge(rk_prefix, r + 1)
                v.tensor_tensor(rk_bases[:, 1:IT + 1, :], sort_a[0:HI, :].rearrange("h (t l) -> h t l", l=LO),
                                rk_bases[:, 0:1, :].to_broadcast((HI, IT, LO)), ALU.add).then_inc(rk_base, 1)

            def rank_end(r):
                dve.wait_ge(rk_sel, r + 1)
                dve.wait_ge(rk_base, r + 1)
                dve.wait_ge(rk_step, 5 * r + 1)
                v.tensor_copy(rk_bases[:, 0, :], rk_bases[:, IT, :])
                v.tensor_tensor(rk_prod[:, :, :], sort_b[:, :].rearrange("p (t l) -> p t l", l=LO),
                                rk_hot_lo[:, :, :], ALU.mult).then_inc(rk_read, 1)
                dve.wait_ge(rk_read, r + 1)
                v.tensor_reduce(rk_prior[:, :], rk_prod[:, :, :], AX_X, ALU.add).then_inc(rk_used, 1)
                dve.wait_ge(rk_used, r + 1)
                v.tensor_tensor(rk_rank[:, :], rk_prior[:, :], rk_within[:, :], ALU.add).then_inc(rk_step, 1)
                dve.wait_ge(rk_step, 5 * r + 2)
                v.tensor_scalar(rk_p_i[:, :], rk_rank[:, :], P - 1, None, ALU.bitwise_and).then_inc(rk_step, 1)
                v.tensor_scalar(rk_t_i[:, :], rk_rank[:, :], 7, None, ALU.logical_shift_right).then_inc(rk_step, 1)
                dve.wait_ge(rk_step, 5 * r + 4)
                v.tensor_copy(rank_pt[:, bass.ds(r * IT, IT)], rk_p_i[:, :])
                v.tensor_copy(rank_pt[:, bass.ds(r * IT + TILES, IT)], rk_t_i[:, :]).then_inc(rk_step, 1)

            def put(g, a):
                if some(g - 1):
                    dve.wait_ge(pl_used, g - 1)
                for j in range(GROUP):
                    t = g * GROUP + j
                    p_at, t_at = rank_pt[:, bass.ds(t, 1)], rank_pt[:, bass.ds(t + TILES, 1)]
                    v.tensor_scalar(pl_p[:, a, j, :], iota[:, 0:P], p_at, part16[:, 0:1], ALU.is_equal, ALU.mult)
                    v.tensor_scalar(pl_t[:, a, j, :], iota[:, 0:P], p_at, iota[:, bass.ds(t, 1)], ALU.is_equal, ALU.mult)
                    last = v.tensor_scalar(pl_tile[:, a, j, :], iota[:, 0:TILES], t_at, None, ALU.is_equal)
                last.then_inc(pl_ready, 1)

            def edge_pass(l):
                base, conv = l * GROUPS, l < LAYERS

                def iteration(it, counting=False, final=False):
                    for u in range(UNROLL):
                        g = it * UNROLL + u
                        if conv and not (final and u == UNROLL - 1):
                            hot(g + 1, 1 - u % 2, base)
                        if counting:
                            count_edges(g)
                        if l == 1 and u % 2 == 0:
                            rank_begin(it * 2 + u // 2)
                        if l == 1 and u % 2 == 1:
                            rank_bases(it * 2 + u // 2)
                        if l == 2:
                            put(g, u % 2)
                        if not (isinstance(g, int) and g < 1):
                            scan(g - 1, 1 - u % 2, base, conv, 16 * (it * 2 + (u + 1) // 2))
                        if conv and not (final and u == UNROLL - 1):
                            mark(g + 1, 1 - u % 2, base)
                        if l == 1 and u % 2 == 1:
                            rank_end(it * 2 + u // 2)

                if conv:
                    hot(0, 0, base)
                    mark(0, 0, base)
                if l == 0:
                    iteration(0, True)
                    with dve.Fori(1, ITER // 2) as it:
                        iteration(it, True)
                    tables()
                    keep_flags()
                    with dve.Fori(ITER // 2, ITER - 1) as it:
                        iteration(it)
                else:
                    iteration(0)
                    with dve.Fori(1, ITER - 1) as it:
                        iteration(it)
                iteration(ITER - 1, final=True)
                scan(GROUPS - 1, 1, base, conv, 16 * (GROUPS // 2))

            for l in range(LAYERS):
                for k in range(BLOCKS + 1):
                    if l and k < BLOCKS:
                        node_rows(l, k)
                    if k == 0:
                        continue
                    for q in pairs_of(k - 1):
                        n = min(2, CH - 2 * q)
                        dve.wait_ge(ab_ready, PAIRS * l + q + 1)
                        v.tensor_tensor(rows_a[:, 2 * q:2 * q + n, :],
                                        hidden[q % 2][:, :].rearrange("p (c n) -> p c n", c=2)[:, 0:n, 0:D],
                                        along(b1_sb[:, l, :], n), ALU.add).then_inc(a_ready, 1)
                    dve.wait_ge(a_ready, PAIRS * l + pairs_of(k - 1)[-1] + 1)
                    split(k - 1).then_inc(a_split, 1)
                dve.wait_ge(a_split, BLOCKS * (l + 1))
                steps_before = taken[0]
                with dve.If(occurring != N):
                    dve.wait_ge(compact, l + 1)
                    for k in range(BLOCKS):
                        split(k).then_inc(a_resplit, 1)
                    nc.vector.sem_inc(split_done, 1)
                with dve.Else():
                    nc.vector.sem_inc(dve_steps, taken[0] - steps_before)
                    nc.vector.sem_inc(split_done, 1)
                dve.wait_ge(codes_loaded, 32 + 8 * 16)
                dve.wait_ge(b_saved, 16 * BLOCKS * (l + 1))
                if l == 0:
                    v.memset(ones_h[:, :], 1.0)
                    v.memset(zeros_b[:, :], 0.0).then_inc(hist_zero, 1)
                    step(v.tensor_scalar(dst_part[:, :], dst_cols[:, :], 6, None, ALU.logical_shift_right))
                    step(v.tensor_copy(dst_hi[:, :], dst_part[:, :]))
                    step(v.tensor_scalar(dst_part[:, :], dst_cols[:, :], LO - 1, None, ALU.bitwise_and))
                    step(v.tensor_copy(dst_lo[:, :], dst_part[:, :]))
                    dve.wait_ge(rows_turned, BLOCKS)
                    v.memset(nodes[:, :, :], 0.0).then_inc(nodes_cleared, 1)
                    dve.wait_ge(consts, 2)
                if l == 1:
                    step(v.tensor_copy(rk_bases[:, 0, :], base_keep[0:HI, :]))
                    step(v.tensor_copy(rk_ident[:, :], ident[:, :]))
                if l == 2:
                    v.memset(pl_zero[:, :], 0.0).then_inc(pl_zeroed, 1)
                edge_pass(l)

            dve.wait_ge(pl_used, GROUPS + 1)
            step(v.tensor_copy(pl_perm[:, :], sort_a[:, 0:TILES]))
            step(v.scalar_tensor_tensor(pl_perm[:, :], sort_b[:, 0:TILES], float(P), pl_perm[:, :], ALU.mult, ALU.add))
            step(v.tensor_scalar(perm_cols[:, :], pl_perm[:, :], float(E - 1), None, ALU.min))
            v.memset(rows_a[:, :, :], 0.0).then_inc(agg_cleared, 1)
            nc.vector.sem_inc(perm_ready, 1)
            edge_pass(LAYERS)

            for k in range(BLOCKS):
                dve.wait_ge(ends[k], 16 * block_chunks(k)[1] * LAYERS)
            step(v.tensor_tensor(nodes[:, :, :], nodes[:, :, :], along(b2_sb[:, LAYERS - 1, :]), ALU.add))
            step(v.tensor_tensor(nodes[:, :, :], nodes[:, :, :], spread(present[:, :]), ALU.mult))
            step(v.tensor_tensor(xres[:, :, :], xres[:, :, :], nodes[:, :, :], ALU.add))
            normalise(2, xres[:, :, :], nodes[:, :, :], fin_tmp[:, :, :])
            for k in range(BLOCKS):
                c, n = block_chunks(k)
                v.scalar_tensor_tensor(nodes[:, c:c + n, :], nodes[:, c:c + n, :], 0.0, spread(stat[:, 2, c:c + n], n),
                                       ALU.max, ALU.mult).then_inc(ln_done, 1)
            dve.wait_ge(ln_done, BLOCKS)
            dve.wait_ge(fin_w, 96)
            step(v.tensor_tensor(xres[:, :, :], xres[:, :, :], nodes[:, :, :], ALU.add))
            step(v.tensor_tensor(xres[:, :, :], xres[:, :, :], along(fbeta), ALU.add))

            for k in range(BLOCKS):
                c, n = block_chunks(k)
                y, sq = fin_y[:, c:c + n, :], fin_tmp[:, c:c + n, :]
                dve.wait_ge(fin_h2, k + 1)
                v.tensor_tensor(y, back[k % 2][:, :].rearrange("p (c d) -> p c d", d=D)[:, 0:n, :], along(fc2, n),
                                ALU.add).then_inc(fin_copied, 1)
                dve.wait_ge(fin_copied, k + 1)
                step(v.tensor_reduce(stat[:, 2, c:c + n], y, AX_X, ALU.add))
                step(v.tensor_scalar(stat[:, 3, c:c + n], stat[:, 2, c:c + n], -1.0 / D, None, ALU.mult))
                step(v.tensor_tensor(y, y, spread(stat[:, 3, c:c + n], n), ALU.add))
                step(v.tensor_tensor(sq, y, y, ALU.mult))
                step(v.tensor_reduce(stat[:, 2, c:c + n], sq, AX_X, ALU.add))
            v.tensor_scalar(stat[:, 0, :], stat[:, 2, :], 1.0 / D, EPS, ALU.mult, ALU.add).then_inc(ln_var, 1)
            dve.wait_ge(ln_std, 3)
            step(v.reciprocal(stat[:, 2, :], stat[:, 1, :]))
            for k in range(BLOCKS):
                c, n = block_chunks(k)
                y = fin_y[:, c:c + n, :]
                step(v.tensor_tensor(y, y, spread(stat[:, 2, c:c + n], n), ALU.mult))
                step(v.tensor_tensor(y, y, along(fgamma, n), ALU.mult))
                v.tensor_tensor(y, y, xres[:, c:c + n, :], ALU.add).then_inc(fin_rows, 1)


_INS = ["x", "src", "dst", "edge_attr_128"] + [
    f"L0_gnn_{w}_{l}" for l in ("in", "hid", "out") for w in ("W1", "b1", "W2", "b2")] + [
    f"L1_gnn_{w}" for w in ("W1", "b1", "W2", "b2", "ln_gamma", "ln_beta")]


def kernel(**inputs):
    import concourse.bacc as _bacc
    from concourse.bass_utils import run_bass_kernel_spmd as _run

    nc = _bacc.Bacc("TRN2", target_bir_lowering=False, num_devices=1)
    arrays, aps = {}, {}
    for name in _INS:
        a = np.ascontiguousarray(inputs[name])
        arrays[f"in_{name}"] = a
        aps[name] = nc.dram_tensor(f"in_{name}", a.shape, mybir.dt.from_np(a.dtype), kind="ExternalInput").ap()
    out = nc.dram_tensor("out_0", (N, D), F32, kind="ExternalOutput").ap()
    layers = [[aps[f"L0_gnn_{w}_{l}"] for l in ("in", "hid", "out")] for w in ("W1", "b1", "W2", "b2")]
    build(nc, aps["x"], aps["src"], aps["dst"], aps["edge_attr_128"], *layers,
          *(aps[f"L1_gnn_{w}"] for w in ("W1", "b1", "W2", "b2", "ln_gamma", "ln_beta")), out)
    r = _run(nc, [arrays], core_ids=[0])
    return r.results[0]["out_0"]
```

```python
from contextlib import ExitStack

import numpy as np
import concourse.bass as bass
from concourse import mybir

F32 = mybir.dt.float32
BF16 = mybir.dt.bfloat16
FP16 = mybir.dt.float16
I32 = mybir.dt.int32
I16 = mybir.dt.int16
ALU = mybir.AluOpType
ACT = mybir.ActivationFunctionType
AX_X = mybir.AxisListType.X

P = 128
N, D, E = 3125, 128, 53125
LAYERS = 3
EPS = 1e-5
CH = -(-N // P)
NP = CH * P
NLAST = N - (CH - 1) * P
TILES = -(-E // P)
EP = TILES * P
GROUP = 4
GE = GROUP * P
GROUPS = TILES // GROUP
UNROLL = 4
ITER = GROUPS // UNROLL
IT = 8
PUT = 2
SUM_TILES = (EP + CH * (P - 1)) // P
SUM_GROUPS = SUM_TILES // GROUP
SUM_ITER = SUM_GROUPS // UNROLL
EARLY = 5
CODE_LOADS = 1 + ITER - EARLY
AHEAD = 4
AHEAD_BLOCKS = 3
A_LAG = (5, 2, 2)
SHIFT = 1280
ROUNDS = TILES // IT
NB4 = CH // 4
FULLROWS = E // GE
TAIL = E - FULLROWS * GE
BLOCKS = -(-CH // 4)
LO = 64
HI = NP // LO
HUGE = 3.0e38
SKIP = 1 << 17
assert GROUPS % UNROLL == 0 and ITER % 2 == 0 and FULLROWS == GROUPS - 1 and TAIL < GE
assert ROUNDS * 2 == GROUPS and NP == HI * LO and SUM_TILES % GROUP == 0 and PUT * GROUPS * 2 == TILES
assert TILES * 8 - SHIFT <= 2048 and SHIFT <= 2048 and SUM_TILES <= 512 and BLOCKS + 2 < SUM_ITER


def some(n):
    return not (isinstance(n, int) and n <= 0)


def block_chunks(k):
    return 4 * k, min(4, CH - 4 * k)


def build(nc, x, src, dst, attr, w1, b1, w2, b2, v1, c1, v2, c2, gamma, beta, out):
    with ExitStack() as ctx:
        def sb(name, shape, dt=F32):
            return ctx.enter_context(nc.sbuf_tensor(name, shape, dt))

        def sem(name):
            return ctx.enter_context(nc.semaphore(name))

        def dram(name, shape, dt=F32):
            return nc.dram_tensor(name, shape, dt).ap()

        def view(region, at, shape, dt=F32):
            count = int(np.prod(shape))
            ap = region[:, at:at + (-(-count // 2) if dt in (BF16, FP16) else count)]
            if dt != F32:
                ap = ap.bitcast(dt)
            ap = ap[:, 0:count]
            if len(shape) == 2:
                ap = ap.rearrange("p (a b) -> p a b", a=shape[0])
            if len(shape) == 3:
                ap = ap.rearrange("p (a b c) -> p a b c", a=shape[0], b=shape[1])
            return ap

        b_rows = dram("b_rows", (NP, D))
        a_rows = dram("a_rows", (NP, D))
        max_rows = dram("max_rows", (EP, D))
        code_row = dram("code_row", (EP,), FP16)
        base_row = dram("base_row", (TILES,), I16)
        count_row = dram("count_row", (GROUPS * 2,), I32)
        seg_node = dram("seg_node", (NP, 1), I32)
        node_cols = dram("node_cols", (2, NP))

        xres = sb("xres", [P, CH, D])
        nodes = sb("nodes", [P, CH, D])
        rows_a = sb("rows_a", [P, CH, D])
        big = sb("big", [P, EP // 2])
        work = sb("work", [P, 2 * CH * D])
        a_parts = sb("a_parts", [P, CH + 1, 3, D], BF16)
        ring_lo = sb("ring_lo", [P, 2, GROUP, D])
        src_cols = sb("src_cols", [P, SUM_TILES], I32)
        perm_cols = sb("perm_cols", [P, SUM_TILES], I32)
        base_sb = sb("base_sb", [1, TILES], I16)
        idx = sb("idx", [P, UNROLL, GROUP], I32)
        w_ab = sb("w_ab", [P, LAYERS, 2 * D])
        w2_sb = sb("w2_sb", [P, LAYERS, D])
        b1_sb = sb("b1_sb", [P, LAYERS, D])
        b2_sb = sb("b2_sb", [P, LAYERS, D])
        ident = sb("ident", [P, P])
        before = sb("before", [P, P])
        place = sb("place", [P, 2])
        iota = sb("iota", [P, GE], FP16)
        pack_a = sb("pack_a", [P, TILES], FP16)
        pack_b = sb("pack_b", [P, TILES], FP16)
        bucket_sb = sb("bucket_sb", [1, SUM_TILES], I16)
        first_state = sb("first_state", [P, 1])
        present = sb("present", [P, CH])
        end_dst = sb("end_dst", [P, CH], I32)
        stat = sb("stat", [P, 4, CH])
        counter = sb("counter", [1, 4], I32)
        list_idx = sb("list_idx", [P, CH], I32)
        list_at = sb("list_at", [P, 1], I32)
        list_val = sb("list_val", [P, 1], I32)

        rows_b = view(work, 0, (CH, D))
        xt = view(work, CH * D, (CH * D,))
        rest = view(work, CH * D, (CH, D))
        hin = view(work, 0, (2, GE))
        run = view(work, 2 * GE, (2, GE))
        outb = view(work, 4 * GE, (2, GROUP, D))
        onehot = [view(work, 6 * GE + a * GE, (2, GE), BF16) for a in range(2)]
        mask = view(work, 8 * GE, (2, GE), BF16)
        spots = view(work, 9 * GE, (2, GE), FP16)
        ring_hi = view(work, 10 * GE, (2, GROUP, D))
        ring = [ring_lo[:, 0], ring_lo[:, 1], ring_hi[:, 0], ring_hi[:, 1]]
        codes = big[:, :].bitcast(FP16)
        dst_cols = perm_cols
        rank_f = perm_cols[:, :].bitcast(F32)
        rank_pt = perm_cols[:, :].bitcast(FP16)
        lo_cols = src_cols[:, :].bitcast(F32)
        hot_sum = view(work, 2 * GE, (2, GROUP, P))

        banks = [ctx.enter_context(nc.psum_tensor(f"bank{i}", [P, 512], F32)) for i in range(8)]
        mixed, hidden, back, sort_a, sort_b = banks[0:2], banks[2:4], banks[4:6], banks[6], banks[7]

        ids_cleared = sem("ids_cleared")
        ids_loaded = sem("ids_loaded")
        src_loaded = sem("src_loaded")
        x_cleared = sem("x_cleared")
        x_loaded = sem("x_loaded")
        weights_loaded = sem("weights_loaded")
        w_ready = sem("w_ready")
        consts = sem("consts")
        clears = sem("clears")
        seg_totals = sem("seg_totals")
        seg_before = sem("seg_before")
        wide_groups = sem("wide_groups")
        wide_sum = sem("wide_sum")
        codes_ready = sem("codes_ready")
        codes_saved = sem("codes_saved")
        codes_first = sem("codes_first")
        codes_loaded = sem("codes_loaded")
        srcf_ready = sem("srcf_ready")
        cols_turned = sem("cols_turned")
        cols_copied = sem("cols_copied")
        x_mean = sem("x_mean")
        x_squares = sem("x_squares")
        x_scale = sem("x_scale")
        edge_cols_done = sem("edge_cols_done")
        node_list = sem("node_list")
        node_list_ready = sem("node_list_ready")
        list_copied = sem("list_copied")
        may_gather = sem("may_gather")
        a_gather = sem("a_gather")
        a_saved = sem("a_saved")
        compact = sem("compact")
        a_resplit = sem("a_resplit")
        ln_var = sem("ln_var")
        ln_std = sem("ln_std")
        ln_done = sem("ln_done")
        rows_ready = sem("rows_ready")
        rows_turned = sem("rows_turned")
        xt_ready = sem("xt_ready")
        b_done = sem("b_done")
        a_done = sem("a_done")
        a_ready = sem("a_ready")
        b_ready = sem("b_ready")
        b_saved = sem("b_saved")
        cast = [sem(f"cast{i}") for i in range(3)]
        left = [sem(f"left{i}") for i in range(2)]
        split_done = sem("split_done")
        idx_ready = sem("idx_ready")
        mixed_done = sem("mixed_done")
        spots_ready = sem("spots_ready")
        hot_done = sem("hot_done")
        mask_ready = sem("mask_ready")
        relu_done = sem("relu_done")
        hidden_done = sem("hidden_done")
        scanned = sem("scanned")
        backed = sem("backed")
        out_copied = sem("out_copied")
        hist_zero = sem("hist_zero")
        hist_hot = sem("hist_hot")
        hist_used = sem("hist_used")
        hist_done = sem("hist_done")
        hist_rows = sem("hist_rows")
        hist_base = sem("hist_base")
        tables_ready = sem("tables_ready")
        tables_saved = sem("tables_saved")
        tables_loaded = sem("tables_loaded")
        cols_ready = sem("cols_ready")
        ends_hot = sem("ends_hot")
        buckets_found = sem("buckets_found")
        rk_hot = sem("rk_hot")
        rk_prefix = sem("rk_prefix")
        rk_read = sem("rk_read")
        rk_step = sem("rk_step")
        pl_zeroed = sem("pl_zeroed")
        pl_ready = sem("pl_ready")
        pl_used = sem("pl_used")
        perm_ready = sem("perm_ready")
        sum_hot = sem("sum_hot")
        agg_added = sem("agg_added")
        nodes_cleared = sem("nodes_cleared")
        fin_w = sem("fin_w")
        fin_turned = sem("fin_turned")
        fin_t = sem("fin_t")
        may_act = sem("may_act")
        res_mean = sem("res_mean")
        res_squares = sem("res_squares")
        res_scale = sem("res_scale")
        res_step = sem("res_step")
        fin_h0 = sem("fin_h0")
        fin_half = sem("fin_half")
        fin_h1 = sem("fin_h1")
        fin_sum = sem("fin_sum")
        fin_mean = sem("fin_mean")
        fin_squares = sem("fin_squares")
        fin_scale = sem("fin_scale")
        fin_scaled = sem("fin_scaled")
        fin_act = sem("fin_act")
        fin_h2 = sem("fin_h2")
        fin_copied = sem("fin_copied")
        fin_rows = sem("fin_rows")
        fin_saved = sem("fin_saved")
        pool_steps = sem("pool_steps")
        dve_steps = sem("dve_steps")
        gathered = [sem(f"gathered{i}") for i in range(UNROLL * GROUP)]
        stored = [sem(f"stored{i}") for i in range(2)]
        ends = [sem(f"ends{k}") for k in range(BLOCKS)]

        def chunks(ap):
            return ap.rearrange("(c p) f -> p c f", p=P)

        def row(ap):
            return ap.rearrange("(a n) -> a n", a=1)

        def edges_2d(ap, lo, hi):
            return ap[lo * GE:hi * GE].rearrange("(q r) -> q r", r=GE)

        dst_i, prev_i, src_i = (view(big, i * GE, (GE,), I32)[0:GROUPS] for i in range(3))
        dst_f, src_f, head, cum, ones_e, seg = (view(big, (3 + i) * GE, (GE,))[0:GROUPS] for i in range(6))
        sign = view(big, 9 * GE, (GE,))[0:GROUPS]
        code_b = view(big, 10 * GE, (GE,), FP16)[0:GROUPS]
        rel = view(big, 11 * GE, (GE,))[0:GROUPS]
        head_seg = view(big, 12 * GE, (GE,))[0:GROUPS]
        seg_i = view(big, 13 * GE, (GE,), I32)[0:GROUPS]
        sm = 14 * GE
        base_i = view(big, sm, (GROUP,), I32)[0:GROUPS]
        base_h = view(big, sm + 8, (GROUP,), BF16)[0:GROUPS].bitcast(I16)
        base_f = view(big, sm + 16, (GROUP,))[0:GROUPS]
        seg_last = view(big, sm + 24, (2,), I32)[0:GROUPS]
        base_u = view(big, sm + 40, (GROUP,))[0:GROUPS]
        last_i = view(big, sm + 48, (1,), I32)[0:GROUPS]
        last_f, wide_q, wide_f = (view(big, sm + 56 + 8 * i, (1,))[0:GROUPS] for i in range(3))
        head_cols = view(big, sm + 80, (TILES,), I32)

        sort = rows_a[:, :, :].rearrange("p c d -> p (c d)")
        hot_hi = [view(sort, i * 200, (IT, HI), BF16) for i in range(2)]
        hot_lo = [view(sort, 400 + i * 256, (IT, LO), BF16) for i in range(2)]
        hot_src = [view(sort, 912 + i * 114, (IT + 1, CH), BF16) for i in range(2)]
        dst_hi = view(sort, 1140, (TILES,), BF16)
        dst_lo = view(sort, 1348, (TILES,), BF16)
        src_chunk = view(sort, 1556, (TILES,), BF16)
        c_sb, c_cum, c_end, c_none, ones_h = (view(sort, 1764 + i * LO, (LO,))[0:HI] for i in range(5))
        c_out = view(sort, 2084, (2, LO))[0:HI]
        c_last = view(sort, 3199, (1,), I32)[0:HI]
        cols_f = view(sort, 2212, (2, CH))
        zeros_b = view(sort, 2262, (2 * P,), BF16)
        before_b = view(sort, 2390, (P,), BF16)
        ones_b = view(sort, 2454, (P,), BF16)
        bk_count, bk_size, bk_cum, bk_end, bk_next, bk_diag = (view(sort, 2518 + i * 26, (CH,)) for i in range(6))
        bk_i = view(sort, 2674, (CH,), I32)
        ones_c = view(sort, 3174, (CH,))
        bk_col = view(sort, 2700, (1,))
        bk_past = view(sort, 2702, (SUM_TILES,), BF16)
        part_j = view(sort, 2702, (TILES,), I32)
        part_k = view(sort, 0, (TILES,))
        rk_prod = view(sort, 0, (IT, CH))
        rank_i, rank_p, rank_t = (view(sort, i * TILES, (TILES,), I32) for i in range(3))
        pl_tile = view(sort, 0, (2, PUT, SUM_TILES), FP16)
        pl_a = view(sort, 2 * SUM_TILES, (2, PUT, P), FP16)
        pl_b = view(sort, 2 * SUM_TILES + 2 * P, (2, PUT, P), FP16)
        pl_zero = view(sort, 2 * SUM_TILES + 4 * P, (SUM_TILES,), FP16)
        un_i, un_j = (view(sort, i * SUM_TILES, (SUM_TILES,), I32) for i in range(2))
        un_a, un_b, un_c = (view(sort, (2 + i) * SUM_TILES, (SUM_TILES,)) for i in range(3))
        un_perm, un_low = (view(sort, (5 + i) * SUM_TILES, (SUM_TILES,), I32) for i in range(2))

        fv1 = view(big, 0, (2, 2 * D))
        fv2 = view(big, 512, (2, D))
        fc1 = view(big, 768, (2,))
        fc2, fgamma, fbeta = (view(big, 776 + i * D, (D,)) for i in range(3))
        fin_xt = view(big, 1280, (NP,))
        agg = view(big, 1280 + NP, (NP,))
        fin_g = view(big, 1280 + 2 * NP, (2, NP))
        fin_y = view(big, 1280 + 4 * NP, (CH, D))
        fin_tmp = view(big, 1280 + 5 * NP, (CH, D))
        h_block = fin_y[:, CH - 4:CH, :]

        block = ctx.enter_context(nc.Block())

        @block.sync
        def _(sp):
            sp.wait_ge(x_cleared, 1)
            sp.dma_start(xres[:, 0:CH - 1, :], chunks(x[0:(CH - 1) * P, :])).then_inc(x_loaded, 16)
            sp.dma_start(xres[0:NLAST, CH - 1, :], x[(CH - 1) * P:N, :]).then_inc(x_loaded, 16)
            sp.wait_ge(ids_cleared, 1)
            sp.dma_start(dst_i[0:FULLROWS, :], edges_2d(dst, 0, FULLROWS)).then_inc(ids_loaded, 16)
            sp.dma_start(dst_i[FULLROWS:GROUPS, 0:TAIL], row(dst[FULLROWS * GE:E])).then_inc(ids_loaded, 16)
            sp.dma_start(prev_i[0:1, 1:GE], row(dst[0:GE - 1])).then_inc(ids_loaded, 16)
            sp.dma_start(prev_i[1:FULLROWS, :],
                         dst[GE - 1:FULLROWS * GE - 1].rearrange("(q r) -> q r", r=GE)).then_inc(ids_loaded, 16)
            sp.dma_start(prev_i[FULLROWS:GROUPS, 0:TAIL + 1],
                         row(dst[FULLROWS * GE - 1:E])).then_inc(ids_loaded, 16)
            sp.dma_start(src_i[0:FULLROWS, :], edges_2d(src, 0, FULLROWS)).then_inc(src_loaded, 16)
            sp.dma_start(src_i[FULLROWS:GROUPS, 0:TAIL], row(src[FULLROWS * GE:E])).then_inc(src_loaded, 16)
            for l in range(LAYERS):
                for ap, w in ((w_ab[:, l, 0:D], w1[l][0:D, :]), (w_ab[:, l, D:2 * D], w1[l][D:2 * D, :]),
                              (w2_sb[:, l, :], w2[l][:, :]), (b1_sb[:, l, :], b1[l].partition_broadcast(P)),
                              (b2_sb[:, l, :], b2[l].partition_broadcast(P))):
                    sp.dma_start(ap, w).then_inc(weights_loaded, 16)
            sp.wait_ge(codes_ready, 1)
            sp.dma_start(code_row.rearrange("(q r) -> q r", r=GE), code_b[:, :]).then_inc(codes_saved, 16)
            sp.dma_start(base_row.rearrange("(q r) -> q r", r=GROUP), base_h[:, :]).then_inc(codes_saved, 16)
            sp.dma_start(count_row.rearrange("(q r) -> q r", r=2), seg_last[:, :]).then_inc(codes_saved, 16)
            sp.wait_ge(codes_saved, 48)
            sp.dma_start(base_sb[:, :], row(base_row)).then_inc(codes_loaded, 16)
            sp.dma_start(counter[0:1, 0:2], row(count_row[2 * GROUPS - 2:2 * GROUPS])).then_inc(codes_loaded, 16)
            def save_b(l):
                for k in range(BLOCKS):
                    c, n = block_chunks(k)
                    sp.wait_ge(b_ready, BLOCKS * l + k + 1)
                    sp.dma_start(chunks(b_rows)[:, c:c + n, :], rows_b[:, c:c + n, :]).then_inc(b_saved, 16)

            save_b(0)
            sp.wait_ge(edge_cols_done, 1)
            sp.wait_ge(node_list_ready, 1)
            first, early = (UNROLL + 1) * GE, EARLY * UNROLL * GE
            sp.dma_start(codes[:, 0:first], code_row[0:first].partition_broadcast(P)).then_inc(codes_first, 16)
            sp.dma_start(codes[:, first:early], code_row[first:early].partition_broadcast(P)).then_inc(codes_loaded, 16)

            def load_codes(it):
                at = it * UNROLL * GE
                sp.wait_ge(codes_loaded, 32 + 16 * (it - EARLY + 1))
                sp.dma_start(codes[:, bass.ds(at, UNROLL * GE)],
                             code_row[bass.ds(at, UNROLL * GE)].partition_broadcast(P)).then_inc(codes_loaded, 16)

            def store(g, a, base):
                sp.wait_ge(out_copied, base + g + 1)
                sp.dma_start(max_rows[bass.ds(g * GE, GE), :].rearrange("(j p) f -> p j f", p=P),
                             outb[:, a, :, :]).then_inc(stored[a], 16)

            def save_pass(l):
                base = l * GROUPS

                def iteration(it, loads=False):
                    if loads:
                        load_codes(it + EARLY)
                    for u in range(UNROLL):
                        g = it * UNROLL + u
                        if not (isinstance(g, int) and g < 2):
                            store(g - 2, u % 2, base)

                def node_tables_out():
                    sp.wait_ge(tables_ready, 1)
                    sp.dma_start(node_cols.rearrange("k (h l) -> h k l", l=LO), c_out[:, :, :]).then_inc(tables_saved, 16)
                    ahead = AHEAD_BLOCKS * 4 * P // LO
                    sp.dma_start(counter[0:1, 2:3], c_last[ahead - 1:ahead, 0:1]).then_inc(tables_loaded, 16)
                    sp.wait_ge(tables_saved, 16)
                    with nc.allow_non_contiguous_dma(reason="3200 node words, once"):
                        for k in range(2):
                            sp.dma_start(cols_f[:, k, :], node_cols[k].rearrange("(c p) -> p c", p=P)).then_inc(tables_loaded, 16)

                iteration(0, l == 0)
                if l == 0:
                    with sp.Fori(1, ITER // 2) as it:
                        iteration(it, True)
                    node_tables_out()
                    with sp.Fori(ITER // 2, ITER - EARLY) as it:
                        iteration(it, True)
                    with sp.Fori(ITER - EARLY, ITER - 1) as it:
                        iteration(it)
                else:
                    with sp.Fori(1, ITER - 1) as it:
                        iteration(it)
                iteration(ITER - 1)
                store(GROUPS - 2, 0, base)
                store(GROUPS - 1, 1, base)

            for l in range(LAYERS):
                if l > 0:
                    save_b(l)
                save_pass(l)
            sp.wait_ge(scanned, LAYERS * GROUPS)
            sp.dma_start(fv1[:, :, :], v1.rearrange("(s p) n -> p s n", p=P)).then_inc(fin_w, 16)
            sp.dma_start(fv2[:, :, :], v2.rearrange("(s p) n -> p s n", p=P)).then_inc(fin_w, 16)
            with nc.allow_non_contiguous_dma(reason="256 words, once"):
                sp.dma_start(fc1[:, :], c1.rearrange("(m p) -> p m", p=P)).then_inc(fin_w, 16)
            for ap, v in ((fc2, c2), (fgamma, gamma), (fbeta, beta)):
                sp.dma_start(ap, v.partition_broadcast(P)).then_inc(fin_w, 16)
            for k in range(BLOCKS):
                c, n = block_chunks(k)
                sp.wait_ge(fin_rows, k + 1)
                if k < BLOCKS - 1:
                    sp.dma_start(chunks(out[c * P:(c + n) * P, :]), fin_y[:, c:c + n, :]).then_inc(fin_saved, 16)
                else:
                    sp.dma_start(out[c * P:N, :], fin_y[0:NLAST, c, :]).then_inc(fin_saved, 16)
            sp.wait_ge(fin_saved, 16 * BLOCKS)

        @block.gpsimd
        def _(pool):
            taken = [0]

            def step(ins):
                taken[0] += 1
                ins.then_inc(pool_steps, 1)
                pool.wait_ge(pool_steps, taken[0])

            step(nc.gpsimd.memset(ident[:, :], 0.0))
            step(nc.gpsimd.affine_select(out=ident[:, :], in_=ident[:, :], compare_op=ALU.not_equal, fill=1.0,
                                         base=0, pattern=[[-1, P]], channel_multiplier=1))
            step(nc.gpsimd.memset(before[:, :], 0.0))
            nc.gpsimd.affine_select(out=before[:, :], in_=before[:, :], compare_op=ALU.is_ge, fill=1.0,
                                    base=0, pattern=[[-1, P]], channel_multiplier=1).then_inc(consts, 1)
            nc.gpsimd.iota(place[:, :], pattern=[[P, 2]], base=1, channel_multiplier=1,
                           allow_small_or_imprecise_dtypes=True)
            nc.gpsimd.iota(iota[:, :], pattern=[[1, GE]], base=0, channel_multiplier=0,
                           allow_small_or_imprecise_dtypes=True).then_inc(consts, 1)

            pool.wait_ge(codes_loaded, 32)
            pool.wait_ge(edge_cols_done, 1)
            occurring = pool.value_load(counter[0:1, 0:1], min_val=0, max_val=NP)
            with pool.If(occurring != N):
                with nc.allow_non_contiguous_dma(reason="3200 words, only where nodes lack edges"):
                    pool.dma_start(chunks(seg_node), list_idx[:, :].unsqueeze(2)).then_inc(node_list, 16)
                pool.wait_ge(node_list, 16)
                with pool.Fori(0, TILES) as t:
                    nc.gpsimd.tensor_copy(list_at[:, 0:1], head_cols[:, bass.ds(t, 1)]).then_inc(list_copied, 1)
                    nc.gpsimd.tensor_copy(list_val[:, 0:1], dst_cols[:, bass.ds(t, 1)]).then_inc(list_copied, 1)
                    pool.wait_ge(list_copied, 2 * t + 2)
                    nc.gpsimd.sem_inc(may_gather, 1)
                    nc.gpsimd.indirect_dma_start(seg_node, bass.IndirectOffsetOnAxis(ap=list_at[:, 0:1], axis=0),
                                                 list_val[:, 0:1], None, bounds_check=NP - 1,
                                                 oob_is_err=False).then_inc(node_list, 16)
                    pool.wait_ge(node_list, 16 * t + 32)
                with nc.allow_non_contiguous_dma(reason="3200 words, only where nodes lack edges"):
                    pool.dma_start(list_idx[:, :].unsqueeze(2), chunks(seg_node)).then_inc(node_list, 16)
                pool.wait_ge(node_list, 16 * TILES + 32)
                nc.gpsimd.sem_inc(node_list_ready, 1)
            with pool.Else():
                nc.gpsimd.sem_inc(node_list_ready, 1)

            def compact_a(l):
                with pool.If(occurring != N):
                    pool.wait_ge(cast[2], BLOCKS * (l + 1))
                    pool.dma_start(chunks(a_rows), rows_a[:, :, :]).then_inc(a_saved, 16)
                    pool.wait_ge(a_saved, 16 * (l + 1))
                    for c in range(CH):
                        nc.gpsimd.indirect_dma_start(rows_a[:, c, :], None, a_rows,
                                                     bass.IndirectOffsetOnAxis(ap=list_idx[:, c:c + 1], axis=0),
                                                     bounds_check=NP - 1, oob_is_err=False).then_inc(a_gather, 16)
                    pool.wait_ge(a_gather, 16 * CH * (l + 1))
                    nc.gpsimd.sem_inc(compact, 1)
                with pool.Else():
                    nc.gpsimd.sem_inc(may_gather, 1)

            def gather_group(g, u, base, table):
                pool.wait_ge(idx_ready, base + g + 1)
                if some(base + g - UNROLL + 1):
                    pool.wait_ge(mixed_done, base + g - UNROLL + 1)
                nc.gpsimd.sem_inc(may_gather, 1)
                for j in range(GROUP):
                    nc.gpsimd.indirect_dma_start(
                        ring[u][:, j, :], None, table,
                        bass.IndirectOffsetOnAxis(ap=idx[:, u, j:j + 1], axis=0)).then_inc(gathered[u * GROUP + j], 16)

            def gather_ends(k, table, size):
                c0, n = block_chunks(k)
                for c in range(c0, c0 + n):
                    nc.gpsimd.indirect_dma_start(nodes[:, c, :], None, table,
                                                 bass.IndirectOffsetOnAxis(ap=end_dst[:, c:c + 1], axis=0),
                                                 bounds_check=size - 1, oob_is_err=False).then_inc(ends[k], 16)

            for l in range(LAYERS + 1):
                base = l * GROUPS
                if l < LAYERS:
                    compact_a(l)
                    pool.wait_ge(b_saved, 16 * BLOCKS * (l + 1))
                table = b_rows if l < LAYERS else attr
                for u in range(UNROLL):
                    if u == 2 and l < LAYERS:
                        pool.wait_ge(split_done, l + 1)
                    gather_group(u, u, base, table)
                with pool.Fori(1, ITER if l < LAYERS else SUM_ITER) as it:
                    for u in range(UNROLL):
                        gather_group(it * UNROLL + u, u, base, table)
                if l == LAYERS:
                    for g in range(SUM_ITER * UNROLL, SUM_GROUPS):
                        gather_group(g, g % UNROLL, base, table)
                    break
                if l == 0:
                    pool.wait_ge(nodes_cleared, 1)
                    pool.wait_ge(cols_ready, 1)
                    edges_ahead = pool.value_load(counter[0:1, 2:3], min_val=0, max_val=EP)
                early = (GROUPS - AHEAD) * GE
                with pool.If(edges_ahead <= early):
                    for a in range(2):
                        pool.wait_ge(stored[a], 16 * (GROUPS // 2 * (l + 1) - AHEAD // 2))
                    nc.gpsimd.sem_inc(may_gather, 1)
                    for k in range(AHEAD_BLOCKS):
                        gather_ends(k, max_rows[0:early, :], early)
                with pool.Else():
                    for a in range(2):
                        pool.wait_ge(stored[a], 16 * (GROUPS // 2) * (l + 1))
                    nc.gpsimd.sem_inc(may_gather, 1)
                    for k in range(AHEAD_BLOCKS):
                        gather_ends(k, max_rows, EP)
                for a in range(2):
                    pool.wait_ge(stored[a], 16 * (GROUPS // 2) * (l + 1))
                nc.gpsimd.sem_inc(may_gather, 1)
                for k in range(AHEAD_BLOCKS, BLOCKS):
                    gather_ends(k, max_rows, EP)

        @block.tensor
        def _(pe):
            pe.wait_ge(seg_totals, 1)
            pe.wait_ge(consts, 1)
            nc.tensor.matmul(banks[7][0:GROUPS, 0:1], before[0:GROUPS, 0:GROUPS], cum[:, GE - 1:GE],
                             start=True, stop=True).then_inc(seg_before, 1)
            flat_parts = a_parts[:, :, :, :].rearrange("p c k d -> p (c k d)")

            def edge_columns(bank, rows):
                for j in range(GROUP):
                    last = nc.tensor.transpose(bank[:, j * P:j * P + GROUPS], rows[:, j * P:(j + 1) * P],
                                               ident[0:GROUPS, 0:GROUPS])
                return last

            def node_tables(l):
                for k in range(BLOCKS + A_LAG[l]):
                    if k < BLOCKS:
                        pe.wait_ge(rows_ready, BLOCKS * l + k + 1)
                        if some(BLOCKS * l + k - 1):
                            pe.wait_ge(xt_ready, BLOCKS * l + k - 1)
                        c0, n = block_chunks(k)
                        for c in range(n):
                            last = nc.tensor.transpose(mixed[k % 2][:, c * P:(c + 1) * P], nodes[:, c0 + c, :], ident[:, :])
                        last.then_inc(rows_turned, 1)
                    if k == 0:
                        if l == 0:
                            pe.wait_ge(w_ready, 1)
                            pe.wait_ge(wide_groups, 1)
                            nc.tensor.matmul(banks[7][0:GROUPS, 8:9], ones_e[:, 0:GROUPS], wide_q[:, :],
                                             start=True, stop=True).then_inc(wide_sum, 1)
                        continue
                    if l == 0 and k == 3:
                        pe.wait_ge(codes_ready, 1)
                        pe.wait_ge(srcf_ready, 1)
                        edge_columns(sort_a, dst_f)
                        edge_columns(sort_b, src_f).then_inc(cols_turned, 1)
                    if l == 0 and k == 5:
                        pe.wait_ge(cols_copied, 1)
                        edge_columns(sort_a, head_seg).then_inc(cols_turned, 1)
                    if k <= BLOCKS:
                        pe.wait_ge(xt_ready, BLOCKS * l + k)
                    for b, to, at, done, used in ((k - 1, back, D, b_done, b_ready),
                                                  (k - A_LAG[l], hidden, 0, a_done, a_ready)):
                        if not 0 <= b < BLOCKS:
                            continue
                        c0, n = block_chunks(b)
                        if some(BLOCKS * l + b - 1):
                            pe.wait_ge(used, BLOCKS * l + b - 1)
                        for c in range(n):
                            last = nc.tensor.matmul(to[b % 2][:, c * D:(c + 1) * D], xt[:, (c0 + c) * P:(c0 + c + 1) * P],
                                                    w_ab[:, l, at:at + D], start=True, stop=True)
                        last.then_inc(done, 1)

            def mix(g, u, base, landed, bases):
                if some(base + g - 1):
                    pe.wait_ge(relu_done, base + g - 1)
                pe.wait_ge(hot_done, base + g + 1)
                for j in range(GROUP):
                    pe.wait_ge(gathered[u * GROUP + j], landed)
                    nc.tensor.matmul(mixed[u % 2][:, j * P:(j + 1) * P], ring[u][:, j, :], ident[:, :], is_transpose=True,
                                     start=(len(bases) > 1 or j == 0), stop=False)
                    if j >= GROUP - len(bases):
                        edges = slice(j * P, (j + 1) * P) if len(bases) > 1 else slice(0, GE)
                        first = bases[j if len(bases) > 1 else 0]
                        for k in range(2):
                            for part in range(3):
                                at = (first + k) * (3 * D) + part * D
                                last = nc.tensor.matmul(mixed[u % 2][:, edges], flat_parts[:, bass.ds(at, D)],
                                                        onehot[u % 2][:, k, edges], start=False,
                                                        stop=(k == 1 and part == 2))
                last.then_inc(mixed_done, 1)

            def second(g, a, base, l):
                pe.wait_ge(relu_done, base + g + 1)
                if some(base + g - 1):
                    pe.wait_ge(scanned, base + g - 1)
                nc.tensor.matmul(hidden[a][:, :], w2_sb[:, l, :], hin[:, a, :], start=True, stop=True).then_inc(hidden_done, 1)

            def turn_back(g, a, base):
                pe.wait_ge(scanned, base + g + 1)
                if some(base + g - 1):
                    pe.wait_ge(out_copied, base + g - 1)
                for j in range(GROUP):
                    last = nc.tensor.transpose(back[a][:, j * P:(j + 1) * P], run[:, a, j * P:(j + 1) * P], ident[:, :])
                last.then_inc(backed, 1)

            def count_edges(r, a):
                pe.wait_ge(hist_hot, r + 1)
                for j in range(IT):
                    nc.tensor.matmul(sort_a[0:HI, 0:LO], hot_hi[a][:, j, :], hot_lo[a][:, j, :],
                                     start=False, stop=False, skip_group_check=True)
                nc.tensor.matmul(sort_b[:, 0:IT * CH].rearrange("p (t c) -> p t c", c=CH), ones_b[:, :],
                                 hot_src[a][:, 0:IT, :], start=False, stop=False, skip_group_check=True).then_inc(hist_used, 1)

            def tables():
                nc.tensor.matmul(sort_a[0:HI, 0:LO], zeros_b[:, 0:HI], zeros_b[:, 0:LO], start=False, stop=True)
                nc.tensor.matmul(sort_b[:, 0:IT * CH], zeros_b[:, 0:P], zeros_b[:, 0:IT * CH], start=False,
                                 stop=True).then_inc(hist_done, 1)
                pe.wait_ge(hist_rows, 1)
                nc.tensor.matmul(sort_a[0:HI, P:P + 1], before[0:HI, 0:HI], c_cum[:, LO - 1:LO],
                                 start=True, stop=True).then_inc(hist_base, 1)
                pe.wait_ge(ends_hot, 1)
                nc.tensor.matmul(sort_b[:, 0:SUM_TILES], ones_b[0:CH, :], bk_past[0:CH, :],
                                 start=True, stop=True).then_inc(buckets_found, 1)

            def rank_counts(r, a):
                pe.wait_ge(rk_hot, r + 1)
                if some(r - 1):
                    pe.wait_ge(rk_read, r - 1)
                bank = (sort_a, sort_b)[a][:, 0:(IT + 1) * CH].rearrange("p (t c) -> p t c", c=CH)
                nc.tensor.matmul(bank[:, :, :], before_b[:, :], hot_src[a][:, :, :], start=True, stop=False)
                for t in range(IT):
                    last = nc.tensor.matmul(bank[:, t + 1:IT + 1, :], ones_b[:, :],
                                            hot_src[a][:, t:t + 1, :].to_broadcast((P, IT - t, CH)),
                                            start=False, stop=(t == IT - 1))
                last.then_inc(rk_prefix, 1)

            def put(s, a):
                pe.wait_ge(pl_ready, s + 1)
                for j in range(PUT):
                    nc.tensor.matmul(sort_a[:, 0:SUM_TILES], pl_a[:, a, j, :], pl_tile[:, a, j, :], start=False, stop=False,
                                     skip_group_check=True)
                    last = nc.tensor.matmul(sort_b[:, 0:SUM_TILES], pl_b[:, a, j, :], pl_tile[:, a, j, :], start=False,
                                            stop=False, skip_group_check=True)
                last.then_inc(pl_used, 1)

            def edge_pass(l, wide=False):
                base = l * GROUPS

                def iteration(it, counting=False):
                    for u in range(UNROLL):
                        g = it * UNROLL + u
                        if wide and u % 2 == 0:
                            _, firsts = nc.values_load_multi_w_load_instructions(
                                base_sb[0:1, bass.ds(g * GROUP, 2 * GROUP)], engines=[mybir.EngineType.PE],
                                min_val=0, max_val=CH - 1)
                        if not wide and u == 0:
                            _, firsts = nc.values_load_multi_w_load_instructions(
                                base_sb[0:1, bass.ds(g * GROUP, UNROLL, GROUP)], engines=[mybir.EngineType.PE],
                                min_val=0, max_val=CH - 1)
                        bases = firsts[u % 2 * GROUP:(u % 2 + 1) * GROUP] if wide else firsts[u:u + 1]
                        mix(g, u, base, 16 * ITER * l + it * 16 + 16, bases)
                        if not (isinstance(g, int) and g < 1):
                            second(g - 1, 1 - u % 2, base, l)
                            if counting:
                                count_edges(g - 1, 1 - u % 2)
                            elif l == 0 and not (isinstance(g, int) and g <= ROUNDS):
                                rank_counts(g - ROUNDS - 1, 1 - u % 2)
                            elif l > 0:
                                put((l - 1) * GROUPS + g - 1, 1 - u % 2)
                        if not (isinstance(g, int) and g < 2):
                            turn_back(g - 2, u % 2, base)

                if l == 0:
                    pe.wait_ge(hist_zero, 1)
                    nc.tensor.matmul(sort_a[0:HI, 0:LO], zeros_b[:, 0:HI], zeros_b[:, 0:LO], start=True, stop=False)
                    nc.tensor.matmul(sort_b[:, 0:IT * CH], zeros_b[:, 0:P], zeros_b[:, 0:IT * CH], start=True, stop=False)
                    iteration(0, True)
                    with pe.Fori(1, ITER // 2) as it:
                        iteration(it, True)
                    count_edges(ROUNDS - 1, 1)
                    tables()
                    iteration(ITER // 2)
                    with pe.Fori(ITER // 2 + 1, ITER - 1) as it:
                        iteration(it)
                else:
                    if l == 1:
                        pe.wait_ge(pl_zeroed, 1)
                        for bank in (sort_a, sort_b):
                            nc.tensor.matmul(bank[:, 0:SUM_TILES], pl_zero[:, 0:P], pl_zero[:, :], start=True, stop=False)
                    iteration(0)
                    with pe.Fori(1, ITER - 1) as it:
                        iteration(it)
                iteration(ITER - 1)
                second(GROUPS - 1, 1, base, l)
                turn_back(GROUPS - 2, 0, base)
                if l == 0:
                    rank_counts(ROUNDS - 1, 1)
                else:
                    put(l * GROUPS - 1, 1)
                if l == 2:
                    pe.wait_ge(pl_zeroed, 2)
                    for bank in (sort_a, sort_b):
                        last = nc.tensor.matmul(bank[:, 0:SUM_TILES], pl_zero[:, 0:P], pl_zero[:, :], start=False, stop=True)
                    last.then_inc(pl_used, 1)
                turn_back(GROUPS - 1, 1, base)

            def add_up(g, u, landed):
                pe.wait_ge(sum_hot, g + 1)
                if some(g - 1):
                    pe.wait_ge(agg_added, GROUP * (g - 1))
                for j in range(GROUP):
                    pe.wait_ge(gathered[u * GROUP + j], landed)
                    last = nc.tensor.matmul(mixed[u % 2][:, j * P:(j + 1) * P], ring[u][:, j, :], hot_sum[:, u % 2, j, :],
                                            start=True, stop=True)
                last.then_inc(mixed_done, 1)

            def first_half(k, n):
                pe.wait_ge(ln_done, k + 1)
                for c in range(n):
                    last = nc.tensor.transpose(hidden[0][:, c * P:(c + 1) * P], h_block[:, c, :], ident[:, :])
                last.then_inc(fin_turned, 1)
                pe.wait_ge(fin_t, k + 1)
                for m in range(2):
                    nc.tensor.matmul(back[m][:, 0:n * P], fv1[:, 0, m * P:(m + 1) * P], fin_xt[:, bass.ds(4 * k * P, n * P)],
                                     start=True, stop=True).then_inc(fin_h0, 1)
                pe.wait_ge(fin_half, 2 * k + 2)

            def sum_pass():
                def iteration(it, block_size=0):
                    for u in range(UNROLL):
                        add_up(it * UNROLL + u, u, 16 * ITER * LAYERS + it * 16 + 16)
                    if block_size:
                        first_half(it - 1, block_size)

                iteration(0)
                pe.wait_ge(fin_w, 96)
                pe.wait_ge(out_copied, LAYERS * GROUPS)
                with pe.Fori(1, NB4 + 1) as it:
                    iteration(it, 4)
                iteration(NB4 + 1, CH - 4 * NB4)
                with pe.Fori(NB4 + 2, SUM_ITER) as it:
                    iteration(it)
                for g in range(SUM_ITER * UNROLL, SUM_GROUPS):
                    add_up(g, g % UNROLL, 16 * ITER * LAYERS + SUM_ITER * 16 + 16)

            for l in range(LAYERS):
                node_tables(l)
                pe.wait_ge(split_done, l + 1)
                pe.wait_ge(codes_loaded, 32)
                if l == 0:
                    wide = pe.value_load(counter[0:1, 1:2], min_val=0, max_val=1)
                with pe.If(wide != 0):
                    edge_pass(l, True)
                with pe.Else():
                    edge_pass(l)
            sum_pass()

            pe.wait_ge(agg_added, GROUP * SUM_GROUPS)
            pe.wait_ge(fin_half, 2 * BLOCKS)

            def tail_first(k):
                c0, n = block_chunks(k)
                for m in range(2):
                    at = 2 * k + m
                    if some(at - 3):
                        pe.wait_ge(fin_sum, at - 3)
                    nc.tensor.matmul((mixed + hidden)[at % 4][:, 0:n * P], fv1[:, 1, m * P:(m + 1) * P],
                                     agg[:, c0 * P:(c0 + n) * P], start=True, stop=True).then_inc(fin_h1, 1)

            def tail_second(k):
                pe.wait_ge(fin_act, 2 * k + 2)
                if some(k - 1):
                    pe.wait_ge(fin_copied, k - 1)
                c0, n = block_chunks(k)
                for c in range(n):
                    for m in range(2):
                        last = nc.tensor.matmul(back[k % 2][:, c * D:(c + 1) * D],
                                                fin_g[:, m, (c0 + c) * P:(c0 + c + 1) * P], fv2[:, m, :],
                                                start=(m == 0), stop=(m == 1))
                last.then_inc(fin_h2, 1)

            for k in range(BLOCKS):
                tail_first(k)
                if k >= 1:
                    tail_second(k - 1)
            tail_second(BLOCKS - 1)

        @block.scalar
        def _(act):
            def root(n):
                act.wait_ge(ln_var, n)
                nc.scalar.sqrt(stat[:, 1, :], stat[:, 0, :]).then_inc(ln_std, 1)

            def spot(g, a, base):
                if some(base + g - 1):
                    act.wait_ge(hot_done, base + g - 1)
                nc.scalar.activation(spots[:, a, :], codes[:, bass.ds(g * GE, GE)], ACT.Abs).then_inc(spots_ready, 1)

            def relu(g, a, base):
                act.wait_ge(mixed_done, base + g + 1)
                if some(base + g - 1):
                    act.wait_ge(hidden_done, base + g - 1)
                nc.scalar.activation(hin[:, a, :], mixed[a][:, :], ACT.Relu).then_inc(relu_done, 1)

            def indices(g, u, cols):
                nc.scalar.copy(idx[:, u, :], cols[:, bass.ds(g * GROUP, GROUP)]).then_inc(idx_ready, 1)

            def copy_out(g, a, base):
                act.wait_ge(backed, base + g + 1)
                nc.scalar.copy(outb[:, a, :, :].rearrange("p j d -> p (j d)"), back[a][:, :]).then_inc(out_copied, 1)

            def edge_pass(l):
                base = l * GROUPS

                def iteration(it, last=False):
                    if l == 0 and not (isinstance(it, int) and it < EARLY - 1):
                        act.wait_ge(codes_loaded, 32 + 16 * (CODE_LOADS if last else it + 2 - EARLY + 1))
                    for u in range(UNROLL):
                        g = it * UNROLL + u
                        if not (last and u == UNROLL - 1):
                            spot(g + 1, 1 - u % 2, base)
                        relu(g, u % 2, base)
                        if not last:
                            indices(g + UNROLL, u, src_cols)
                        if not (isinstance(g, int) and g < 2):
                            before_g = GROUPS // 2 * l + it * 2 + u // 2 - 1
                            if some(before_g):
                                act.wait_ge(stored[u % 2], 16 * before_g)
                            copy_out(g - 2, u % 2, base)

                spot(0, 0, base)
                iteration(0)
                act.wait_ge(codes_loaded, 48)
                with act.Fori(1, ITER - 1) as it:
                    iteration(it)
                iteration(ITER - 1, True)
                for a in range(2):
                    act.wait_ge(stored[a], 16 * (GROUPS // 2 * (l + 1) - 1))
                    copy_out(GROUPS - 2 + a, a, base)

            def sum_indices(g, u):
                act.wait_ge(mixed_done, LAYERS * GROUPS + g + 1)
                indices(g + UNROLL, u, perm_cols)

            for k in range(BLOCKS):
                c0, n = block_chunks(k)
                act.wait_ge(x_mean, k + 1)
                for c in range(c0, c0 + n):
                    last = nc.scalar.activation(rows_a[:, c, :], xres[:, c, :], ACT.Square, bias=stat[:, 3, c:c + 1],
                                                accum_out=stat[:, 2, c:c + 1])
            last.then_inc(x_squares, 1)
            root(1)
            act.wait_ge(x_scale, 1)

            def first_rows(k):
                c0, n = block_chunks(k)
                for c in range(c0, c0 + n):
                    last = nc.scalar.activation(nodes[:, c, :], xres[:, c, :], ACT.Relu, scale=stat[:, 2, c:c + 1],
                                                bias=stat[:, 3, c:c + 1])
                last.then_inc(rows_ready, 1)

            first_rows(0)
            for l in range(LAYERS):
                for k in range(BLOCKS + A_LAG[l] + 4):
                    if l == 0 and k + 1 < BLOCKS:
                        first_rows(k + 1)
                    if k < BLOCKS:
                        c0, n = block_chunks(k)
                        act.wait_ge(rows_turned, BLOCKS * l + k + 1)
                        nc.scalar.copy(xt[:, c0 * P:(c0 + n) * P], mixed[k % 2][:, 0:n * P]).then_inc(xt_ready, 1)
                    if 1 <= k <= BLOCKS:
                        c0, n = block_chunks(k - 1)
                        act.wait_ge(b_done, BLOCKS * l + k)
                        nc.scalar.copy(rows_b[:, c0:c0 + n, :],
                                       back[(k - 1) % 2][:, 0:n * D].rearrange("p (c d) -> p c d", d=D)).then_inc(b_ready, 1)
                    if l == 0 and k == BLOCKS:
                        act.wait_ge(cols_copied, 1)
                        for u in range(UNROLL):
                            indices(u, u, src_cols)
                    for part, (whole, ready) in enumerate(((rows_a, a_ready), (rest, left[0]), (rest, left[1]))):
                        b = k - A_LAG[l] - 2 - part
                        if 0 <= b < BLOCKS:
                            c0, n = block_chunks(b)
                            act.wait_ge(ready, BLOCKS * l + b + 1)
                            nc.scalar.copy(a_parts[:, c0:c0 + n, part, :], whole[:, c0:c0 + n, :]).then_inc(cast[part], 1)
                act.wait_ge(codes_first, 16)
                act.wait_ge(split_done, l + 1)
                act.wait_ge(b_saved, 16 * BLOCKS * (l + 1))
                edge_pass(l)
                if l < LAYERS - 1:
                    for u in range(UNROLL):
                        indices(u, u, src_cols)
            act.wait_ge(perm_ready, 1)
            for u in range(UNROLL):
                indices(u, u, perm_cols)
            def sum_iteration(it, n=0):
                k = it - 1
                for u in range(UNROLL):
                    sum_indices(it * UNROLL + u, u)
                    if n and u == 0:
                        act.wait_ge(res_mean, k + 1)
                        nc.scalar.sem_inc(may_act, 1)
                        for c in range(n):
                            at = bass.ds(4 * k + c, 1)
                            last = nc.scalar.activation(fin_tmp[:, c, :], xres[:, at, :], ACT.Square,
                                                        bias=stat[:, 3, at], accum_out=stat[:, 2, at])
                        last.then_inc(res_squares, 1)
                    if n and u == 1:
                        act.wait_ge(ln_var, 2 + k)
                        nc.scalar.sem_inc(may_act, 1)
                        at = bass.ds(4 * k, n)
                        nc.scalar.sqrt(stat[:, 1, at], stat[:, 0, at]).then_inc(ln_std, 1)
                    if n and u == 2:
                        act.wait_ge(res_scale, k + 1)
                        nc.scalar.sem_inc(may_act, 1)
                        for c in range(n):
                            at = bass.ds(4 * k + c, 1)
                            last = nc.scalar.activation(h_block[:, c, :], xres[:, at, :], ACT.Relu, scale=stat[:, 2, at],
                                                        bias=stat[:, 3, at])
                        last.then_inc(ln_done, 1)
                    if n and u == 3:
                        act.wait_ge(fin_turned, k + 1)
                        at = bass.ds(4 * k * P, n * P)
                        nc.scalar.copy(fin_xt[:, at], hidden[0][:, 0:n * P]).then_inc(fin_t, 1)
                        for m in range(2):
                            act.wait_ge(fin_h0, 2 * k + m + 1)
                            nc.scalar.sem_inc(may_act, 1)
                            nc.scalar.activation(fin_g[:, m, at], back[m][:, 0:n * P], ACT.Identity,
                                                 bias=fc1[:, m:m + 1]).then_inc(fin_half, 1)

            sum_iteration(0)
            with act.Fori(1, NB4 + 1) as it:
                sum_iteration(it, 4)
            sum_iteration(NB4 + 1, CH - 4 * NB4)
            with act.Fori(NB4 + 2, SUM_ITER - 1) as it:
                sum_iteration(it)
            for g in range((SUM_ITER - 1) * UNROLL, SUM_GROUPS - UNROLL):
                sum_indices(g, g % UNROLL)
            for k in range(BLOCKS + 1):
                if k < BLOCKS:
                    c0, n = block_chunks(k)
                    for m in range(2):
                        act.wait_ge(fin_sum, 2 * k + m + 1)
                        nc.scalar.activation(fin_g[:, m, c0 * P:(c0 + n) * P], fin_g[:, m, c0 * P:(c0 + n) * P],
                                             ACT.Silu).then_inc(fin_act, 1)
                if k >= 1:
                    c0, n = block_chunks(k - 1)
                    act.wait_ge(fin_mean, k)
                    for c in range(c0, c0 + n):
                        last = nc.scalar.activation(fin_tmp[:, c, :], fin_y[:, c, :], ACT.Square,
                                                    bias=stat[:, 3, c:c + 1], accum_out=stat[:, 2, c:c + 1])
                    last.then_inc(fin_squares, 1)
            root(2 + BLOCKS)
            act.wait_ge(fin_scale, 1)
            for k in range(BLOCKS):
                c0, n = block_chunks(k)
                for c in range(c0, c0 + n):
                    last = nc.scalar.activation(fin_y[:, c, :], fin_y[:, c, :], ACT.Identity, scale=stat[:, 2, c:c + 1],
                                                bias=stat[:, 3, c:c + 1])
                last.then_inc(fin_scaled, 1)

        @block.vector
        def _(dve):
            taken = [0]
            v = nc.vector

            def step(ins):
                taken[0] += 1
                ins.then_inc(dve_steps, 1)
                dve.wait_ge(dve_steps, taken[0])

            def spread(col, n=CH):
                return col.unsqueeze(2).to_broadcast((P, n, D))

            def along(vec, n=CH):
                return vec.unsqueeze(1).to_broadcast((P, n, D))

            v.memset(xres[:, CH - 1, :], 0.0).then_inc(x_cleared, 1)
            v.memset(prev_i[:, :], N).then_inc(clears, 1)
            v.memset(dst_i[:, :], N)
            v.memset(src_i[:, :], N)
            dve.wait_ge(clears, 1)
            v.memset(prev_i[0:1, 0:1], -1).then_inc(ids_cleared, 1)
            v.memset(list_idx[:, :], SKIP)
            v.memset(a_parts[:, CH, :, :], 0.0)
            v.memset(first_state[:, :], 0.0)
            step(v.memset(ones_e[:, :], 1.0))

            dve.wait_ge(x_loaded, 32)
            for k in range(BLOCKS):
                c, n = block_chunks(k)
                step(v.tensor_reduce(stat[:, 2, c:c + n], xres[:, c:c + n, :], AX_X, ALU.add))
                v.tensor_scalar(stat[:, 3, c:c + n], stat[:, 2, c:c + n], -1.0 / D, None, ALU.mult).then_inc(x_mean, 1)

            dve.wait_ge(ids_loaded, 16 * 5)
            step(v.tensor_tensor(head[:, :], dst_i[:, :], prev_i[:, :], ALU.not_equal))
            v.tensor_copy(dst_f[:, :], dst_i[:, :])
            v.tensor_tensor_scan(cum[:, :], ones_e[:, :], head[:, :], 0.0, ALU.mult, ALU.add).then_inc(seg_totals, 1)
            v.tensor_scalar(sign[:, :], head[:, :], -2.0, 1.0, ALU.mult, ALU.add)
            dve.wait_ge(seg_totals, 1)
            step(v.tensor_scalar(rel[:, :], head[:, :], -float(SKIP), float(SKIP - 1), ALU.mult, ALU.add))
            dve.wait_ge(weights_loaded, 16 * 5 * LAYERS)
            v.tensor_tensor(w_ab[:, :, 0:D], w_ab[:, :, 0:D], w_ab[:, :, D:2 * D], ALU.subtract).then_inc(w_ready, 1)
            dve.wait_ge(x_squares, 1)
            v.tensor_scalar(stat[:, 0, :], stat[:, 2, :], 1.0 / D, EPS, ALU.mult, ALU.add).then_inc(ln_var, 1)
            dve.wait_ge(ln_std, 1)
            step(v.reciprocal(stat[:, 2, :], stat[:, 1, :]))
            v.tensor_tensor(stat[:, 3, :], stat[:, 3, :], stat[:, 2, :], ALU.mult).then_inc(x_scale, 1)
            dve.wait_ge(seg_before, 1)
            step(v.tensor_scalar(seg[:, :], cum[:, :], banks[7][0:GROUPS, 0:1], None, ALU.add))
            step(v.tensor_tensor(head_seg[:, :], seg[:, :], rel[:, :], ALU.add))
            step(v.tensor_scalar(seg[:, :], seg[:, :], -1.0, None, ALU.add))
            step(v.tensor_copy(seg_i[:, :], seg[:, :]))
            v.tensor_copy(seg_last[:, 0:1], seg_i[:, GE - 1:GE])
            v.tensor_scalar(last_i[:, :], seg_i[:, GE - 1:GE], 7, None, ALU.logical_shift_right)
            step(v.tensor_scalar(base_i[:, :], seg_i[:, 0:GE:P], 7, None, ALU.logical_shift_right))
            v.tensor_copy(last_f[:, :], last_i[:, :])
            step(v.tensor_copy(base_f[:, :], base_i[:, :]))
            v.tensor_scalar(wide_q[:, :], last_f[:, :], base_f[:, 0:1], 1.5, ALU.subtract, ALU.is_gt).then_inc(wide_groups, 1)
            dve.wait_ge(wide_sum, 1)
            step(v.tensor_scalar(wide_f[:, :], banks[7][0:GROUPS, 8:9], 0.5, None, ALU.is_gt))
            v.tensor_copy(seg_last[:, 1:2], wide_f[:, :])
            step(v.tensor_scalar(base_u[:, :], base_f[:, :], base_f[:, 0:1], wide_f[:, 0:1], ALU.subtract, ALU.mult))
            step(v.tensor_scalar(base_u[:, :], base_u[:, :], base_f[:, 0:1], None, ALU.add))
            v.tensor_copy(base_h[:, :], base_u[:, :])
            step(v.tensor_scalar(base_f[:, :], base_u[:, :], float(P), -1.0, ALU.mult, ALU.add))
            tiles = lambda ap: ap.rearrange("q (j r) -> q j r", r=P)
            step(v.tensor_tensor(tiles(rel[:, :]), tiles(seg[:, :]), base_f[:, :].unsqueeze(2).to_broadcast((GROUPS, GROUP, P)),
                                 ALU.subtract))
            v.tensor_tensor(code_b[:, :], rel[:, :], sign[:, :], ALU.mult).then_inc(codes_ready, 1)
            dve.wait_ge(src_loaded, 32)
            v.tensor_copy(src_f[:, :], src_i[:, :]).then_inc(srcf_ready, 1)

            def copy_columns(bank, cols):
                return v.tensor_copy(cols[:, 0:TILES].rearrange("p (q j) -> p j q", j=GROUP),
                                     bank[:, :].rearrange("p (j q) -> p j q", j=GROUP)[:, :, 0:GROUPS])

            def split(k):
                c, n = block_chunks(k)
                a, left, parts = rows_a[:, c:c + n, :], rest[:, c:c + n, :], a_parts[:, c:c + n]
                step(v.tensor_copy(parts[:, :, 0, :], a))
                step(v.tensor_tensor(left, a, parts[:, :, 0, :], ALU.subtract))
                step(v.tensor_copy(parts[:, :, 1, :], left))
                step(v.tensor_tensor(left, left, parts[:, :, 1, :], ALU.subtract))
                return v.tensor_copy(parts[:, :, 2, :], left)

            def node_rows(l, k):
                c, n = block_chunks(k)
                rows = nodes[:, c:c + n, :]
                dve.wait_ge(ends[k], 16 * n * l)
                step(v.tensor_tensor(rows, rows, along(b2_sb[:, l - 1, :], n), ALU.add))
                v.scalar_tensor_tensor(rows, rows, 0.0, spread(present[:, c:c + n], n),
                                       ALU.max, ALU.mult).then_inc(rows_ready, 1)

            def hot(g, a, base):
                if some(base + g - 1):
                    dve.wait_ge(mixed_done, base + g - 1)
                dve.wait_ge(spots_ready, base + g + 1)
                for k in range(2):
                    last = v.tensor_scalar(onehot[a][:, k, :], spots[:, a, :], place[:, k:k + 1], None, ALU.is_equal)
                last.then_inc(hot_done, 1)

            def mark(g, a, base):
                if some(base + g - 1):
                    dve.wait_ge(scanned, base + g - 1)
                v.tensor_scalar(mask[:, a, :], codes[:, bass.ds(g * GE, GE)], 0.0, -HUGE, ALU.is_lt,
                                ALU.mult).then_inc(mask_ready, 1)

            def scan(g, a, base):
                dve.wait_ge(hidden_done, base + g + 1)
                if some(base + g - 1):
                    dve.wait_ge(backed, base + g - 1)
                if some(base + g):
                    dve.wait_ge(scanned, base + g)
                state = first_state[:, :] if isinstance(g, int) and g == 0 else run[:, 1 - a, GE - 1:GE]
                dve.wait_ge(mask_ready, base + g + 1)
                v.tensor_tensor_scan(run[:, a, :], mask[:, a, :], hidden[a][:, :], state,
                                     ALU.add, ALU.max).then_inc(scanned, 1)

            def one_hot(to, cols, r, width):
                return v.tensor_tensor(to, cols[:, bass.ds(r * IT, IT)].unsqueeze(2).to_broadcast((P, IT, width)),
                                       iota[:, 0:width].unsqueeze(1).to_broadcast((P, IT, width)), ALU.is_equal)

            def count_edges(r, a):
                if some(r - 1):
                    dve.wait_ge(hist_used, r - 1)
                one_hot(hot_hi[a][:, :, :], dst_hi, r, HI)
                one_hot(hot_lo[a][:, :, :], dst_lo, r, LO)
                one_hot(hot_src[a][:, 0:IT, :], src_chunk, r, CH).then_inc(hist_hot, 1)

            def tables():
                dve.wait_ge(hist_done, 1)
                v.tensor_reduce(bk_count[:, :], sort_b[:, 0:IT * CH].rearrange("p (t c) -> p c t", c=CH), AX_X, ALU.add)
                step(v.tensor_copy(c_sb[:, :], sort_a[0:HI, 0:LO]))
                v.tensor_tensor_scan(c_cum[:, :], ones_h[:, :], c_sb[:, :], 0.0, ALU.mult, ALU.add).then_inc(hist_rows, 1)
                v.tensor_scalar(c_out[:, 1, :], c_sb[:, :], 0.0, None, ALU.is_gt)
                step(v.tensor_scalar(c_none[:, :], c_sb[:, :], 0.0, float(SKIP), ALU.is_equal, ALU.mult))
                dve.wait_ge(hist_base, 1)
                dve.wait_ge(hist_rows, 1)
                step(v.tensor_scalar(c_end[:, :], c_cum[:, :], sort_a[0:HI, P:P + 1], None, ALU.add))
                v.tensor_copy(c_last[:, :], c_end[:, LO - 1:LO])
                v.scalar_tensor_tensor(c_out[:, 0, :], c_end[:, :], -1.0, c_none[:, :], ALU.add, ALU.add).then_inc(tables_ready, 1)
                step(v.tensor_scalar(bk_count[:, :], bk_count[:, :], float(P - 1), None, ALU.add))
                step(v.tensor_copy(bk_i[:, :], bk_count[:, :]))
                step(v.tensor_scalar(bk_i[:, :], bk_i[:, :], 7, None, ALU.logical_shift_right))
                step(v.tensor_copy(bk_size[:, :], bk_i[:, :]))
                step(v.tensor_tensor_scan(bk_end[:, :], ones_c[:, :], bk_size[:, :], 0.0, ALU.mult, ALU.add))
                step(v.tensor_tensor(bk_next[:, :], bk_end[:, :], bk_size[:, :], ALU.subtract))
                step(v.tensor_scalar(bk_next[:, :], bk_next[:, :], float(P), None, ALU.mult))
                step(v.tensor_tensor(bk_diag[:, :], bk_end[:, :], ident[:, 0:CH], ALU.mult))
                step(v.tensor_reduce(bk_col[:, :], bk_diag[:, :], AX_X, ALU.add))
                v.tensor_scalar(bk_past[:, :], iota[:, 0:SUM_TILES], bk_col[:, 0:1], None, ALU.is_ge).then_inc(ends_hot, 1)
                dve.wait_ge(buckets_found, 1)
                step(v.tensor_scalar(bucket_sb[:, :], sort_b[0:1, 0:SUM_TILES], float(CH - 1), None, ALU.min))

            def node_columns():
                v.memset(nodes[:, :, :], 0.0).then_inc(nodes_cleared, 1)
                dve.wait_ge(tables_loaded, 48)
                v.tensor_copy(end_dst[:, :], cols_f[:, 0, :])
                v.tensor_copy(present[:, :], cols_f[:, 1, :]).then_inc(cols_ready, 1)

            def rank_hot(r, a):
                if some(r - 1):
                    dve.wait_ge(rk_step, 3 * (r - 1) - 1)
                one_hot(hot_src[a][:, 0:IT, :], src_chunk, r, CH).then_inc(rk_hot, 1)

            def rank_end(r, a):
                bank = (sort_a, sort_b)[a][:, 0:(IT + 1) * CH].rearrange("p (t c) -> p t c", c=CH)
                dve.wait_ge(rk_prefix, r + 1)
                if some(r):
                    dve.wait_ge(rk_read, r)
                    dve.wait_ge(rk_step, 3 * r)
                v.tensor_tensor(rk_prod[:, :, :], bank[:, 0:IT, :],
                                bk_next[:, :].unsqueeze(1).to_broadcast((P, IT, CH)), ALU.add).then_inc(rk_step, 1)
                dve.wait_ge(rk_step, 3 * r + 1)
                v.tensor_tensor(bk_next[:, :], bk_next[:, :], bank[:, IT, :], ALU.add).then_inc(rk_read, 1)
                v.tensor_tensor(rk_prod[:, :, :], rk_prod[:, :, :], hot_src[a][:, 0:IT, :], ALU.mult).then_inc(rk_step, 1)
                dve.wait_ge(rk_step, 3 * r + 2)
                v.tensor_reduce(rank_f[:, bass.ds(r * IT, IT)], rk_prod[:, :, :], AX_X, ALU.add).then_inc(rk_step, 1)

            def put(s, a):
                if some(s - 1):
                    dve.wait_ge(pl_used, s - 1)
                for j in range(PUT):
                    t = s * PUT + j
                    p_at, t_at = rank_pt[:, bass.ds(t, 1)], rank_pt[:, bass.ds(t + TILES, 1)]
                    v.tensor_scalar(pl_a[:, a, j, :], iota[:, 0:P], p_at, pack_a[:, bass.ds(t, 1)], ALU.is_equal, ALU.mult)
                    v.tensor_scalar(pl_b[:, a, j, :], iota[:, 0:P], p_at, pack_b[:, bass.ds(t, 1)], ALU.is_equal, ALU.mult)
                    last = v.tensor_scalar(pl_tile[:, a, j, :], iota[:, 0:SUM_TILES], t_at, None, ALU.is_equal)
                last.then_inc(pl_ready, 1)

            def edge_pass(l):
                base = l * GROUPS

                def iteration(it, counting=False, final=False):
                    if l == 0 and not (isinstance(it, int) and it < EARLY - 1):
                        dve.wait_ge(codes_loaded, 32 + 16 * (CODE_LOADS if final else it + 2 - EARLY + 1))
                    for u in range(UNROLL):
                        g = it * UNROLL + u
                        if not (final and u == UNROLL - 1):
                            hot(g + 1, 1 - u % 2, base)
                        if counting:
                            count_edges(g, u % 2)
                        elif l == 0:
                            if not (isinstance(g, int) and g < ROUNDS + 2):
                                rank_end(g - ROUNDS - 2, u % 2)
                            rank_hot(g - ROUNDS, u % 2)
                        else:
                            put((l - 1) * GROUPS + g, u % 2)
                        if not (isinstance(g, int) and g < 1):
                            scan(g - 1, 1 - u % 2, base)
                        if not (final and u == UNROLL - 1):
                            mark(g + 1, 1 - u % 2, base)

                if l == 0:
                    iteration(0, True)
                    dve.wait_ge(codes_loaded, 48)
                    with dve.Fori(1, ITER // 2) as it:
                        iteration(it, True)
                    tables()
                    iteration(ITER // 2)
                    node_columns()
                    with dve.Fori(ITER // 2 + 1, ITER - 1) as it:
                        iteration(it)
                else:
                    iteration(0)
                    with dve.Fori(1, ITER - 1) as it:
                        iteration(it)
                iteration(ITER - 1, final=True)
                scan(GROUPS - 1, 1, base)
                if l == 0:
                    rank_end(ROUNDS - 2, 0)
                    rank_end(ROUNDS - 1, 1)
                    dve.wait_ge(rk_step, 3 * ROUNDS)
                    step(v.tensor_copy(rank_i[:, :], rank_f[:, 0:TILES]))
                    v.tensor_scalar(rank_p[:, :], rank_i[:, :], P - 1, None, ALU.bitwise_and)
                    step(v.tensor_scalar(rank_t[:, :], rank_i[:, :], 7, None, ALU.logical_shift_right))
                    v.tensor_copy(rank_pt[:, 0:TILES], rank_p[:, :])
                    step(v.tensor_copy(rank_pt[:, TILES:2 * TILES], rank_t[:, :]))
                if l == 1:
                    dve.wait_ge(pl_used, GROUPS)

            def add_chunks(g, a, firsts):
                dve.wait_ge(mixed_done, LAYERS * GROUPS + g + 1)
                for j in range(GROUP):
                    to = agg[:, bass.ds(firsts[j] * P, P)]
                    if some(g * GROUP + j):
                        dve.wait_ge(agg_added, g * GROUP + j)
                    v.tensor_tensor(to, to, mixed[a][:, j * P:(j + 1) * P], ALU.add).then_inc(agg_added, 1)

            def hot_nodes(g, a):
                if some(g - 1):
                    dve.wait_ge(mixed_done, LAYERS * GROUPS + g - 1)
                v.tensor_tensor(hot_sum[:, a, :, :], lo_cols[:, bass.ds(g * GROUP, GROUP)].unsqueeze(2).to_broadcast((P, GROUP, P)),
                                iota[:, 0:P].unsqueeze(1).to_broadcast((P, GROUP, P)), ALU.is_equal).then_inc(sum_hot, 1)

            def residual(k, n, stage):
                at = bass.ds(4 * k, n)
                rows, res = nodes[:, at, :], xres[:, at, :]
                if stage == 0:
                    v.tensor_tensor(rows, rows, along(b2_sb[:, LAYERS - 1, :], n), ALU.add).then_inc(res_step, 1)
                    dve.wait_ge(res_step, 7 * k + 1)
                    v.tensor_tensor(rows, rows, spread(present[:, at], n), ALU.mult).then_inc(res_step, 1)
                    dve.wait_ge(res_step, 7 * k + 2)
                    v.tensor_tensor(res, res, rows, ALU.add).then_inc(res_step, 1)
                    dve.wait_ge(res_step, 7 * k + 3)
                    v.tensor_reduce(stat[:, 2, at], res, AX_X, ALU.add).then_inc(res_step, 1)
                    dve.wait_ge(res_step, 7 * k + 4)
                    v.tensor_scalar(stat[:, 3, at], stat[:, 2, at], -1.0 / D, None, ALU.mult).then_inc(res_mean, 1)
                if stage == 1:
                    dve.wait_ge(res_squares, k + 1)
                    v.tensor_scalar(stat[:, 0, at], stat[:, 2, at], 1.0 / D, EPS, ALU.mult, ALU.add).then_inc(ln_var, 1)
                if stage == 2:
                    dve.wait_ge(ln_std, 2 + k)
                    v.reciprocal(stat[:, 2, at], stat[:, 1, at]).then_inc(res_step, 1)
                    dve.wait_ge(res_step, 7 * k + 5)
                    v.tensor_tensor(stat[:, 3, at], stat[:, 3, at], stat[:, 2, at], ALU.mult).then_inc(res_scale, 1)
                if stage == 3:
                    dve.wait_ge(ln_done, k + 1)
                    v.tensor_tensor(res, res, h_block[:, 0:n, :], ALU.add).then_inc(res_step, 1)
                    dve.wait_ge(res_step, 7 * k + 6)
                    v.tensor_tensor(res, res, along(fbeta, n), ALU.add).then_inc(res_step, 1)

            def sum_groups(it, count=UNROLL, block_size=0):
                for u in range(count):
                    g = it * UNROLL + u
                    if u % 2 == 0:
                        _, firsts = nc.values_load_multi_w_load_instructions(
                            bucket_sb[0:1, bass.ds(g * GROUP, 2 * GROUP)], engines=[mybir.EngineType.DVE],
                            min_val=0, max_val=CH - 1)
                    if not (isinstance(g, int) and g == SUM_GROUPS - 1):
                        hot_nodes(g + 1, 1 - u % 2)
                    add_chunks(g, u % 2, firsts[u % 2 * GROUP:(u % 2 + 1) * GROUP])
                    if block_size:
                        residual(it - 1, block_size, u)

            def sum_pass():
                dve.wait_ge(backed, LAYERS * GROUPS)
                hot_nodes(0, 0)
                sum_groups(0)
                for k in range(BLOCKS):
                    dve.wait_ge(ends[k], 16 * block_chunks(k)[1] * LAYERS)
                dve.wait_ge(fin_w, 96)
                with dve.Fori(1, NB4 + 1) as it:
                    sum_groups(it, block_size=4)
                sum_groups(NB4 + 1, block_size=CH - 4 * NB4)
                with dve.Fori(NB4 + 2, SUM_ITER) as it:
                    sum_groups(it)
                sum_groups(SUM_ITER, SUM_GROUPS - SUM_ITER * UNROLL)

            for l in range(LAYERS):
                for k in range(BLOCKS + A_LAG[l] + 5):
                    if l and k < BLOCKS:
                        node_rows(l, k)
                    b = k - A_LAG[l] - 1
                    if 0 <= b < BLOCKS:
                        c, n = block_chunks(b)
                        dve.wait_ge(a_done, BLOCKS * l + b + 1)
                        v.tensor_tensor(rows_a[:, c:c + n, :],
                                        hidden[b % 2][:, 0:n * D].rearrange("p (c d) -> p c d", d=D),
                                        along(b1_sb[:, l, :], n), ALU.add).then_inc(a_ready, 1)
                    if l == 0 and k == 4:
                        dve.wait_ge(cols_turned, 1)
                        copy_columns(sort_a, dst_cols)
                        copy_columns(sort_b, src_cols).then_inc(cols_copied, 1)
                    if l == 0 and k == 6:
                        dve.wait_ge(cols_turned, 2)
                        copy_columns(sort_a, head_cols).then_inc(edge_cols_done, 1)
                    for part, whole in enumerate((rows_a, rest)):
                        b = k - A_LAG[l] - 3 - part
                        if 0 <= b < BLOCKS:
                            c, n = block_chunks(b)
                            dve.wait_ge(cast[part], BLOCKS * l + b + 1)
                            v.tensor_tensor(rest[:, c:c + n, :], whole[:, c:c + n, :], a_parts[:, c:c + n, part, :],
                                            ALU.subtract).then_inc(left[part], 1)
                dve.wait_ge(cast[2], BLOCKS * (l + 1))
                if l == 0:
                    dve.wait_ge(codes_loaded, 32)
                    occurring = dve.value_load(counter[0:1, 0:1], min_val=0, max_val=NP)
                steps_before = taken[0]
                with dve.If(occurring != N):
                    dve.wait_ge(compact, l + 1)
                    for k in range(BLOCKS):
                        split(k).then_inc(a_resplit, 1)
                    nc.vector.sem_inc(split_done, 1)
                with dve.Else():
                    nc.vector.sem_inc(dve_steps, taken[0] - steps_before)
                    nc.vector.sem_inc(split_done, 1)
                dve.wait_ge(codes_first, 16)
                dve.wait_ge(b_saved, 16 * BLOCKS * (l + 1))
                if l == 0:
                    dve.wait_ge(consts, 2)
                hot(0, 0, l * GROUPS)
                mark(0, 0, l * GROUPS)
                if l == 0:
                    v.memset(ones_h[:, :], 1.0)
                    v.memset(ones_c[:, :], 1.0)
                    v.memset(hot_src[0][:, IT, :], 0.0)
                    v.memset(hot_src[1][:, IT, :], 0.0)
                    v.tensor_copy(before_b[:, :], before[:, :])
                    v.memset(ones_b[:, :], 1.0)
                    v.memset(zeros_b[:, :], 0.0).then_inc(hist_zero, 1)
                    for cols, shift, low, to in ((dst_cols, 6, 0, dst_hi), (dst_cols, 0, LO - 1, dst_lo), (src_cols, 7, 0, src_chunk)):
                        step(v.tensor_scalar(part_j[:, :], cols[:, 0:TILES], shift or low, None,
                                             ALU.logical_shift_right if shift else ALU.bitwise_and))
                        step(v.tensor_copy(to[:, :], part_j[:, :]))
                    step(v.tensor_scalar(part_j[:, :], src_cols[:, 0:TILES], P - 1, None, ALU.bitwise_and))
                    step(v.tensor_scalar(part_j[:, :], part_j[:, :], 4, None, ALU.logical_shift_right))
                    step(v.tensor_copy(part_k[:, :], part_j[:, :]))
                    step(v.tensor_scalar(part_k[:, :], part_k[:, :], -float(SHIFT), None, ALU.add))
                    step(v.scalar_tensor_tensor(pack_a[:, :], iota[:, 0:TILES], 8.0, part_k[:, :], ALU.mult, ALU.add))
                    step(v.tensor_scalar(part_j[:, :], src_cols[:, 0:TILES], 15, None, ALU.bitwise_and))
                    step(v.tensor_copy(part_k[:, :], part_j[:, :]))
                    step(v.tensor_scalar(bk_col[:, :], place[:, 0:1], 16.0, -15.0, ALU.mult, ALU.add))
                    step(v.tensor_scalar(pack_b[:, :], part_k[:, :], bk_col[:, 0:1], None, ALU.add))
                else:
                    v.memset(pl_zero[:, :], 0.0).then_inc(pl_zeroed, 1)
                edge_pass(l)

            dve.wait_ge(pl_used, 2 * GROUPS + 1)
            dve.wait_ge(idx_ready, LAYERS * GROUPS)
            step(v.tensor_scalar(un_a[:, :], sort_a[:, 0:SUM_TILES], float(SHIFT), None, ALU.add))
            v.tensor_scalar(un_b[:, :], sort_b[:, 0:SUM_TILES], -1.0, 0.0, ALU.add, ALU.max)
            step(v.tensor_scalar(lo_cols[:, :], sort_b[:, 0:SUM_TILES], 0.0, -float(SHIFT), ALU.is_equal, ALU.mult))
            v.tensor_copy(un_i[:, :], un_a[:, :])
            step(v.tensor_copy(un_j[:, :], un_b[:, :]))
            v.tensor_scalar(un_perm[:, :], un_i[:, :], 3, None, ALU.logical_shift_right)
            step(v.tensor_scalar(un_low[:, :], un_i[:, :], 7, None, ALU.bitwise_and))
            v.tensor_copy(un_a[:, :], un_perm[:, :])
            step(v.tensor_copy(un_c[:, :], un_low[:, :]))
            step(v.scalar_tensor_tensor(lo_cols[:, :], un_c[:, :], 16.0, lo_cols[:, :], ALU.mult, ALU.add))
            v.tensor_scalar(un_i[:, :], un_j[:, :], 15, None, ALU.bitwise_and)
            step(v.tensor_scalar(un_low[:, :], un_j[:, :], 4, None, ALU.logical_shift_right))
            v.tensor_copy(un_b[:, :], un_i[:, :])
            step(v.tensor_copy(un_c[:, :], un_low[:, :]))
            v.tensor_tensor(lo_cols[:, :], lo_cols[:, :], un_b[:, :], ALU.add)
            step(v.scalar_tensor_tensor(un_a[:, :], un_a[:, :], float(P), un_c[:, :], ALU.mult, ALU.add))
            step(v.tensor_scalar(perm_cols[:, :], un_a[:, :], float(E - 1), None, ALU.min))
            nc.vector.sem_inc(perm_ready, 1)
            step(v.memset(agg[:, :], 0.0))
            sum_pass()

            dve.wait_ge(res_step, 7 * BLOCKS)
            for k in range(BLOCKS + 1):
                if k < BLOCKS:
                    c, n = block_chunks(k)
                    for m in range(2):
                        half = fin_g[:, m, c * P:(c + n) * P]
                        dve.wait_ge(fin_h1, 2 * k + m + 1)
                        dve.wait_ge(fin_half, 2 * k + m + 1)
                        v.tensor_tensor(half, half, (mixed + hidden)[(2 * k + m) % 4][:, 0:n * P], ALU.add).then_inc(fin_sum, 1)
                if k >= 1:
                    c, n = block_chunks(k - 1)
                    y = fin_y[:, c:c + n, :]
                    dve.wait_ge(fin_h2, k)
                    v.tensor_tensor(y, back[(k - 1) % 2][:, 0:n * D].rearrange("p (c d) -> p c d", d=D), along(fc2, n),
                                    ALU.add).then_inc(fin_copied, 1)
                    dve.wait_ge(fin_copied, k)
                    step(v.tensor_reduce(stat[:, 2, c:c + n], y, AX_X, ALU.add))
                    v.tensor_scalar(stat[:, 3, c:c + n], stat[:, 2, c:c + n], -1.0 / D, None, ALU.mult).then_inc(fin_mean, 1)
            dve.wait_ge(fin_squares, BLOCKS)
            v.tensor_scalar(stat[:, 0, :], stat[:, 2, :], 1.0 / D, EPS, ALU.mult, ALU.add).then_inc(ln_var, 1)
            dve.wait_ge(ln_std, 2 + BLOCKS)
            step(v.reciprocal(stat[:, 2, :], stat[:, 1, :]))
            v.tensor_tensor(stat[:, 3, :], stat[:, 3, :], stat[:, 2, :], ALU.mult).then_inc(fin_scale, 1)
            for k in range(BLOCKS):
                c, n = block_chunks(k)
                y = fin_y[:, c:c + n, :]
                dve.wait_ge(fin_scaled, k + 1)
                step(v.tensor_tensor(y, y, along(fgamma, n), ALU.mult))
                v.tensor_tensor(y, y, xres[:, c:c + n, :], ALU.add).then_inc(fin_rows, 1)


_INS = ["x", "src", "dst", "edge_attr_128"] + [
    f"L0_gnn_{w}_{l}" for l in ("in", "hid", "out") for w in ("W1", "b1", "W2", "b2")] + [
    f"L1_gnn_{w}" for w in ("W1", "b1", "W2", "b2", "ln_gamma", "ln_beta")]


def kernel(**inputs):
    import concourse.bacc as _bacc
    from concourse.bass_utils import run_bass_kernel_spmd as _run

    nc = _bacc.Bacc("TRN2", target_bir_lowering=False, num_devices=1)
    arrays, aps = {}, {}
    for name in _INS:
        a = np.ascontiguousarray(inputs[name])
        arrays[f"in_{name}"] = a
        aps[name] = nc.dram_tensor(f"in_{name}", a.shape, mybir.dt.from_np(a.dtype), kind="ExternalInput").ap()
    out = nc.dram_tensor("out_0", (N, D), F32, kind="ExternalOutput").ap()
    layers = [[aps[f"L0_gnn_{w}_{l}"] for l in ("in", "hid", "out")] for w in ("W1", "b1", "W2", "b2")]
    build(nc, aps["x"], aps["src"], aps["dst"], aps["edge_attr_128"], *layers,
          *(aps[f"L1_gnn_{w}"] for w in ("W1", "b1", "W2", "b2", "ln_gamma", "ln_beta")), out)
    r = _run(nc, [arrays], core_ids=[0])
    return r.results[0]["out_0"]
```
